# Optimizing a Trainium2 kernel written in Bass

```python
import numpy as np
import jax
import jax.numpy as jnp

def _softmax(x, axis=-1):
    return jax.nn.softmax(x, axis=axis)

def _gelu(x):
    return jax.nn.gelu(x, approximate=True)

def _silu(x):
    return jax.nn.silu(x)

def _sigmoid(x):
    return jax.nn.sigmoid(x)

def _layernorm(x, axis=-1, eps=1e-05):
    m = jnp.mean(x, axis=axis, keepdims=True)
    v = jnp.var(x, axis=axis, keepdims=True)
    return (x - m) / jnp.sqrt(v + eps)

def _scatter_add(tgt, idx, src, axis=0):
    return tgt.at[idx].add(src)

def _segment_sum(src, seg, n):
    return jax.ops.segment_sum(src, seg, n)
kernel_name = 'mk_gnn_resnorm_d4_gnn_r8_0f7d98'

def setup_inputs(seed: int=0):
    np.random.seed(seed)
    _w = jnp.asarray

    def _rec_inputs():
        import jax
        import jax.numpy as jnp
        _gk = jax.random.key(seed)
        x = -0.0003713 + 1 * jax.random.normal(jax.random.fold_in(_gk, 1), (6250, 128), jnp.float32)
        src = jax.random.randint(jax.random.fold_in(_gk, 2), (100000,), 0, 6250, jnp.int32)
        dst = jax.random.randint(jax.random.fold_in(_gk, 3), (100000,), 0, 6250, jnp.int32)
        _o = jnp.argsort(dst, stable=True)
        src = src[_o]
        dst = dst[_o]
        edge_type_8 = jax.random.randint(jax.random.fold_in(_gk, 13), (100000,), 0, 8, jnp.int32)
        edge_weight = jax.random.uniform(jax.random.fold_in(_gk, 14), (100000,), jnp.float32, 0.0, 1)
        node_type_8 = jax.random.randint(jax.random.fold_in(_gk, 15), (6250,), 0, 8, jnp.int32)
        return (x, src, dst, edge_type_8, edge_weight, node_type_8)
    x, src, dst, edge_type_8, edge_weight, node_type_8 = _rec_inputs()

    def _L0_gnn_setup():
        import jax, jax.numpy as jnp
        import numpy as np
        N_NODES = 12500
        N_EDGES = 400000
        FIN = 128
        FOUT = 128
        K = 4
        key = jax.random.key(seed)
        k1, k2, k3, k4 = jax.random.split(key, 4)
        x = jax.random.normal(k1, (N_NODES, FIN), dtype=jnp.float32)
        edge_index = jax.random.randint(k2, (2, N_EDGES), 0, N_NODES, dtype=jnp.int64)
        edge_weight = jax.random.uniform(k3, (N_EDGES,), dtype=jnp.float32)
        weights = jax.random.normal(k4, (K, FIN, FOUT), dtype=jnp.float32)
        return {'x': x, 'edge_index': edge_index, 'edge_weight': edge_weight, 'weights': weights}
    _L0_gnn_all = _L0_gnn_setup()
    _L0_gnn_in = {k: v for k, v in _L0_gnn_all.items() if k in ('weights',)}
    del _L0_gnn_all

    def _L1_gnn_setup():
        import jax, jax.numpy as jnp
        import numpy as np
        N = 6250
        E = 100000
        DIN = 128
        DH = 128
        H = 8
        DK = DH // H
        TN = 8
        TE = 8
        NB = 4

        def _decomp(x, nt, w_comp, w_basis):
            T = w_comp.shape[0]
            W = (w_comp @ w_basis).reshape(T, x.shape[-1], -1)
            h_all = jnp.einsum('ni,tio->tno', x, W)
            return h_all[nt, jnp.arange(x.shape[0])]
        key = jax.random.key(seed)
        ks = jax.random.split(key, 20)
        inp = {}
        inp['node_feat'] = jax.random.normal(ks[0], (N, DIN), jnp.float32)
        inp['node_type'] = jax.random.randint(ks[1], (N,), 0, TN)
        inp['src'] = jax.random.randint(ks[2], (E,), 0, N)
        inp['dst'] = jax.random.randint(ks[3], (E,), 0, N)
        inp['edge_type'] = jax.random.randint(ks[4], (E,), 0, TE)
        s = 0.05
        for i, nm in enumerate(['k', 'q', 'v', 'a']):
            inp['w_comp_' + nm] = jax.random.normal(ks[5 + 2 * i], (TN, NB), jnp.float32) * s
            inp['w_basis_' + nm] = jax.random.normal(ks[6 + 2 * i], (NB, DIN * DH), jnp.float32) * s
        inp['relation_pri'] = jnp.ones((TE, H), jnp.float32)
        inp['relation_att'] = jax.random.uniform(ks[13], (TE, H, DK, DK), jnp.float32, -0.25, 0.25)
        inp['relation_msg'] = jax.random.uniform(ks[14], (TE, H, DK, DK), jnp.float32, -0.25, 0.25)
        inp['loop_weight'] = jax.random.uniform(ks[15], (DIN, DH), jnp.float32, -0.08, 0.08)
        inp['bias'] = jnp.zeros((DH,), jnp.float32)
        return inp
    _L1_gnn_all = _L1_gnn_setup()
    _L1_gnn_in = {k: v for k, v in _L1_gnn_all.items() if k in ('w_comp_k', 'w_basis_k', 'w_comp_q', 'w_basis_q', 'w_comp_v', 'w_basis_v', 'w_comp_a', 'w_basis_a', 'relation_pri', 'relation_att', 'relation_msg', 'loop_weight', 'bias')}
    del _L1_gnn_all

    def _L2_gnn_setup():
        import jax, jax.numpy as jnp
        import numpy as np
        N, E, F, H, C = (6250, 100000, 128, 4, 32)
        NEG_SLOPE = 0.2
        key = jax.random.key(seed)
        k0, k1, k2, k3, k4 = jax.random.split(key, 5)
        x = jax.random.normal(k0, (N, F), dtype=jnp.float32)
        edge_index = jax.random.randint(k1, (2, E), 0, N, dtype=jnp.int64)
        s_w = 1.0 / np.sqrt(F).astype(np.float32)
        W_l = jax.random.normal(k2, (H * C, F), dtype=jnp.float32) * s_w
        W_r = jax.random.normal(k3, (H * C, F), dtype=jnp.float32) * s_w
        att = jax.random.normal(k4, (H, C), dtype=jnp.float32) * (1.0 / np.sqrt(C).astype(np.float32))
        bias = jnp.zeros((H * C,), dtype=jnp.float32)
        return {'x': x, 'edge_index': edge_index, 'W_l': W_l, 'W_r': W_r, 'att': att, 'bias': bias}
    _L2_gnn_all = _L2_gnn_setup()
    _L2_gnn_in = {k: v for k, v in _L2_gnn_all.items() if k in ('W_l', 'W_r', 'att', 'bias')}
    del _L2_gnn_all

    def _L3_gnn_setup():
        import jax, jax.numpy as jnp
        import numpy as np
        N = 6250
        E = 75000
        FEAT = 128
        H = 8
        D = FEAT // H
        key = jax.random.key(seed)
        ks = jax.random.split(key, 8)
        s = 1.0 / np.sqrt(FEAT)
        inp = {'node_features': jax.random.normal(ks[0], (N, FEAT), dtype=jnp.float32), 'edge_index': jax.random.randint(ks[1], (2, E), 0, N, dtype=jnp.int64), 'Wq': jax.random.normal(ks[2], (FEAT, FEAT), dtype=jnp.float32) * s, 'bq': jnp.zeros((FEAT,), dtype=jnp.float32), 'Wk': jax.random.normal(ks[3], (FEAT, FEAT), dtype=jnp.float32) * s, 'bk': jnp.zeros((FEAT,), dtype=jnp.float32), 'Wv': jax.random.normal(ks[4], (FEAT, FEAT), dtype=jnp.float32) * s, 'bv': jnp.zeros((FEAT,), dtype=jnp.float32), 'Wo': jax.random.normal(ks[5], (FEAT, FEAT), dtype=jnp.float32) * s, 'bo': jnp.zeros((FEAT,), dtype=jnp.float32)}
        return inp
    _L3_gnn_all = _L3_gnn_setup()
    _L3_gnn_in = {k: v for k, v in _L3_gnn_all.items() if k in ('Wq', 'bq', 'Wk', 'bk', 'Wv', 'bv', 'Wo', 'bo')}
    del _L3_gnn_all
    return {'x': x, 'src': src, 'dst': dst, 'edge_type_8': edge_type_8, 'edge_weight': edge_weight, 'node_type_8': node_type_8, 'L0_gnn_weights': _L0_gnn_in['weights'], 'L1_gnn_w_comp_k': _L1_gnn_in['w_comp_k'], 'L1_gnn_w_basis_k': _L1_gnn_in['w_basis_k'], 'L1_gnn_w_comp_q': _L1_gnn_in['w_comp_q'], 'L1_gnn_w_basis_q': _L1_gnn_in['w_basis_q'], 'L1_gnn_w_comp_v': _L1_gnn_in['w_comp_v'], 'L1_gnn_w_basis_v': _L1_gnn_in['w_basis_v'], 'L1_gnn_w_comp_a': _L1_gnn_in['w_comp_a'], 'L1_gnn_w_basis_a': _L1_gnn_in['w_basis_a'], 'L1_gnn_relation_pri': _L1_gnn_in['relation_pri'], 'L1_gnn_relation_att': _L1_gnn_in['relation_att'], 'L1_gnn_relation_msg': _L1_gnn_in['relation_msg'], 'L1_gnn_loop_weight': _L1_gnn_in['loop_weight'], 'L1_gnn_bias': _L1_gnn_in['bias'], 'L2_gnn_W_l': _L2_gnn_in['W_l'], 'L2_gnn_W_r': _L2_gnn_in['W_r'], 'L2_gnn_att': _L2_gnn_in['att'], 'L2_gnn_bias': _L2_gnn_in['bias'], 'L3_gnn_Wq': _L3_gnn_in['Wq'], 'L3_gnn_bq': _L3_gnn_in['bq'], 'L3_gnn_Wk': _L3_gnn_in['Wk'], 'L3_gnn_bk': _L3_gnn_in['bk'], 'L3_gnn_Wv': _L3_gnn_in['Wv'], 'L3_gnn_bv': _L3_gnn_in['bv'], 'L3_gnn_Wo': _L3_gnn_in['Wo'], 'L3_gnn_bo': _L3_gnn_in['bo']}

def reference(x, src, dst, edge_type_8, edge_weight, node_type_8, L0_gnn_weights, L1_gnn_w_comp_k, L1_gnn_w_basis_k, L1_gnn_w_comp_q, L1_gnn_w_basis_q, L1_gnn_w_comp_v, L1_gnn_w_basis_v, L1_gnn_w_comp_a, L1_gnn_w_basis_a, L1_gnn_relation_pri, L1_gnn_relation_att, L1_gnn_relation_msg, L1_gnn_loop_weight, L1_gnn_bias, L2_gnn_W_l, L2_gnn_W_r, L2_gnn_att, L2_gnn_bias, L3_gnn_Wq, L3_gnn_bq, L3_gnn_Wk, L3_gnn_bk, L3_gnn_Wv, L3_gnn_bv, L3_gnn_Wo, L3_gnn_bo):
    import jax
    import jax.numpy as jnp

    def _L0_gnn_ref(x, edge_index, edge_weight, weights):
        import jax, jax.numpy as jnp
        import numpy as np
        N_NODES = 12500
        N_EDGES = 400000
        FIN = 128
        FOUT = 128
        K = 4
        N, d = x.shape
        Kh = weights.shape[0]
        row, col = (edge_index[0], edge_index[1])

        def spmm(z):
            return jax.ops.segment_sum(edge_weight[:, None] * z[col], row, num_segments=N)
        z = x
        y = z @ weights[0]
        for k in range(1, Kh):
            z = spmm(z)
            y = y + z @ weights[k]
        return y / jnp.sqrt(jnp.asarray(d, dtype=x.dtype))

    def _L1_gnn_ref(node_feat, node_type, src, dst, edge_type, w_comp_k, w_basis_k, w_comp_q, w_basis_q, w_comp_v, w_basis_v, w_comp_a, w_basis_a, relation_pri, relation_att, relation_msg, loop_weight, bias):
        import jax, jax.numpy as jnp
        import numpy as np
        N = 6250
        E = 100000
        DIN = 128
        DH = 128
        H = 8
        DK = DH // H
        TN = 8
        TE = 8
        NB = 4

        def _decomp(x, nt, w_comp, w_basis):
            T = w_comp.shape[0]
            W = (w_comp @ w_basis).reshape(T, x.shape[-1], -1)
            h_all = jnp.einsum('ni,tio->tno', x, W)
            return h_all[nt, jnp.arange(x.shape[0])]
        n = node_feat.shape[0]
        scale = (DH / H) ** (-0.5)
        k = _decomp(node_feat, node_type, w_comp_k, w_basis_k).reshape(n, H, DK)
        q = _decomp(node_feat, node_type, w_comp_q, w_basis_q).reshape(n, H, DK)
        v = _decomp(node_feat, node_type, w_comp_v, w_basis_v).reshape(n, H, DK)
        kt = jnp.einsum('nhi,thij->tnhj', k, relation_att)[edge_type, src]
        e = (q[dst] * kt).sum(-1) * relation_pri[edge_type] * scale
        m = jax.ops.segment_max(e, dst, num_segments=n)
        ex = jnp.exp(e - m[dst])
        denom = jax.ops.segment_sum(ex, dst, num_segments=n)
        a = ex / denom[dst]
        vt = jnp.einsum('nhi,thij->tnhj', v, relation_msg)[edge_type, src]
        agg = jax.ops.segment_sum(a[..., None] * vt, dst, num_segments=n)
        agg = agg.reshape(n, DH)
        out = _decomp(agg, node_type, w_comp_a, w_basis_a)
        out = out + node_feat @ loop_weight + bias
        return jax.nn.relu(out)

    def _L2_gnn_ref(x, edge_index, W_l, W_r, att, bias):
        import jax, jax.numpy as jnp
        import numpy as np
        N, E, F, H, C = (6250, 100000, 128, 4, 32)
        NEG_SLOPE = 0.2
        n = x.shape[0]
        x_l = (x @ W_l.T).reshape(n, H, C)
        x_r = (x @ W_r.T).reshape(n, H, C)
        loop = jnp.arange(n, dtype=edge_index.dtype)
        src = jnp.concatenate([edge_index[0], loop])
        dst = jnp.concatenate([edge_index[1], loop])
        e = jax.nn.leaky_relu(x_l[src] + x_r[dst], NEG_SLOPE)
        logits = jnp.einsum('ehc,hc->eh', e, att)
        m = jax.ops.segment_max(logits, dst, num_segments=n)
        m = jnp.where(jnp.isfinite(m), m, 0.0)
        num = jnp.exp(logits - m[dst])
        den = jax.ops.segment_sum(num, dst, num_segments=n)
        alpha = num / jnp.maximum(den[dst], 1e-16)
        out = jax.ops.segment_sum(alpha[:, :, None] * x_l[src], dst, num_segments=n)
        return out.reshape(n, H * C) + bias

    def _L3_gnn_ref(node_features, edge_index, Wq, bq, Wk, bk, Wv, bv, Wo, bo):
        import jax, jax.numpy as jnp
        import numpy as np
        N = 6250
        E = 75000
        FEAT = 128
        H = 8
        D = FEAT // H
        n = node_features.shape[0]
        src, dest = (edge_index[0], edge_index[1])
        q = (node_features @ Wq.T + bq).reshape(n, H, D)
        k = (node_features @ Wk.T + bk).reshape(n, H, D)
        v = (node_features @ Wv.T + bv).reshape(n, H, D)
        scores = jnp.einsum('ehd,ehd->eh', q[src], k[dest]) / np.sqrt(D)
        seg_max = jax.ops.segment_max(scores, src, num_segments=n)
        ex = jnp.exp(scores - seg_max[src])
        seg_sum = jax.ops.segment_sum(ex, src, num_segments=n)
        weights = ex / seg_sum[src]
        weighted_values = v[src] * weights[..., None]
        agg = jax.ops.segment_sum(weighted_values, dest, num_segments=n)
        out = agg.reshape(n, FEAT) @ Wo.T + bo
        return out
    edge_index = jnp.stack([src, dst])
    x = _layernorm(x + _L0_gnn_ref(x, edge_index, edge_weight, L0_gnn_weights), axis=-1)
    x = _layernorm(x + _L1_gnn_ref(x, node_type_8, src, dst, edge_type_8, L1_gnn_w_comp_k, L1_gnn_w_basis_k, L1_gnn_w_comp_q, L1_gnn_w_basis_q, L1_gnn_w_comp_v, L1_gnn_w_basis_v, L1_gnn_w_comp_a, L1_gnn_w_basis_a, L1_gnn_relation_pri, L1_gnn_relation_att, L1_gnn_relation_msg, L1_gnn_loop_weight, L1_gnn_bias), axis=-1)
    x = _layernorm(x + _L2_gnn_ref(x, edge_index, L2_gnn_W_l, L2_gnn_W_r, L2_gnn_att, L2_gnn_bias), axis=-1)
    x = _layernorm(x + _L3_gnn_ref(x, edge_index, L3_gnn_Wq, L3_gnn_bq, L3_gnn_Wk, L3_gnn_bk, L3_gnn_Wv, L3_gnn_bv, L3_gnn_Wo, L3_gnn_bo), axis=-1)
    return x

_drawn_inputs = setup_inputs


def setup_inputs(seed=0):
    import zlib

    import numpy as np

    out = dict(_drawn_inputs(seed))
    spreads = {'L1_gnn_relation_pri': (1.0, 0.6),
     'L1_gnn_bias': (0.0, 0.8),
     'L2_gnn_bias': (0.0, 0.1),
     'L3_gnn_bq': (0.0, 0.1),
     'L3_gnn_bk': (0.0, 2.0),
     'L3_gnn_bv': (0.0, 0.1),
     'L3_gnn_bo': (0.0, 0.1)}
    factors = {'L1_gnn_w_comp_k': 8.0,
     'L1_gnn_w_basis_k': 8.0,
     'L1_gnn_w_comp_q': 8.0,
     'L1_gnn_w_basis_q': 8.0,
     'L1_gnn_w_comp_v': 8.0,
     'L1_gnn_w_basis_v': 8.0,
     'L1_gnn_w_comp_a': 8.0,
     'L1_gnn_w_basis_a': 8.0,
     'L1_gnn_relation_att': 8.0,
     'L1_gnn_relation_msg': 8.0,
     'L1_gnn_loop_weight': 2.847}
    for name, (base, spread) in spreads.items():
        noise = np.random.default_rng([zlib.crc32(name.encode()), seed]).standard_normal(out[name].shape)
        drawn = base * np.exp(spread * noise) if base else spread * noise
        out[name] = jnp.asarray(drawn.astype(out[name].dtype))
    for name, factor in factors.items():
        out[name] = (out[name] * factor).astype(out[name].dtype)
    return out
```

```python
from contextlib import ExitStack

import concourse.bass as bass
from concourse import mybir

ALU = mybir.AluOpType
ACT = mybir.ActivationFunctionType
AX = mybir.AxisListType
F32 = mybir.dt.float32
BF16 = mybir.dt.bfloat16
I32 = mybir.dt.int32

P = 128
N = 6250
E = 100000
D = 128
NBLK = -(-N // P)
NP = NBLK * P
TAIL = N - (NBLK - 1) * P
TYPES = 8
BASES = 4
G = 4
SLOTS = 4
EC = -(-E // (P * G * SLOTS)) * G * SLOTS
PADS = EC * P - E
EMAIN = E // P
HIS = NBLK + 1
CH = -(-((E + NBLK * (P - 1)) // P + -(-PADS // P)) // (G * SLOTS)) * G * SLOTS
NSLOT = CH * P
LEAD = 1
GROUPS = CH // G
ROUNDS = GROUPS // SLOTS
TQ = 104
QT = CH // TQ
SPARE = SLOTS * G
BIG = 1.0e30
EPS = 1e-5
TINY = 1e-16
assert QT * TQ == CH and EC % (G * SLOTS) == 0


class Shared:
    pass


class Order:
    pass


def free_semaphores(nc, k):
    nc.clear_and_free_semaphores(k.semaphores)
    nc.all_engine_barrier()
    k.semaphores = []


def tools(nc, k, ctx, phase):
    def sb(name, shape, dt=F32):
        return ctx.enter_context(nc.sbuf_tensor(f"{phase}_{name}", shape, dt))

    def ps(name, shape, dt=F32):
        return ctx.enter_context(nc.psum_tensor(f"{phase}_{name}", shape, dt))

    def sem(name):
        semaphore = nc.alloc_semaphore(f"{phase}_{name}")
        k.semaphores.append(semaphore)
        return semaphore

    return sb, ps, sem


def load_blocks(nc, engine, chunk, count):
    _, regs = nc.values_load_multi_w_load_instructions(
        chunk, engines=[engine], min_val=0, max_val=NBLK - 1,
        skip_runtime_bounds_check_because="the table is clamped to the last block")
    return regs


def in_rounds(engine, count, body):
    body(0, True)
    with engine.Fori(1, count) as i:
        body(i, False)


def make_constants(nc, k):
    with ExitStack() as ctx:
        sb, ps, sem = tools(nc, k, ctx, "const")
        pool_step = sem("pool_step")
        made = sem("made")
        block = ctx.enter_context(nc.Block())

        @block.gpsimd
        def _(pool):
            nc.gpsimd.memset(k.ident[:], 0.0)
            nc.gpsimd.memset(k.before[:], 1.0).then_inc(pool_step, 1)
            nc.gpsimd.iota(k.count[:], [[1, P]], base=0, channel_multiplier=0,
                           allow_small_or_imprecise_dtypes=True)
            nc.gpsimd.memset(k.ones[:], 1.0)
            pool.wait_ge(pool_step, 1)
            nc.gpsimd.affine_select(out=k.ident[:], in_=k.ident[:], compare_op=ALU.not_equal, fill=1.0,
                                    base=0, pattern=[[-1, P]], channel_multiplier=1)
            nc.gpsimd.affine_select(out=k.before[:], in_=k.before[:], compare_op=ALU.is_gt, fill=0.0,
                                    base=0, pattern=[[-1, P]], channel_multiplier=1).then_inc(made, 1)

        @block.vector
        def _(dve):
            dve.wait_ge(made, 1)
            nc.vector.tensor_copy(k.identb[:], k.ident[:])
            nc.vector.tensor_copy(k.countb[:], k.count[:])


def load_edges(nc, k, key, fields, rec, keys, prepare):
    with ExitStack() as ctx:
        sb, ps, sem = tools(nc, k, ctx, prepare)
        raw = sb("raw", [P, len(fields) + 1, EC], I32)
        hi = sb("hi", [P, EC], I32)
        lo = sb("lo", [P, EC], I32)
        padded = sem("padded")
        loaded = sem("loaded")
        step = sem("step")
        rest = E - EMAIN * P
        block = ctx.enter_context(nc.Block())

        @block.sync
        def _(sp):
            sp.wait_ge(padded, 1)
            for n, field in enumerate([key, *fields]):
                tile = raw[:, n, :] if field.dtype == I32 else raw[:, n, :].bitcast(F32)
                sp.dma_start(tile[:, 0:EMAIN],
                             field[0:EMAIN * P].rearrange("(p c) -> p c", p=P)).then_inc(loaded, 16)
                sp.dma_start(tile[0:rest, EMAIN:EMAIN + 1],
                             field[EMAIN * P:E].rearrange("(p c) -> p c", c=1)).then_inc(loaded, 16)

        @block.vector
        def _(dve):
            nc.vector.memset(raw[:, 1:, EMAIN:], 0)
            nc.vector.memset(raw[:, 0, EMAIN:], NP).then_inc(padded, 1)
            dve.wait_ge(loaded, 32 * (len(fields) + 1))
            for n, field in enumerate([key, *fields]):
                tile = raw[:, n, :] if field.dtype == I32 else raw[:, n, :].bitcast(F32)
                nc.vector.tensor_copy(rec[:, :, n], tile)
            for n in range(len(fields) + 1, 4):
                nc.vector.memset(rec[:, :, n], 0.0)
            nc.vector.tensor_single_scalar(hi[:], raw[:, 0, :], 7, ALU.arith_shift_right).then_inc(step, 1)
            nc.vector.tensor_single_scalar(lo[:], raw[:, 0, :], P - 1, ALU.bitwise_and).then_inc(step, 1)
            dve.wait_ge(step, 2)
            nc.vector.tensor_copy(keys[:, 0, 0:EC], hi[:])
            nc.vector.tensor_copy(keys[:, 1, 0:EC], lo[:])
            nc.vector.memset(keys[:, :, EC:], 0.0)


def prefill(nc, k, tables, name):
    with ExitStack() as ctx:
        sb, ps, sem = tools(nc, k, ctx, name)
        pad = sb("pad", [P, CH, 4])
        filled = sem("filled")
        stored = sem("stored")
        block = ctx.enter_context(nc.Block())

        @block.vector
        def _(dve):
            nc.vector.memset(pad[:, :, 0:1], -1.0)
            nc.vector.memset(pad[:, :, 1:4], 0.0).then_inc(filled, 1)

        @block.sync
        def _(sp):
            sp.wait_ge(filled, 1)
            for table in tables:
                sp.dma_start(table[LEAD:LEAD + NSLOT, :].rearrange("(p c) f -> p (c f)", p=P),
                             pad[:].rearrange("p c f -> p (c f)")).then_inc(stored, 16)
                sp.dma_start(table[0:LEAD, :], pad[0:1, 0, :]).then_inc(stored, 16)
            sp.wait_ge(stored, 32 * len(tables))


def histogram(nc, k, keys, counts, name):
    with ExitStack() as ctx:
        sb, ps, sem = tools(nc, k, ctx, name)
        oh_hi = sb("oh_hi", [P, 2, G, HIS], BF16)
        oh_lo = sb("oh_lo", [P, 2, G, P], BF16)
        zero = sb("zero", [P, P], BF16)
        total = ps("total", [HIS, P])
        onehots = sem("onehots")
        summed = sem("summed")
        zeroed = sem("zeroed")
        block = ctx.enter_context(nc.Block())

        @block.vector
        def _(dve):
            nc.vector.memset(zero[:], 0.0).then_inc(zeroed, 1)
            with dve.Fori(0, EC // G // 2) as i:
                for b in range(2):
                    dve.wait_ge(summed, i * 2 + b + 1)
                    for g in range(G):
                        c = i * 2 * G + b * G + g
                        nc.vector.tensor_scalar(oh_hi[:, b, g, :], k.countb[:, 0:HIS], keys[:, 0, bass.ds(c, 1)],
                                                None, ALU.is_equal)
                        last = nc.vector.tensor_scalar(oh_lo[:, b, g, :], k.countb[:], keys[:, 1, bass.ds(c, 1)],
                                                       None, ALU.is_equal)
                    last.then_inc(onehots, 1)
            dve.wait_ge(summed, EC // G + 2)
            nc.vector.tensor_copy(counts[:], total[:])

        @block.tensor
        def _(pe):
            pe.sem_inc(summed, 2)
            pe.wait_ge(zeroed, 1)
            nc.tensor.matmul(total[:], zero[:, 0:HIS], zero[:], start=True, stop=False, skip_group_check=True)
            with pe.Fori(0, EC // G // 2) as i:
                for b in range(2):
                    pe.wait_ge(onehots, i * 2 + b + 1)
                    for g in range(G):
                        last = nc.tensor.matmul(total[:], oh_hi[:, b, g, :], oh_lo[:, b, g, :], start=False,
                                                stop=False, skip_group_check=True)
                    last.then_inc(summed, 1)


def place_blocks(nc, k, counts, first_place, o, name):
    with ExitStack() as ctx:
        sb, ps, sem = tools(nc, k, ctx, name)
        edges = sb("edges", [HIS, 1])
        edges_i = sb("edges_i", [HIS, 1], I32)
        chunks_i = sb("chunks_i", [HIS, 1], I32)
        chunks = sb("chunks", [HIS, 1])
        start = sb("start", [HIS, 1])
        upto = sb("upto", [HIS, P])
        zeros = sb("zeros", [HIS, P])
        above = sb("above", [P, P])
        chunk_no = sb("chunk_no", [HIS, CH])
        begun = sb("begun", [HIS, CH])
        block_f = sb("block_f", [P, CH])
        starts = ps("starts", [HIS, 1])
        turned = ps("turned", [P, P])
        begun_n = ps("begun_n", [P, 2, 512])
        half = CH // 2
        numbered = sem("numbered")
        d = sem("d")
        pe_step = sem("pe_step")
        block = ctx.enter_context(nc.Block())

        @block.gpsimd
        def _(pool):
            nc.gpsimd.iota(chunk_no[:], [[1, CH]], base=0, channel_multiplier=0,
                           allow_small_or_imprecise_dtypes=True).then_inc(numbered, 1)

        @block.tensor
        def _(pe):
            nc.tensor.transpose(turned[:], k.before[:], k.ident[:]).then_inc(pe_step, 1)
            pe.wait_ge(d, 6)
            nc.tensor.matmul(starts[:], above[0:HIS, 0:HIS], chunks[:], start=True, stop=True).then_inc(pe_step, 1)
            pe.wait_ge(d, 8)
            for h in range(2):
                last = nc.tensor.matmul(begun_n[:, h, 0:half], k.ones[0:HIS, :], begun[:, h * half:(h + 1) * half],
                                        start=True, stop=True)
            last.then_inc(pe_step, 1)

        @block.vector
        def _(dve):
            nc.vector.memset(zeros[:], 0.0)
            nc.vector.tensor_reduce(edges[:], counts[:], AX.X, ALU.add).then_inc(d, 1)
            dve.wait_ge(d, 1)
            nc.vector.tensor_scalar(edges_i[:], edges[:], float(P - 1), None, ALU.add).then_inc(d, 1)
            dve.wait_ge(d, 2)
            nc.vector.tensor_single_scalar(chunks_i[:], edges_i[:], 7, ALU.arith_shift_right).then_inc(d, 1)
            dve.wait_ge(d, 3)
            nc.vector.tensor_copy(chunks[:], chunks_i[:]).then_inc(d, 1)
            dve.wait_ge(pe_step, 1)
            nc.vector.tensor_copy(above[:], turned[:]).then_inc(d, 1)
            nc.vector.tensor_tensor_scan(upto[:], zeros[:], counts[:], 0.0, ALU.add, ALU.add).then_inc(d, 1)
            dve.wait_ge(pe_step, 2)
            nc.vector.tensor_copy(start[:], starts[:]).then_inc(d, 1)
            dve.wait_ge(numbered, 1)
            dve.wait_ge(d, 7)
            nc.vector.tensor_scalar(begun[:], chunk_no[:], start[:], None, ALU.is_ge).then_inc(d, 1)
            nc.vector.tensor_tensor(upto[:], upto[:], counts[:], ALU.subtract).then_inc(d, 1)
            nc.vector.tensor_scalar(start[:], start[:], float(P), float(LEAD), ALU.mult, ALU.add).then_inc(d, 1)
            dve.wait_ge(d, 10)
            nc.vector.tensor_scalar(first_place[:], upto[:], start[:], None, ALU.add)
            dve.wait_ge(pe_step, 3)
            nc.vector.tensor_scalar(block_f[:].rearrange("p (h c) -> p h c", h=2), begun_n[:, :, 0:half], -1.0,
                                    float(NBLK - 1), ALU.add, ALU.min).then_inc(d, 1)
            dve.wait_ge(d, 11)
            nc.vector.tensor_scalar(o.block_base[:], block_f[:], float(P), None, ALU.mult)
            nc.vector.memset(o.block[:, CH:], 0)
            nc.vector.tensor_copy(o.block[:, 0:CH], block_f[0:1, :])


def scatter_edges(nc, k, rec, keys, first_place, table, name):
    with ExitStack() as ctx:
        sb, ps, sem = tools(nc, k, ctx, name)
        oh_hi = sb("oh_hi", [P, 2, G, HIS], BF16)
        oh_lo = sb("oh_lo", [P, 2, G, P], BF16)
        oh_hi_t = sb("oh_hi_t", [HIS, 2, G, P])
        next_sb = sb("next_sb", [HIS, 2, P])
        keys_next = sb("keys_next", [P, 2, 2 * G])
        picked = sb("picked", [P, 2, P])
        same = sb("same", [P, 2, P])
        base = sb("base", [P, 2, G])
        earlier = sb("earlier", [P, 2, G])
        places = sb("places", [P, SLOTS, G], I32)
        records = sb("records", [P, SLOTS, G, 4])
        next_ps = ps("next_ps", [HIS, 512])
        turned = ps("turned", [HIS, 2, 2 * G, P], BF16)
        nexts = ps("nexts", [P, 2, G, P])
        keyrow = ps("keyrow", [P, 2, G, P])
        taken = sem("taken")
        onehots = sem("onehots")
        turned_ok = sem("turned_ok")
        hi_t = sem("hi_t")
        rows = sem("rows")
        next_ready = sem("next_ready")
        next_copied = sem("next_copied")
        looked = sem("looked")
        ranked = sem("ranked")
        placed = sem("placed")
        sent = [sem(f"sent{s}") for s in range(SLOTS)]
        running = sem("running")
        groups = EC // G
        block = ctx.enter_context(nc.Block())

        @block.scalar
        def _(act):
            def a_round(i, first):
                for s in range(SLOTS):
                    b = s % 2
                    g1 = i * SLOTS + s + 1
                    if not first:
                        act.wait_ge(sent[s], i * 64)
                    nc.scalar.copy(records[:, s, :, :], rec[:, bass.ds(i * SLOTS * G + s * G, G), :]).then_inc(taken, 1)
                    act.wait_ge(turned_ok, g1)
                    act.wait_ge(looked, g1 * G)
                    nc.scalar.copy(oh_hi_t[:, b, :, :], turned[:, b, 0:G, :]).then_inc(hi_t, 1)
                    for g in range(G):
                        c1 = (i * SLOTS + s) * G + g + 1
                        act.wait_ge(next_ready, c1)
                        act.wait_ge(looked, c1 + 2 * G - 2)
                        nc.scalar.copy(next_sb[:, g % 2, :], next_ps[:, 0:P]).then_inc(next_copied, 1)

            in_rounds(act, groups // SLOTS, a_round)

        @block.tensor
        def _(pe):
            pe.sem_inc(looked, 2 * G)
            nc.tensor.matmul(next_ps[:, 0:P], k.ident[0:HIS, 0:HIS], first_place[:], start=True, stop=False,
                             skip_group_check=True).then_inc(next_ready, 1)
            with pe.Fori(0, groups // SLOTS) as i:
                for s in range(SLOTS):
                    b = s % 2
                    g1 = i * SLOTS + s + 1
                    pe.wait_ge(onehots, g1)
                    pe.wait_ge(hi_t, g1)
                    pe.wait_ge(taken, g1)
                    pe.wait_ge(ranked, g1 * G)
                    for g in range(G):
                        last = nc.tensor.transpose(keyrow[:, b, g, :], records[:, s, g, 0:1].to_broadcast([P, P]),
                                                   k.ident[:])
                    last.then_inc(rows, 1)
                    for g in range(G):
                        last = nc.tensor.transpose(turned[:, b, g, :], oh_hi[:, b, g, :], k.identb[:])
                    last.then_inc(turned_ok, 1)
                    pe.wait_ge(hi_t, g1 + 2)
                    for g in range(G):
                        c1 = (i * SLOTS + s) * G + g + 1
                        pe.wait_ge(next_copied, c1)
                        nc.tensor.matmul(next_ps[:, 0:P], oh_hi[:, b, g, :], oh_lo[:, b, g, :], start=False,
                                         stop=False, skip_group_check=True).then_inc(next_ready, 1)
                        nc.tensor.matmul(nexts[:, b, g, :], oh_hi_t[:, b, g, :], next_sb[:, g % 2, :], start=True,
                                         stop=True).then_inc(looked, 1)

        @block.vector
        def _(dve):
            dve.sem_inc(hi_t, 2)
            dve.sem_inc(ranked, 2 * G)

            def hot(c, b, g):
                nc.vector.tensor_scalar(oh_hi[:, b, g, :], k.countb[:, 0:HIS], keys[:, 0, bass.ds(c, 1)], None,
                                        ALU.is_equal)
                return nc.vector.tensor_scalar(oh_lo[:, b, g, :], k.countb[:], keys[:, 1, bass.ds(c, 1)], None,
                                               ALU.is_equal)

            for g in range(G):
                last = hot(g, 0, g)
            last.then_inc(onehots, 1)

            def a_round(i, first):
                for s in range(SLOTS):
                    b = s % 2
                    g1 = i * SLOTS + s + 1
                    dve.wait_ge(next_ready, g1 * G - G + 1)
                    dve.wait_ge(looked, g1 * G + G)
                    for g in range(G):
                        last = hot(i * SLOTS * G + s * G + G + g, 1 - b, g)
                    last.then_inc(onehots, 1)
                    dve.wait_ge(rows, g1)
                    dve.wait_ge(looked, g1 * G + 2 * G)
                    for g in range(G):
                        c1 = (i * SLOTS + s) * G + g + 1
                        dve.wait_ge(ranked, c1 + 2 * G - 2)
                        nc.vector.scalar_tensor_tensor(out=same[:, g % 2, :], in0=keyrow[:, b, g, :],
                                                       scalar=records[:, s, g, 0:1], in1=k.before[:],
                                                       op0=ALU.is_equal, op1=ALU.mult,
                                                       accum_out=earlier[:, b, g:g + 1])
                        nc.vector.scalar_tensor_tensor(out=picked[:, g % 2, :], in0=nexts[:, b, g, :], scalar=1.0,
                                                       in1=oh_lo[:, b, g, :], op0=ALU.mult, op1=ALU.mult,
                                                       accum_out=base[:, b, g:g + 1]).then_inc(ranked, 1)
                    dve.wait_ge(ranked, g1 * G + 2 * G)
                    if not first:
                        dve.wait_ge(sent[s], i * 64)
                    nc.vector.tensor_tensor(places[:, s, :], base[:, b, :], earlier[:, b, :], ALU.add).then_inc(placed, 1)

            in_rounds(dve, groups // SLOTS, a_round)

        @block.gpsimd
        def _(pool):
            with pool.Fori(0, groups // SLOTS) as i:
                for s in range(SLOTS):
                    pool.wait_ge(placed, i * SLOTS + s + 1)
                    pool.sem_inc(running, 1)
                    for g in range(G):
                        nc.gpsimd.indirect_dma_start(table, bass.IndirectOffsetOnAxis(ap=places[:, s, g:g + 1], axis=0),
                                                     records[:, s, g, :], None).then_inc(sent[s], 16)
            for s in range(SLOTS):
                pool.wait_ge(sent[s], 64 * (groups // SLOTS))


def read_order(nc, k, table, o, breaks, ints, floats, name):
    with ExitStack() as ctx:
        sb, ps, sem = tools(nc, k, ctx, name)
        lst = sb("lst", [TQ, QT, P * 4])
        prev = sb("prev", [TQ, QT, P * 4])
        starts = sb("starts", [TQ, QT, P])
        breaks_sb = sb("breaks_sb", [TQ, QT, P], BF16)
        end = sb("end", [1, P], BF16)
        fields = [(0, o.place)] + ints + floats
        turned = ps("turned", [P, 8, 512])
        loaded = sem("loaded")
        found = sem("found")
        flagged = sem("flagged")
        turned_ok = sem("turned_ok")
        done = sem("done")
        stored = sem("stored")
        block = ctx.enter_context(nc.Block())

        def chunk_major(row):
            return table[row:row + NSLOT, :].rearrange("(q p e) f -> p q (e f)", q=QT, e=P)

        @block.sync
        def _(sp):
            sp.dma_start(lst[:], chunk_major(LEAD)).then_inc(loaded, 16)
            sp.dma_start(prev[:], chunk_major(LEAD - 1)).then_inc(loaded, 16)
            sp.wait_ge(flagged, 2)
            sp.dma_start(breaks[0:NSLOT].rearrange("(q p e) -> p q e", q=QT, e=P), breaks_sb[:]).then_inc(stored, 16)
            sp.dma_start(breaks[NSLOT:NSLOT + P].rearrange("(a b) -> a b", a=1), end[:]).then_inc(stored, 16)
            sp.wait_ge(stored, 32)

        @block.tensor
        def _(pe):
            pe.wait_ge(loaded, 32)
            for n, (f, _) in enumerate(fields):
                if n >= 2:
                    pe.wait_ge(done, n - 1)
                for q in range(QT):
                    last = nc.tensor.transpose(turned[:, 4 * (n % 2) + q // 4, (q % 4) * TQ:(q % 4 + 1) * TQ],
                                               lst[:, q, :].rearrange("p (e f) -> p f e", f=4)[:, f, :],
                                               k.ident[0:TQ, 0:TQ])
                last.then_inc(turned_ok, 1)
            pe.wait_ge(found, 1)
            n = len(fields)
            pe.wait_ge(done, n - 1)
            for q in range(QT):
                last = nc.tensor.transpose(turned[:, 4 * (n % 2) + q // 4, (q % 4) * TQ:(q % 4 + 1) * TQ],
                                           starts[:, q, :], k.ident[0:TQ, 0:TQ])
            last.then_inc(turned_ok, 1)

        @block.vector
        def _(dve):
            dve.wait_ge(loaded, 32)
            nc.vector.memset(end[:], -BIG)
            nc.vector.tensor_tensor(starts[:], lst[:].rearrange("p q (e f) -> p q e f", f=4)[:, :, :, 0],
                                    prev[:].rearrange("p q (e f) -> p q e f", f=4)[:, :, :, 0],
                                    ALU.not_equal).then_inc(found, 1)
            dve.wait_ge(found, 1)
            nc.vector.tensor_scalar(breaks_sb[:], starts[:], -BIG, None, ALU.mult).then_inc(flagged, 2)
            for n, (f, out) in enumerate(fields + [(None, o.begins)]):
                dve.wait_ge(turned_ok, n + 1)
                src = turned[:, 4 * (n % 2):4 * (n % 2) + QT // 4, 0:4 * TQ]
                dst = out[:, 0:CH].rearrange("p (a c) -> p a c", a=QT // 4)
                if n == 0:
                    base = o.block_base[:].rearrange("p (a c) -> p a c", a=QT // 4)
                    nc.vector.tensor_tensor(dst, src, base, ALU.subtract).then_inc(done, 1)
                else:
                    nc.vector.tensor_copy(dst, src).then_inc(done, 1)
            nc.vector.memset(o.place[:, CH:], -1.0)
            for _, out in ints + floats:
                nc.vector.memset(out[:, CH:], 0)


def hop(nc, k, o, table_in, table_out, name):
    with ExitStack() as ctx:
        sb, ps, sem = tools(nc, k, ctx, name)
        total = sb("total", [P, NBLK, D])
        rows = sb("rows", [P, SLOTS, G, D])
        ring = sb("ring", [P, SLOTS, G], I32)
        weighted = sb("weighted", [P, 2, G, P])
        sums = ps("sums", [P, 2, G, D])
        listed = sem("listed")
        got = [sem(f"got{s}") for s in range(SLOTS)]
        hot = sem("hot")
        summed = sem("summed")
        added = sem("added")
        cleared = sem("cleared")
        stored = sem("stored")
        running = sem("running")
        block = ctx.enter_context(nc.Block())

        @block.scalar
        def _(act):
            with act.Fori(0, ROUNDS) as i:
                for s in range(SLOTS):
                    act.wait_ge(summed, i * SLOTS + s + 1)
                    nc.scalar.copy(ring[:, s, :], o.other[:, bass.ds((i * SLOTS + s) * G, G)]).then_inc(listed, 1)

        @block.gpsimd
        def _(pool):
            with pool.Fori(0, ROUNDS) as i:
                for s in range(SLOTS):
                    pool.wait_ge(listed, i * SLOTS + s + 1)
                    pool.sem_inc(running, 1)
                    for g in range(G):
                        nc.gpsimd.indirect_dma_start(rows[:, s, g, :], None, table_in,
                                                     bass.IndirectOffsetOnAxis(ap=ring[:, s, g:g + 1], axis=0),
                                                     ).then_inc(got[s], 16)

        @block.tensor
        def _(pe):
            pe.sem_inc(summed, SLOTS)
            with pe.Fori(0, ROUNDS) as i:
                for s in range(SLOTS):
                    b = s % 2
                    pe.wait_ge(got[s], i * 16 * G + 16 * G)
                    pe.wait_ge(hot, i * SLOTS + s + 1)
                    pe.wait_ge(added, (i * SLOTS + s + 1) * G)
                    for g in range(G):
                        last = nc.tensor.matmul(sums[:, b, g, :], weighted[:, b, g, :], rows[:, s, g, :],
                                                start=True, stop=True)
                    last.then_inc(summed, 1)

        @block.vector
        def _(dve):
            def weigh(c, b, g):
                return nc.vector.tensor_scalar(weighted[:, b, g, :], k.count[:], o.place[:, bass.ds(c, 1)],
                                               o.weight[:, bass.ds(c, 1)], ALU.is_equal, ALU.mult)

            dve.sem_inc(added, 2 * G - 1)
            nc.vector.memset(total[:], 0.0).then_inc(added, 1)
            for g in range(G):
                last = weigh(g, 0, g)
            last.then_inc(hot, 1)
            with dve.Fori(0, ROUNDS) as i:
                for s in range(SLOTS):
                    b = s % 2
                    n = i * SLOTS + s
                    blocks = load_blocks(nc, dve.engine, o.block[:, bass.ds(n * G, G)], G)
                    dve.wait_ge(summed, n + SLOTS)
                    for g in range(G):
                        last = weigh(n * G + G + g, 1 - b, g)
                    last.then_inc(hot, 1)
                    dve.wait_ge(summed, n + 1 + SLOTS)
                    for g in range(G):
                        dve.wait_ge(added, n * G + g + 2 * G)
                        here = total[:, bass.ds(blocks[g], 1), :]
                        nc.vector.tensor_tensor(here, here, sums[:, b, g:g + 1, :], ALU.add).then_inc(added, 1)

        @block.sync
        def _(sp):
            sp.wait_ge(added, GROUPS * G + 2 * G)
            sp.dma_start(table_out.rearrange("(b p) f -> p b f", p=P), total[:]).then_inc(stored, 16)
            sp.wait_ge(stored, 16)


def segment_maximum(nc, k, o, breaks, heads, scores, minus, keep, name):
    strips = P // heads
    width = CH // strips
    length = width * P
    with ExitStack() as ctx:
        sb, ps, sem = tools(nc, k, ctx, name)
        line = sb("line", [P, length])
        line2 = sb("line2", [P, length])
        brk = sb("brk", [P, length + 1], BF16)
        piece = sb("piece", [P, 2, P])
        column = sb("column", [P, 4])
        row = sb("row", [1, 2, P])
        states = sb("states", [1, P])
        carry = sb("carry", [1, P])
        carried = sb("carried", [P, 1])
        turned = ps("turned", [P, 2, 512])
        small = ps("small", [P, 2, 512])
        back = ps("back", [P, 2, 512])
        loaded = sem("loaded")
        copied = sem("copied")
        turned_ok = sem("turned_ok")
        lined = sem("lined")
        d = sem("d")
        pe_step = sem("pe_step")
        piece2 = sem("piece2")
        back_ok = sem("back_ok")
        used = sem("used")
        view = [t[:].rearrange("p (s c) h -> p s c h", s=strips) for t in [scores, *minus]]
        keep_view = keep[:].rearrange("p (s c) h -> p s c h", s=strips) if keep is not None else None
        begins_view = o.begins[:].rearrange("p (s c) -> p s c", s=strips)
        block = ctx.enter_context(nc.Block())

        @block.sync
        def _(sp):
            for s in range(strips):
                sp.dma_start(brk[s * heads:(s + 1) * heads, :],
                             breaks[s * length:(s + 1) * length + 1].rearrange("(a l) -> a l", a=1)
                             .to_broadcast([heads, length + 1])).then_inc(loaded, 16)

        @block.scalar
        def _(act):
            with act.Fori(0, width // 2) as i:
                for b in range(2):
                    act.wait_ge(turned_ok, i * 2 + b + 1)
                    nc.scalar.copy(piece[:, b, :].rearrange("p (s h) -> p s h", h=heads),
                                   view[0][:, :, bass.ds(i * 2 + b, 1), :]).then_inc(copied, 1)
            act.wait_ge(d, DONE)
            with act.Fori(0, width // 2) as i:
                for b in range(2):
                    act.wait_ge(back_ok, i * 2 + b + 1)
                    nc.scalar.copy(piece[:, b, :], line[:, bass.ds((i * 2 + b) * P, P)]).then_inc(piece2, 1)

        @block.tensor
        def _(pe):
            pe.sem_inc(turned_ok, 2)
            pe.sem_inc(back_ok, 2)
            with pe.Fori(0, width // 2) as i:
                for b in range(2):
                    pe.wait_ge(copied, i * 2 + b + 1)
                    pe.wait_ge(lined, i * 2 + b + 1)
                    nc.tensor.transpose(turned[:, b, 0:P], piece[:, b, :], k.ident[:]).then_inc(turned_ok, 1)
            for step in range(2):
                pe.wait_ge(d, ENDS[step])
                nc.tensor.transpose(small[0:1, 0, 0:P], column[:, 2 * step:2 * step + 1], k.ident[:])
                nc.tensor.transpose(small[0:1, 0, P:2 * P], column[:, 2 * step + 1:2 * step + 2],
                                    k.ident[:]).then_inc(pe_step, 1)
                pe.wait_ge(d, CARRIES[step])
                nc.tensor.transpose(small[:, 1, 0:1], carry[:], k.ident[0:1, 0:1]).then_inc(pe_step, 1)
            with pe.Fori(0, width // 2) as i:
                for b in range(2):
                    pe.wait_ge(piece2, i * 2 + b + 1)
                    pe.wait_ge(used, i * 2 + b + 1)
                    nc.tensor.transpose(back[:, b, 0:P], piece[:, b, :], k.ident[:]).then_inc(back_ok, 1)

        @block.vector
        def _(dve):
            dve.sem_inc(lined, 2)
            dve.sem_inc(used, 2)
            with dve.Fori(0, width // 2) as i:
                for b in range(2):
                    dve.wait_ge(turned_ok, i * 2 + b + 3)
                    nc.vector.tensor_copy(line[:, bass.ds((i * 2 + b) * P, P)], turned[:, b, 0:P]).then_inc(lined, 1)
            dve.wait_ge(lined, width + 2)
            dve.wait_ge(loaded, 16 * strips)
            count = [0]

            def stepped(ins):
                count[0] += 1
                ins.then_inc(d, 1)
                dve.wait_ge(d, count[0])

            for step in range(2):
                flip = slice(None, None, -1 if step else 1)
                src, dst = (line, line2) if step == 0 else (line2, line)
                gaps = brk[:, 0:length] if step == 0 else brk[:, 1:length + 1]
                end = length - 1 if step == 0 else 0
                nc.vector.tensor_reduce(column[:, 2 * step:2 * step + 1], gaps, AX.X, ALU.min)
                stepped(nc.vector.tensor_tensor_scan(dst[:, flip], gaps[:, flip], src[:, flip], -BIG, ALU.add, ALU.max))
                stepped(nc.vector.tensor_copy(column[:, 2 * step + 1:2 * step + 2], dst[:, end:end + 1]))
                assert count[0] == ENDS[step]
                dve.wait_ge(pe_step, 2 * step + 1)
                stepped(nc.vector.tensor_copy(row[:], small[0:1, 0, 0:2 * P].rearrange("p (a c) -> p a c", a=2)))
                for h in range(heads):
                    way = row[:].rearrange("p a (s h) -> p a h s", h=heads)[:, :, h, :]
                    out = states[:].rearrange("p (s h) -> p h s", h=heads)[:, h, :]
                    last = nc.vector.tensor_tensor_scan(out[:, flip], way[:, 0, flip], way[:, 1, flip], -BIG,
                                                        ALU.add, ALU.max)
                stepped(last)
                nc.vector.memset(carry[:], -BIG).then_inc(d, 1)
                count[0] += 1
                dve.wait_ge(d, count[0])
                if step == 0:
                    stepped(nc.vector.tensor_copy(carry[:, heads:P], states[:, 0:P - heads]))
                else:
                    stepped(nc.vector.tensor_copy(carry[:, 0:P - heads], states[:, heads:P]))
                assert count[0] == CARRIES[step]
                dve.wait_ge(pe_step, 2 * step + 2)
                stepped(nc.vector.tensor_copy(carried[:], small[:, 1, 0:1]))
                if step == 0:
                    stepped(nc.vector.tensor_tensor_scan(dst[:, flip], gaps[:, flip], src[:, flip], carried[:],
                                                         ALU.add, ALU.max))
                else:
                    stepped(nc.vector.tensor_tensor_scan(line[:, flip], gaps[:, flip], src[:, flip], carried[:],
                                                         ALU.add, ALU.max))
            assert count[0] == DONE
            with dve.Fori(0, width // 2) as i:
                for b in range(2):
                    dve.wait_ge(back_ok, i * 2 + b + 3)
                    top = back[:, b, 0:P].rearrange("p (s h) -> p s h", h=heads)
                    c = bass.ds(i * 2 + b, 1)
                    if keep is not None:
                        nc.vector.tensor_tensor(keep_view[:, :, c, :].rearrange("p s c h -> p s (c h)"), top,
                                                begins_view[:, :, c].to_broadcast([P, strips, heads]), ALU.mult)
                    for v in view[1:]:
                        here = v[:, :, c, :].rearrange("p s c h -> p s (c h)")
                        last = nc.vector.tensor_tensor(here, here, top, ALU.subtract)
                    last.then_inc(used, 1)


ENDS = [2, 10]
CARRIES = [6, 14]
DONE = 16

NBD = NBLK + NBLK % 2
NPD = NBD * P


def score_pass(nc, k, o, index, table, row, head, values_at, store, spread, scores, extra, name):
    heads = D // head
    with ExitStack() as ctx:
        sb, ps, sem = tools(nc, k, ctx, name)
        rows = sb("rows", [P, SLOTS, G, row])
        ring = sb("ring", [P, SLOTS, G], I32)
        onehot = sb("onehot", [P, 2, G, P], BF16)
        onehot_t = sb("onehot_t", [P, 2, G, P], BF16)
        pair = sb("pair", [P, 2, G, D])
        turned = ps("turned", [P, 2, 2 * G, P], BF16)
        own = ps("own", [P, 2, G, D])
        own_self = ps("own_self", [P, 2, 512]) if extra else None
        listed = sem("listed")
        got = [sem(f"got{s}") for s in range(SLOTS)]
        kept = [sem(f"kept{s}") for s in range(SLOTS)]
        running = sem("running")
        hot = sem("hot")
        turned_ok = sem("turned_ok")
        copied = sem("copied")
        spread_ok = sem("spread_ok")
        scored = sem("scored")
        d = sem("d")
        steps = 4 if extra else 1
        block = ctx.enter_context(nc.Block())

        @block.scalar
        def _(act):
            def list_rows(n, s):
                act.wait_ge(scored, n + 1)
                nc.scalar.copy(ring[:, s, :], index[:, bass.ds(n * G, G)]).then_inc(listed, 1)

            act.sem_inc(copied, 2)
            for n in range(SLOTS - 1):
                list_rows(n, n)
            with act.Fori(0, ROUNDS) as i:
                for s in range(SLOTS):
                    n = i * SLOTS + s
                    b = s % 2
                    list_rows(n + SLOTS - 1, (s + SLOTS - 1) % SLOTS)
                    act.wait_ge(turned_ok, n + 2)
                    act.wait_ge(spread_ok, n + 1)
                    nc.scalar.copy(onehot_t[:, b, :, :], turned[:, b, 0:G, :]).then_inc(copied, 1)

        @block.gpsimd
        def _(pool):
            def a_round(i, first):
                for s in range(SLOTS):
                    if store is not None and not first:
                        pool.wait_ge(kept[s], i * 16)
                    pool.wait_ge(listed, i * SLOTS + s + 1)
                    pool.sem_inc(running, 1)
                    for g in range(G):
                        nc.gpsimd.indirect_dma_start(rows[:, s, g, :], None, table,
                                                     bass.IndirectOffsetOnAxis(ap=ring[:, s, g:g + 1], axis=0),
                                                     ).then_inc(got[s], 16)

            in_rounds(pool, ROUNDS, a_round)

        @block.sync
        def _(sp):
            if store is not None:
                with sp.Fori(0, ROUNDS) as i:
                    for s in range(SLOTS):
                        sp.wait_ge(got[s], i * 16 * G + 16 * G)
                        sp.dma_start(store[bass.ds(i * SLOTS + s, 1), :, :].rearrange("a p (g f) -> p (a g) f", g=G),
                                     rows[:, s, :, values_at:values_at + D]).then_inc(kept[s], 16)
                for s in range(SLOTS):
                    sp.wait_ge(kept[s], 16 * ROUNDS)

        @block.tensor
        def _(pe):
            pe.sem_inc(turned_ok, 1)
            pe.sem_inc(spread_ok, 2)
            with pe.Fori(0, ROUNDS) as i:
                for s in range(SLOTS):
                    n = i * SLOTS + s
                    b = s % 2
                    blocks = load_blocks(nc, pe.engine, o.block[:, bass.ds(n * G, G)], G)
                    pe.wait_ge(hot, n + 1)
                    pe.wait_ge(copied, n + 1)
                    for g in range(G):
                        last = nc.tensor.transpose(turned[:, b, g, :], onehot[:, b, g, :], k.identb[:])
                    last.then_inc(turned_ok, 1)
                    pe.wait_ge(copied, n + 3)
                    pe.wait_ge(scored, n + SLOTS - 1)
                    for g in range(G):
                        for part in range(3):
                            last = nc.tensor.matmul(own[:, b, g, :], onehot_t[:, b, g, :],
                                                    spread[:, bass.ds(blocks[g], 1), part, 0:D],
                                                    start=(part == 0), stop=(part == 2))
                        if extra:
                            for part in range(3):
                                last = nc.tensor.matmul(own_self[:, b, g * heads:(g + 1) * heads], onehot_t[:, b, g, :],
                                                        spread[:, bass.ds(blocks[g], 1), part, D:D + heads],
                                                        start=(part == 0), stop=(part == 2))
                    last.then_inc(spread_ok, 1)

        @block.vector
        def _(dve):
            def mark(c, b, g):
                return nc.vector.tensor_scalar(onehot[:, b, g, :], k.countb[:], o.place[:, bass.ds(c, 1)], None,
                                               ALU.is_equal)

            dve.sem_inc(scored, SLOTS)
            for g in range(G):
                last = mark(g, 0, g)
            last.then_inc(hot, 1)
            with dve.Fori(0, ROUNDS) as i:
                for s in range(SLOTS):
                    n = i * SLOTS + s
                    b = s % 2
                    dve.wait_ge(turned_ok, n + 1)
                    for g in range(G):
                        last = mark(n * G + G + g, 1 - b, g)
                    last.then_inc(hot, 1)
                    dve.wait_ge(spread_ok, n + 3)
                    dve.wait_ge(got[s], i * 16 * G + 16 * G)
                    dve.wait_ge(scored, n + SLOTS - 1)
                    here = bass.ds(n * G, G)
                    if not extra:
                        nc.vector.tensor_tensor(pair[:, b, :, :], own[:, b, :, :], rows[:, s, :, 0:D],
                                                ALU.mult).then_inc(d, 1)
                        dve.wait_ge(d, n + 1)
                        nc.vector.tensor_reduce(scores[:, here, :],
                                                pair[:, b, :, :].rearrange("p g (h f) -> p g h f", h=heads),
                                                AX.X, ALU.add).then_inc(scored, 1)
                    else:
                        att, self_score, top = extra
                        nc.vector.tensor_copy(self_score[:, here, :],
                                              own_self[:, b, 0:G * heads].rearrange("p (g h) -> p g h", h=heads))
                        nc.vector.tensor_tensor(pair[:, b, :, :], own[:, b, :, :], rows[:, s, :, 0:D],
                                                ALU.add).then_inc(d, 1)
                        dve.wait_ge(d, n * steps + 1)
                        flat = pair[:, b, :, :].rearrange("p g f -> p (g f)")
                        nc.vector.scalar_tensor_tensor(out=flat, in0=flat, scalar=0.2, in1=flat, op0=ALU.mult,
                                                       op1=ALU.max).then_inc(d, 1)
                        dve.wait_ge(d, n * steps + 2)
                        nc.vector.tensor_tensor(flat, flat, att[:], ALU.mult).then_inc(d, 1)
                        dve.wait_ge(d, n * steps + 3)
                        nc.vector.tensor_reduce(scores[:, here, :],
                                                pair[:, b, :, :].rearrange("p g (h f) -> p g h f", h=heads),
                                                AX.X, ALU.add).then_inc(d, 1)
                        dve.wait_ge(d, n * steps + 4)
                        nc.vector.tensor_tensor(top[:, here, :], scores[:, here, :], self_score[:, here, :],
                                                ALU.max).then_inc(scored, 1)


def exponentials(nc, k, tensors, begins, name):
    with ExitStack() as ctx:
        sb, ps, sem = tools(nc, k, ctx, name)
        raised = sem("raised")
        block = ctx.enter_context(nc.Block())

        @block.scalar
        def _(act):
            for t in tensors:
                nc.scalar.activation(t[:], t[:], ACT.Exp).then_inc(raised, 1)

        @block.vector
        def _(dve):
            if begins is not None:
                dve.wait_ge(raised, len(tensors))
                t = tensors[-1]
                nc.vector.tensor_tensor(t[:], t[:], begins[:, 0:CH].rearrange("p (c a) -> p c a", a=1)
                                        .to_broadcast([P, CH, t[:].shape[2]]), ALU.mult)


def sum_pass(nc, k, o, store, weights, extras, total, name):
    extra_w = sum(t[:].shape[2] for t in extras)
    width = extra_w + (D if store is not None else 0)
    with ExitStack() as ctx:
        sb, ps, sem = tools(nc, k, ctx, name)
        values = sb("values", [P, SLOTS, G * D]) if store is not None else None
        terms = sb("terms", [P, 2, G, width])
        onehot = sb("onehot", [P, 2, G, P])
        sums = ps("sums", [P, 2, 2, 512])
        loaded = [sem(f"loaded{s}") for s in range(SLOTS)]
        hot = sem("hot")
        taken = sem("taken")
        weighed = sem("weighed")
        summed = sem("summed")
        added = sem("added")
        block = ctx.enter_context(nc.Block())

        if store is not None:
            @block.sync
            def _(sp):
                with sp.Fori(0, ROUNDS) as i:
                    for s in range(SLOTS):
                        sp.wait_ge(weighed, i * SLOTS + s + 1)
                        sp.dma_start(values[:, s, :], store[bass.ds(i * SLOTS + s, 1), :, :]
                                     .rearrange("a p f -> p (a f)")).then_inc(loaded[s], 16)

        @block.scalar
        def _(act):
            with act.Fori(0, GROUPS // 2) as i:
                for b in range(2):
                    act.wait_ge(summed, i * 2 + b + 1)
                    at = width - extra_w
                    for t in extras:
                        w = t[:].shape[2]
                        last = nc.scalar.copy(terms[:, b, :, at:at + w], t[:, bass.ds((i * 2 + b) * G, G), :])
                        at += w
                    last.then_inc(taken, 1)

        @block.tensor
        def _(pe):
            pe.sem_inc(summed, 2)
            with pe.Fori(0, ROUNDS) as i:
                for s in range(SLOTS):
                    n = i * SLOTS + s
                    b = s % 2
                    pe.wait_ge(hot, n + 1)
                    pe.wait_ge(taken, n + 1)
                    if store is not None:
                        pe.wait_ge(weighed, n + 1 + SLOTS)
                    pe.wait_ge(added, (n + 1) * G)
                    for g in range(G):
                        last = nc.tensor.matmul(sums[:, b, g // 2, (g % 2) * width:(g % 2 + 1) * width],
                                                onehot[:, b, g, :], terms[:, b, g, :], start=True, stop=True)
                    last.then_inc(summed, 1)

        @block.vector
        def _(dve):
            def mark(c, b, g):
                return nc.vector.tensor_scalar(onehot[:, b, g, :], k.count[:], o.place[:, bass.ds(c, 1)], None,
                                               ALU.is_equal)

            dve.sem_inc(added, 2 * G - 1)
            dve.sem_inc(weighed, SLOTS)
            nc.vector.memset(total[:], 0.0).then_inc(added, 1)
            for g in range(G):
                last = mark(g, 0, g)
            last.then_inc(hot, 1)
            with dve.Fori(0, ROUNDS) as i:
                for s in range(SLOTS):
                    n = i * SLOTS + s
                    b = s % 2
                    blocks = load_blocks(nc, dve.engine, o.block[:, bass.ds(n * G, G)], G)
                    dve.wait_ge(summed, n + 1)
                    if store is not None:
                        dve.wait_ge(loaded[s], i * 16 + 16)
                        heads = weights[:].shape[2]
                        weight = weights[:, bass.ds(n * G, G), :].rearrange("p g (h a) -> p g h a", a=1)
                        nc.vector.tensor_tensor(
                            terms[:, b, :, 0:D].rearrange("p g (h f) -> p g h f", h=heads),
                            values[:, s, :].rearrange("p (g h f) -> p g h f", g=G, h=heads),
                            weight.to_broadcast([P, G, heads, D // heads]), ALU.mult).then_inc(weighed, 1)
                    dve.wait_ge(summed, n + 2)
                    for g in range(G):
                        last = mark(n * G + G + g, 1 - b, g)
                    last.then_inc(hot, 1)
                    dve.wait_ge(summed, n + 3)
                    for g in range(G):
                        dve.wait_ge(added, n * G + g + 2 * G)
                        here = total[:, bass.ds(blocks[g], 1), :]
                        part = sums[:, b, g // 2:g // 2 + 1, (g % 2) * width:(g % 2 + 1) * width]
                        nc.vector.tensor_tensor(here, here, part, ALU.add).then_inc(added, 1)


def weigh_and_sum(nc, k, o, index, table, spread, total, name):
    heads = 8
    row = 2 * D + heads
    with ExitStack() as ctx:
        sb, ps, sem = tools(nc, k, ctx, name)
        rows = sb("rows", [P, SLOTS, G, row])
        ring = sb("ring", [P, SLOTS, G], I32)
        onehot = sb("onehot", [P, 2, G, P], BF16)
        onehot_f = sb("onehot_f", [P, 2, G, P])
        onehot_t = sb("onehot_t", [P, 2, G, P], BF16)
        pair = sb("pair", [P, 2, G, D])
        score = sb("score", [P, 2, G, heads])
        weight = sb("weight", [P, 2, G, heads])
        terms = sb("terms", [P, 2, G, D])
        turned = ps("turned", [P, 2, 2 * G, P], BF16)
        own = ps("own", [P, 2, G, D])
        sums = ps("sums", [P, 2, G, D])
        listed = sem("listed")
        got = [sem(f"got{s}") for s in range(SLOTS)]
        running = sem("running")
        hot = sem("hot")
        turned_ok = sem("turned_ok")
        copied = sem("copied")
        widened = sem("widened")
        spread_ok = sem("spread_ok")
        lowered = sem("lowered")
        raised = sem("raised")
        weighed = sem("weighed")
        summed = sem("summed")
        added = sem("added")
        d = sem("d")
        block = ctx.enter_context(nc.Block())

        @block.scalar
        def _(act):
            def list_rows(n, s):
                act.wait_ge(weighed, n + 1)
                nc.scalar.copy(ring[:, s, :], index[:, bass.ds(n * G, G)]).then_inc(listed, 1)

            def take_onehots(n, b):
                act.wait_ge(turned_ok, n + 2)
                act.wait_ge(spread_ok, n + 1)
                nc.scalar.copy(onehot_t[:, b, :, :], turned[:, b, 0:G, :]).then_inc(copied, 1)
                act.wait_ge(summed, n + 1)
                nc.scalar.copy(onehot_f[:, b, :, :], onehot[:, b, :, :]).then_inc(widened, 1)

            act.sem_inc(copied, 2)
            for n in range(SLOTS - 1):
                list_rows(n, n)
            take_onehots(0, 0)
            with act.Fori(0, ROUNDS) as i:
                for s in range(SLOTS):
                    n = i * SLOTS + s
                    b = s % 2
                    list_rows(n + SLOTS - 1, (s + SLOTS - 1) % SLOTS)
                    act.wait_ge(lowered, n + 1)
                    nc.scalar.activation(weight[:, b, :, :], score[:, b, :, :], ACT.Exp).then_inc(raised, 1)
                    take_onehots(n + 1, 1 - b)

        @block.gpsimd
        def _(pool):
            with pool.Fori(0, ROUNDS) as i:
                for s in range(SLOTS):
                    pool.wait_ge(listed, i * SLOTS + s + 1)
                    pool.sem_inc(running, 1)
                    for g in range(G):
                        nc.gpsimd.indirect_dma_start(rows[:, s, g, :], None, table,
                                                     bass.IndirectOffsetOnAxis(ap=ring[:, s, g:g + 1], axis=0),
                                                     ).then_inc(got[s], 16)

        @block.tensor
        def _(pe):
            def spread_own(n, b):
                blocks = load_blocks(nc, pe.engine, o.block[:, bass.ds(n * G, G)], G)
                pe.wait_ge(hot, n + 1)
                pe.wait_ge(copied, n + 1)
                for g in range(G):
                    last = nc.tensor.transpose(turned[:, b, g, :], onehot[:, b, g, :], k.identb[:])
                last.then_inc(turned_ok, 1)
                pe.wait_ge(copied, n + 3)
                pe.wait_ge(weighed, n + SLOTS - 1)
                for g in range(G):
                    for part in range(3):
                        last = nc.tensor.matmul(own[:, b, g, :], onehot_t[:, b, g, :],
                                                spread[:, bass.ds(blocks[g], 1), part, 0:D],
                                                start=(part == 0), stop=(part == 2))
                last.then_inc(spread_ok, 1)

            pe.sem_inc(turned_ok, 1)
            pe.sem_inc(spread_ok, 2)
            pe.sem_inc(summed, 2)
            spread_own(0, 0)
            with pe.Fori(0, ROUNDS) as i:
                for s in range(SLOTS):
                    n = i * SLOTS + s
                    b = s % 2
                    spread_own(n + 1, 1 - b)
                    pe.wait_ge(weighed, n + 1 + SLOTS)
                    pe.wait_ge(widened, n + 1)
                    pe.wait_ge(added, (n + 1) * G)
                    for g in range(G):
                        last = nc.tensor.matmul(sums[:, b, g, :], onehot_f[:, b, g, :], terms[:, b, g, :],
                                                start=True, stop=True)
                    last.then_inc(summed, 1)

        @block.vector
        def _(dve):
            def mark(c, b, g):
                return nc.vector.tensor_scalar(onehot[:, b, g, :], k.countb[:], o.place[:, bass.ds(c, 1)], None,
                                               ALU.is_equal)

            def add(n, b):
                blocks = load_blocks(nc, dve.engine, o.block[:, bass.ds(n * G, G)], G)
                dve.wait_ge(summed, n + 3)
                for g in range(G):
                    dve.wait_ge(added, n * G + g + 2 * G)
                    here = total[:, bass.ds(blocks[g], 1), :]
                    nc.vector.tensor_tensor(here, here, sums[:, b, g:g + 1, :], ALU.add).then_inc(added, 1)

            dve.sem_inc(added, 2 * G - 1)
            dve.sem_inc(weighed, SLOTS)
            nc.vector.memset(total[:], 0.0).then_inc(added, 1)
            for g in range(G):
                last = mark(g, 0, g)
            last.then_inc(hot, 1)

            def a_round(i, first):
                for s in range(SLOTS):
                    n = i * SLOTS + s
                    b = s % 2
                    dve.wait_ge(spread_ok, n + 3)
                    dve.wait_ge(got[s], i * 16 * G + 16 * G)
                    dve.wait_ge(weighed, n + SLOTS - 1)
                    nc.vector.tensor_tensor(pair[:, b, :, :], own[:, b, :, :], rows[:, s, :, 0:D],
                                            ALU.mult).then_inc(d, 1)
                    dve.wait_ge(turned_ok, n + 1)
                    if not (first and s == 0):
                        dve.wait_ge(widened, n)
                    for g in range(2):
                        mark(n * G + G + g, 1 - b, g)
                    dve.wait_ge(d, n * 3 + 1)
                    nc.vector.tensor_reduce(score[:, b, :, :],
                                            pair[:, b, :, :].rearrange("p g (h f) -> p g h f", h=heads),
                                            AX.X, ALU.add).then_inc(d, 1)
                    dve.wait_ge(d, n * 3 + 2)
                    nc.vector.tensor_tensor(score[:, b, :, :], score[:, b, :, :], rows[:, s, :, 2 * D:row],
                                            ALU.subtract).then_inc(d, 1)
                    dve.wait_ge(d, n * 3 + 3)
                    nc.vector.tensor_single_scalar(score[:, b, :, :], score[:, b, :, :], 0.0,
                                                   ALU.min).then_inc(lowered, 1)
                    for g in range(2, G):
                        last = mark(n * G + G + g, 1 - b, g)
                    last.then_inc(hot, 1)
                    if not (first and s == 0):
                        add(n - 1, 1 - b)
                    dve.wait_ge(raised, n + 1)
                    dve.wait_ge(summed, n + 1)
                    nc.vector.tensor_tensor(
                        terms[:, b, :, :].rearrange("p g (h f) -> p g h f", h=heads),
                        rows[:, s, :, D:2 * D].rearrange("p g (h f) -> p g h f", h=heads),
                        weight[:, b, :, :].rearrange("p g (h a) -> p g h a", a=1)
                        .to_broadcast([P, G, heads, D // heads]), ALU.mult).then_inc(weighed, 1)

            in_rounds(dve, ROUNDS, a_round)
            add(GROUPS - 1, 1)

HEADS1, HEADS2, HEADS3 = 8, 4, 8
PIECE = 10
PIECES = NBD // PIECE
assert PIECES * PIECE == NBD


def in_steps(engine, step):
    count = [0]

    def take(instruction):
        count[0] += 1
        instruction.then_inc(step, 1)
        engine.wait_ge(step, count[0])

    return take


def turn_weights(nc, k, pairs, name):
    with ExitStack() as ctx:
        sb, ps, sem = tools(nc, k, ctx, name)
        w = sb("w", [P, len(pairs), D])
        turned = ps("turned", [P, 512])
        loaded = sem("loaded")
        turned_ok = sem("turned_ok")
        block = ctx.enter_context(nc.Block())

        @block.sync
        def _(sp):
            for n, (_, source) in enumerate(pairs):
                sp.dma_start(w[:, n, :], source).then_inc(loaded, 16)

        @block.tensor
        def _(pe):
            pe.wait_ge(loaded, 16 * len(pairs))
            for n in range(len(pairs)):
                last = nc.tensor.transpose(turned[:, n * D:(n + 1) * D], w[:, n, :], k.ident[:])
            last.then_inc(turned_ok, 1)

        @block.vector
        def _(dve):
            dve.wait_ge(turned_ok, 1)
            for n, (out, _) in enumerate(pairs):
                nc.vector.tensor_copy(out, turned[:, n * D:(n + 1) * D])


def load_all(nc, k, pairs, name):
    with ExitStack() as ctx:
        sb, ps, sem = tools(nc, k, ctx, name)
        loaded = sem("loaded")
        block = ctx.enter_context(nc.Block())

        @block.sync
        def _(sp):
            for out, source in pairs:
                sp.dma_start(out, source).then_inc(loaded, 16)
            sp.wait_ge(loaded, 16 * len(pairs))


def row_on_all(vector):
    return vector.rearrange("(a f) -> a f", a=1).to_broadcast([P, vector.shape[0]])


def split_parts(nc, k, source, spread, at, name):
    width = source.shape[2]
    with ExitStack() as ctx:
        sb, ps, sem = tools(nc, k, ctx, name)
        step = sem("step")
        block = ctx.enter_context(nc.Block())

        @block.vector
        def _(dve):
            chain = in_steps(dve, step)
            for part in range(3):
                out = spread[:, :, part, at:at + width]
                chain(nc.vector.tensor_copy(out, source))
                if part < 2:
                    chain(nc.vector.tensor_tensor(source, source, out, ALU.subtract))


def layernorm(nc, k, x, out, name):
    with ExitStack() as ctx:
        sb, ps, sem = tools(nc, k, ctx, name)
        square = sb("square", [P, 2, PIECE, D])
        mean = sb("mean", [P, NBD])
        var = sb("var", [P, NBD])
        root = sb("root", [P, NBD])
        scale = sb("scale", [P, NBD])
        centred = sem("centred")
        squared = sem("squared")
        summed = sem("summed")
        deviated = sem("deviated")
        step = sem("step")
        scaled = sem("scaled")
        stored = sem("stored")
        block = ctx.enter_context(nc.Block())
        spread = lambda t, n: t[:, n * PIECE:(n + 1) * PIECE].rearrange("p (b a) -> p b a", a=1).to_broadcast([P, PIECE, D])

        @block.vector
        def _(dve):
            chain = in_steps(dve, step)
            dve.sem_inc(summed, 2)
            for n in range(PIECES):
                here = x[:, n * PIECE:(n + 1) * PIECE, :]
                m = mean[:, n * PIECE:(n + 1) * PIECE]
                chain(nc.vector.tensor_reduce(m, here, AX.X, ALU.add))
                chain(nc.vector.tensor_scalar(m, m, 1.0 / D, None, ALU.mult))
                nc.vector.tensor_tensor(here, here, spread(mean, n), ALU.subtract).then_inc(centred, 1)
            for n in range(PIECES):
                dve.wait_ge(squared, n + 1)
                nc.vector.tensor_reduce(var[:, n * PIECE:(n + 1) * PIECE], square[:, n % 2, :, :], AX.X,
                                        ALU.add).then_inc(summed, 1)
            dve.wait_ge(summed, PIECES + 2)
            chain(nc.vector.tensor_scalar(var[:], var[:], 1.0 / D, EPS, ALU.mult, ALU.add))
            dve.wait_ge(deviated, 1)
            chain(nc.vector.reciprocal(scale[:], root[:]))
            for n in range(PIECES):
                here = x[:, n * PIECE:(n + 1) * PIECE, :]
                nc.vector.tensor_tensor(here, here, spread(scale, n), ALU.mult).then_inc(scaled, 1)

        @block.scalar
        def _(act):
            for n in range(PIECES):
                act.wait_ge(centred, n + 1)
                act.wait_ge(summed, n + 1)
                nc.scalar.activation(square[:, n % 2, :, :], x[:, n * PIECE:(n + 1) * PIECE, :],
                                     ACT.Square).then_inc(squared, 1)
            act.wait_ge(step, 2 * PIECES + 1)
            nc.scalar.activation(root[:], var[:], ACT.Sqrt).then_inc(deviated, 1)

        if out is not None:
            @block.sync
            def _(sp):
                full = NBLK - 1
                sp.wait_ge(scaled, PIECES)
                sp.dma_start(out[0:full * P, :].rearrange("(b p) f -> p b f", p=P), x[:, 0:full, :]).then_inc(stored, 16)
                sp.dma_start(out[full * P:N, :], x[0:TAIL, full, :]).then_inc(stored, 16)
                sp.wait_ge(stored, 32)


def polynomial(nc, k, hops, weights, name):
    with ExitStack() as ctx:
        sb, ps, sem = tools(nc, k, ctx, name)
        w = sb("w", [P, 4, D])
        z = sb("z", [P, 2, 4, D])
        zt = sb("zt", [P, 2, 4, P])
        turned = ps("turned", [P, 2, 4, P])
        y = ps("y", [P, 2, 512])
        loaded_w = sem("loaded_w")
        loaded = [sem("loaded0"), sem("loaded1")]
        own = sem("own")
        turned_ok = sem("turned_ok")
        copied = sem("copied")
        mixed = sem("mixed")
        added = sem("added")
        block = ctx.enter_context(nc.Block())

        @block.sync
        def _(sp):
            sp.dma_start(w[:], weights.rearrange("t p f -> p t f")).then_inc(loaded_w, 16)
            with sp.Fori(0, NBD // 2) as i:
                for b in range(2):
                    n = i * 2 + b
                    sp.wait_ge(turned_ok, n + 1)
                    for h in range(3):
                        sp.dma_start(z[:, b, 1 + h, :], hops[h][bass.ds(n * P, P), :]).then_inc(loaded[b], 16)

        @block.scalar
        def _(act):
            act.sem_inc(copied, 1)
            with act.Fori(0, NBD // 2) as i:
                for b in range(2):
                    n = i * 2 + b
                    act.wait_ge(turned_ok, n + 1)
                    nc.scalar.copy(z[:, b, 0, :], k.x[:, bass.ds(n, 1), :]).then_inc(own, 1)
                    act.wait_ge(turned_ok, n + 3)
                    act.wait_ge(mixed, n + 1)
                    nc.scalar.copy(zt[:, b, :, :], turned[:, b, :, :]).then_inc(copied, 1)

        @block.tensor
        def _(pe):
            pe.sem_inc(turned_ok, 2)
            pe.sem_inc(mixed, 2)
            pe.wait_ge(loaded_w, 16)
            with pe.Fori(0, NBD // 2) as i:
                for b in range(2):
                    n = i * 2 + b
                    pe.wait_ge(loaded[b], i * 48 + 48)
                    pe.wait_ge(own, n + 1)
                    pe.wait_ge(copied, n + 1)
                    for t in range(4):
                        last = nc.tensor.transpose(turned[:, b, t, :], z[:, b, t, :], k.ident[:])
                    last.then_inc(turned_ok, 1)
                    pe.wait_ge(copied, n + 2)
                    pe.wait_ge(added, n + 1)
                    for t in range(4):
                        last = nc.tensor.matmul(y[:, b, 0:D], zt[:, b, t, :], w[:, t, :], start=(t == 0), stop=(t == 3))
                    last.then_inc(mixed, 1)

        @block.vector
        def _(dve):
            dve.sem_inc(added, 2)
            with dve.Fori(0, NBD // 2) as i:
                for b in range(2):
                    n = i * 2 + b
                    dve.wait_ge(mixed, n + 3)
                    here = k.x[:, bass.ds(n, 1), :]
                    nc.vector.scalar_tensor_tensor(out=here, in0=y[:, b:b + 1, 0:D], scalar=float(D) ** -0.5, in1=here,
                                                   op0=ALU.mult, op1=ALU.add).then_inc(added, 1)


def type_weights(nc, k, node_type, comps, mix, name):
    with ExitStack() as ctx:
        sb, ps, sem = tools(nc, k, ctx, name)
        kind_i = sb("kind_i", [P, NBD], I32)
        kind = sb("kind", [P, NBD])
        comp = sb("comp", [P, TYPES, 4 * BASES])
        is_type = sb("is_type", [P, 2, NBD])
        part = sb("part", [P, 2, NBD, 4 * BASES])
        step = sem("step")
        padded = sem("padded")
        loaded = sem("loaded")
        full = NBLK - 1
        block = ctx.enter_context(nc.Block())

        @block.sync
        def _(sp):
            for n, c in enumerate(comps):
                sp.dma_start(comp[:, :, n * BASES:(n + 1) * BASES],
                             c.rearrange("(a t) b -> a t b", a=1).to_broadcast([P, TYPES, BASES])).then_inc(loaded, 16)
            sp.wait_ge(padded, 1)
            with nc.allow_non_contiguous_dma(reason="one integer per node, once"):
                sp.dma_start(kind_i[:, 0:full], node_type[0:full * P].rearrange("(b p) -> p b", p=P)).then_inc(loaded, 16)
                sp.dma_start(kind_i[0:TAIL, full:full + 1],
                             node_type[full * P:N].rearrange("(p a) -> p a", a=1)).then_inc(loaded, 16)

        @block.vector
        def _(dve):
            chain = in_steps(dve, step)
            nc.vector.memset(kind_i[:], 0).then_inc(padded, 1)
            nc.vector.memset(mix[:], 0.0)
            dve.wait_ge(loaded, 16 * 6)
            chain(nc.vector.tensor_copy(kind[:], kind_i[:]))
            for t in range(TYPES):
                chain(nc.vector.tensor_single_scalar(is_type[:, t % 2, :], kind[:], float(t), ALU.is_equal))
                chain(nc.vector.tensor_tensor(
                    part[:, t % 2, :, :],
                    is_type[:, t % 2, :].rearrange("p (b a) -> p b a", a=1).to_broadcast([P, NBD, 4 * BASES]),
                    comp[:, t:t + 1, :].to_broadcast([P, NBD, 4 * BASES]), ALU.mult))
                chain(nc.vector.tensor_tensor(mix[:], mix[:], part[:, t % 2, :, :], ALU.add))


def relation_weights(nc, k, att, msg, pri, att_sb, msg_sb, name):
    head = D // HEADS1
    with ExitStack() as ctx:
        sb, ps, sem = tools(nc, k, ctx, name)
        priority = sb("priority", [P, TYPES * HEADS1])
        cleared = sem("cleared")
        loaded = sem("loaded")
        block = ctx.enter_context(nc.Block())

        @block.vector
        def _(dve):
            nc.vector.memset(att_sb[:], 0.0)
            nc.vector.memset(msg_sb[:], 0.0).then_inc(cleared, 1)
            dve.wait_ge(loaded, 16 * (2 * HEADS1 + 1))
            a = att_sb[:].rearrange("p t (h j) -> p (t h) j", h=HEADS1)
            nc.vector.scalar_tensor_tensor(out=a, in0=a, scalar=float(head) ** -0.5,
                                           in1=priority[:].rearrange("p (t a) -> p t a", a=1)
                                           .to_broadcast([P, TYPES * HEADS1, head]), op0=ALU.mult, op1=ALU.mult)

        @block.sync
        def _(sp):
            sp.dma_start(priority[:], row_on_all(pri.rearrange("t h -> (t h)"))).then_inc(loaded, 16)
            sp.wait_ge(cleared, 1)
            for source, out in ((att, att_sb), (msg, msg_sb)):
                for h in range(HEADS1):
                    sp.dma_start(out[h * head:(h + 1) * head, :, h * head:(h + 1) * head],
                                 source[:, h, :, :].rearrange("t i j -> i t j")).then_inc(loaded, 16)


def relation_tables(nc, k, bases, att_sb, msg_sb, mix, queries, table, name):
    with ExitStack() as ctx:
        sb, ps, sem = tools(nc, k, ctx, name)
        w = sb("w", [P, 3, BASES * D])
        x = sb("x", [P, 2, D])
        xt = sb("xt", [P, 2, P])
        scaled = sb("scaled", [P, 4, D])
        kv = sb("kv", [P, 2, D])
        kvt = sb("kvt", [P, 2, P])
        rows = sb("rows", [P, 2, TYPES, 2 * D])
        turned = ps("turned", [P, 4, P])
        based = ps("based", [P, 3, BASES, D])
        related = ps("related", [P, 4, 4, D])
        loaded = sem("loaded")
        own = sem("own")
        turned_x = sem("turned_x")
        xt_ok = sem("xt_ok")
        based_ok = sem("based_ok")
        mixed = sem("mixed")
        d = sem("d")
        turned_kv = sem("turned_kv")
        kvt_ok = sem("kvt_ok")
        related_ok = sem("related_ok")
        left = sem("left")
        right = sem("right")
        stored = [sem("stored0"), sem("stored1")]
        block = ctx.enter_context(nc.Block())
        rows_of = lambda b, half: rows[:, b, :, half * D:(half + 1) * D]

        @block.sync
        def _(sp):
            for n, base in enumerate(bases):
                sp.dma_start(w[:, n, :].rearrange("p (b o) -> p b o", b=BASES),
                             base.rearrange("b (i o) -> i b o", o=D)).then_inc(loaded, 16)
            with sp.Fori(0, NBD // 2) as i:
                for b in range(2):
                    n = i * 2 + b
                    sp.wait_ge(left, n + 1)
                    sp.wait_ge(right, n + 1)
                    sp.dma_start(table[:, bass.ds(n * P, P), :].rearrange("t p f -> p t f"),
                                 rows[:, b, :, :]).then_inc(stored[b], 16)
            for b in range(2):
                sp.wait_ge(stored[b], 16 * (NBD // 2))

        @block.scalar
        def _(act):
            def a_round(i, first):
                for b in range(2):
                    n = i * 2 + b
                    act.wait_ge(turned_x, n + 1)
                    nc.scalar.copy(x[:, b, :], k.x[:, bass.ds(n, 1), :]).then_inc(own, 1)
                    act.wait_ge(turned_x, n + 3)
                    nc.scalar.copy(xt[:, b, :], turned[:, 0, :]).then_inc(xt_ok, 1)
                    act.wait_ge(turned_kv, n + 1)
                    nc.scalar.copy(kvt[:], turned[:, 2:4, :]).then_inc(kvt_ok, 1)
                    act.wait_ge(related_ok, n + 1)
                    if not first:
                        act.wait_ge(stored[b], i * 16)
                    nc.scalar.copy(rows_of(b, 0), related[:, 0:2, :, :].rearrange("p a t f -> p (a t) f")).then_inc(left, 1)

            in_rounds(act, NBD // 2, a_round)

        @block.tensor
        def _(pe):
            pe.sem_inc(turned_x, 2)
            pe.wait_ge(loaded, 48)
            def a_block(i, b, first):
                    n = i * 2 + b
                    pe.wait_ge(own, n + 1)
                    if not first:
                        pe.wait_ge(kvt_ok, n)
                        pe.wait_ge(mixed, n)
                    nc.tensor.transpose(turned[:, 0, :], x[:, b, :], k.ident[:]).then_inc(turned_x, 1)
                    pe.wait_ge(xt_ok, n + 1)
                    for j in range(3):
                        nc.tensor.matmul(based[:, j, :, :], xt[:, b, :], w[:, j, :], start=True,
                                         stop=True).then_inc(based_ok, 1)
                    pe.wait_ge(mixed, n + 1)
                    for j in range(2):
                        last = nc.tensor.transpose(turned[:, 2 + j, :], kv[:, j, :], k.ident[:])
                    last.then_inc(turned_kv, 1)
                    pe.wait_ge(kvt_ok, n + 1)
                    if not first:
                        pe.wait_ge(left, n)
                        pe.wait_ge(right, n)
                    for j, rel in enumerate((att_sb, msg_sb)):
                        for half in range(2):
                            last = nc.tensor.matmul(related[:, 2 * j + half, :, :], kvt[:, j, :],
                                                    rel[:, 4 * half:4 * half + 4, :], start=True, stop=True)
                    last.then_inc(related_ok, 1)

            a_block(0, 0, True)
            a_block(0, 1, False)
            with pe.Fori(1, NBD // 2) as i:
                for b in range(2):
                    a_block(i, b, False)

        @block.vector
        def _(dve):
            def a_round(i, first):
                for b in range(2):
                    n = i * 2 + b
                    steps = 9
                    for basis in range(BASES):
                        for j, out in enumerate((queries[:, bass.ds(n, 1), :], kv[:, 0:1, :], kv[:, 1:2, :])):
                            part = based[:, j:j + 1, basis, :]
                            by = mix[:, bass.ds(n, 1), j * BASES + basis:j * BASES + basis + 1].rearrange("p a b -> p (a b)")
                            if basis == 0:
                                dve.wait_ge(based_ok, n * 3 + 1 + j)
                                if j > 0 and not (first and b == 0):
                                    dve.wait_ge(turned_kv, n)
                                last = nc.vector.tensor_scalar(out, part, by, None, ALU.mult)
                            else:
                                dve.wait_ge(d, n * 12 + (basis - 1) * 3 + j + 1)
                                last = nc.vector.scalar_tensor_tensor(out=out, in0=part, scalar=by, in1=out,
                                                                      op0=ALU.mult, op1=ALU.add)
                            last.then_inc(d, 1)
                    dve.wait_ge(d, n * 12 + 12)
                    dve.sem_inc(mixed, 1)
                    dve.wait_ge(related_ok, n + 1)
                    if not first:
                        dve.wait_ge(stored[b], i * 16)
                    nc.vector.tensor_copy(rows_of(b, 1), related[:, 2:4, :, :].rearrange("p a t f -> p (a t) f")).then_inc(right, 1)

            in_rounds(dve, NBD // 2, a_round)


def relation_output(nc, k, total, base, loop_w, bias, mix, name):
    with ExitStack() as ctx:
        sb, ps, sem = tools(nc, k, ctx, name)
        w = sb("w", [P, BASES * D])
        wl = sb("wl", [P, D])
        bias_row = sb("bias_row", [P, D])
        inputs = sb("inputs", [P, 2, 2, D])
        turned_sb = sb("turned_sb", [P, 2, 2, P])
        mixed = sb("mixed", [P, 2, D])
        turned = ps("turned", [P, 2, 4, P])
        based = ps("based", [P, 2, BASES, D])
        looped = ps("looped", [P, 2, 512])
        loaded = sem("loaded")
        normed = sem("normed")
        step = sem("step")
        own = sem("own")
        turned_ok = sem("turned_ok")
        copied = sem("copied")
        based_ok = sem("based_ok")
        d = sem("d")
        done = sem("done")
        block = ctx.enter_context(nc.Block())

        @block.sync
        def _(sp):
            sp.dma_start(w[:].rearrange("p (b o) -> p b o", b=BASES), base.rearrange("b (i o) -> i b o", o=D)).then_inc(loaded, 16)
            sp.dma_start(wl[:], loop_w).then_inc(loaded, 16)
            sp.dma_start(bias_row[:], row_on_all(bias)).then_inc(loaded, 16)

        @block.scalar
        def _(act):
            act.wait_ge(normed, NBLK)
            act.sem_inc(copied, 1)
            with act.Fori(0, NBD // 2) as i:
                for b in range(2):
                    n = i * 2 + b
                    act.wait_ge(turned_ok, n + 1)
                    nc.scalar.copy(inputs[:, b, 0, :], total[:, bass.ds(n, 1), 0:D])
                    nc.scalar.copy(inputs[:, b, 1, :], k.x[:, bass.ds(n, 1), :]).then_inc(own, 1)
                    act.wait_ge(turned_ok, n + 3)
                    act.wait_ge(based_ok, n + 1)
                    nc.scalar.copy(turned_sb[:, b, :, :], turned[:, b, 0:2, :]).then_inc(copied, 1)

        @block.tensor
        def _(pe):
            pe.sem_inc(turned_ok, 2)
            pe.sem_inc(based_ok, 2)
            pe.wait_ge(loaded, 48)
            with pe.Fori(0, NBD // 2) as i:
                for b in range(2):
                    n = i * 2 + b
                    pe.wait_ge(own, n + 1)
                    pe.wait_ge(copied, n + 1)
                    for j in range(2):
                        last = nc.tensor.transpose(turned[:, b, j, :], inputs[:, b, j, :], k.ident[:])
                    last.then_inc(turned_ok, 1)
                    pe.wait_ge(copied, n + 2)
                    pe.wait_ge(done, n + 1)
                    nc.tensor.matmul(based[:, b, :, :], turned_sb[:, b, 0, :], w[:], start=True, stop=True)
                    nc.tensor.matmul(looped[:, b, 0:D], turned_sb[:, b, 1, :], wl[:], start=True,
                                     stop=True).then_inc(based_ok, 1)

        @block.vector
        def _(dve):
            chain = in_steps(dve, step)
            den = total[:, 0:NBLK, D:D + HEADS1]
            chain(nc.vector.tensor_single_scalar(den, den, TINY, ALU.max))
            chain(nc.vector.reciprocal(den, den))
            for n in range(NBLK):
                part = total[:, n, 0:D].rearrange("p (h f) -> p h f", h=HEADS1)
                by = total[:, n, D:D + HEADS1].rearrange("p (h a) -> p h a", a=1).to_broadcast([P, HEADS1, D // HEADS1])
                nc.vector.tensor_tensor(part, part, by, ALU.mult).then_inc(normed, 1)
            dve.sem_inc(done, 2)
            dve.wait_ge(loaded, 48)
            with dve.Fori(0, NBD // 2) as i:
                for b in range(2):
                    n = i * 2 + b
                    m = mixed[:, b, :]
                    dve.wait_ge(based_ok, n + 3)
                    dve.wait_ge(done, n + 1)
                    nc.vector.tensor_tensor(m, looped[:, b, 0:D], bias_row[:], ALU.add).then_inc(d, 1)
                    for basis in range(BASES):
                        dve.wait_ge(d, n * 5 + basis + 1)
                        by = mix[:, bass.ds(n, 1), 3 * BASES + basis:3 * BASES + basis + 1].rearrange("p a b -> p (a b)")
                        nc.vector.scalar_tensor_tensor(out=m, in0=based[:, b, basis, :], scalar=by, in1=m, op0=ALU.mult,
                                                       op1=ALU.add).then_inc(d, 1)
                    dve.wait_ge(d, n * 5 + 5)
                    here = k.x[:, bass.ds(n, 1), :]
                    nc.vector.scalar_tensor_tensor(out=here, in0=mixed[:, b:b + 1, :], scalar=0.0, in1=here, op0=ALU.max,
                                                   op1=ALU.add).then_inc(done, 1)


def project(nc, k, source, w, bias, outputs, name):
    width = w.shape[1]
    with ExitStack() as ctx:
        sb, ps, sem = tools(nc, k, ctx, name)
        x = sb("x", [P, 2, D])
        xt = sb("xt", [P, 2, P])
        y = sb("y", [P, 2, width]) if bias is not None else None
        turned = ps("turned", [P, 2, 512])
        product = ps("product", [P, 2, 512])
        own = sem("own")
        turned_ok = sem("turned_ok")
        copied = sem("copied")
        made = sem("made")
        d = sem("d")
        used = sem("used")
        block = ctx.enter_context(nc.Block())

        @block.scalar
        def _(act):
            act.sem_inc(copied, 1)
            with act.Fori(0, NBD // 2) as i:
                for b in range(2):
                    n = i * 2 + b
                    act.wait_ge(turned_ok, n + 1)
                    nc.scalar.copy(x[:, b, :], source[:, bass.ds(n, 1), :]).then_inc(own, 1)
                    act.wait_ge(turned_ok, n + 3)
                    act.wait_ge(made, n + 1)
                    nc.scalar.copy(xt[:, b, :], turned[:, b, 0:P]).then_inc(copied, 1)

        @block.tensor
        def _(pe):
            pe.sem_inc(turned_ok, 2)
            pe.sem_inc(made, 2)
            with pe.Fori(0, NBD // 2) as i:
                for b in range(2):
                    n = i * 2 + b
                    pe.wait_ge(own, n + 1)
                    pe.wait_ge(copied, n + 1)
                    nc.tensor.transpose(turned[:, b, 0:P], x[:, b, :], k.ident[:]).then_inc(turned_ok, 1)
                    pe.wait_ge(copied, n + 2)
                    pe.wait_ge(used, n + 1)
                    nc.tensor.matmul(product[:, b, 0:width], xt[:, b, :], w, start=True, stop=True).then_inc(made, 1)

        @block.vector
        def _(dve):
            dve.sem_inc(used, 2)
            with dve.Fori(0, NBD // 2) as i:
                for b in range(2):
                    n = i * 2 + b
                    dve.wait_ge(made, n + 3)
                    dve.wait_ge(used, n + 1)
                    src = product[:, b:b + 1, 0:width]
                    if bias is not None:
                        nc.vector.tensor_tensor(y[:, b, :], product[:, b, 0:width], bias, ALU.add).then_inc(d, 1)
                        dve.wait_ge(d, n + 1)
                        src = y[:, b:b + 1, :]
                    for lo, hi, scale, out, add in outputs:
                        here = out[:, bass.ds(n, 1), :]
                        if add:
                            last = nc.vector.scalar_tensor_tensor(out=here, in0=src[:, :, lo:hi], scalar=scale, in1=here,
                                                                  op0=ALU.mult, op1=ALU.add)
                        else:
                            last = nc.vector.tensor_scalar(here, src[:, :, lo:hi], scale, None, ALU.mult)
                    last.then_inc(used, 1)


def self_scores(nc, k, left, right, att_row, scores, name):
    with ExitStack() as ctx:
        sb, ps, sem = tools(nc, k, ctx, name)
        pair = sb("pair", [P, PIECE, D])
        step = sem("step")
        block = ctx.enter_context(nc.Block())

        @block.vector
        def _(dve):
            chain = in_steps(dve, step)
            for n in range(PIECES):
                here = slice(n * PIECE, (n + 1) * PIECE)
                flat = pair[:].rearrange("p b f -> p (b f)")
                chain(nc.vector.tensor_tensor(pair[:], left[:, here, :], right[:, here, :], ALU.add))
                chain(nc.vector.scalar_tensor_tensor(out=flat, in0=flat, scalar=0.2, in1=flat, op0=ALU.mult, op1=ALU.max))
                chain(nc.vector.tensor_tensor(pair[:], pair[:],
                                              att_row.rearrange("p (a f) -> p a f", a=1).to_broadcast([P, PIECE, D]),
                                              ALU.mult))
                chain(nc.vector.tensor_reduce(scores[:, here, :], pair[:].rearrange("p b (h f) -> p b h f", h=HEADS2),
                                              AX.X, ALU.add))


def attention_output(nc, k, total, left_table, bias, name):
    with ExitStack() as ctx:
        sb, ps, sem = tools(nc, k, ctx, name)
        left = sb("left", [P, NBLK, D])
        bias_row = sb("bias_row", [P, D])
        den = sb("den", [P, NBLK, HEADS2])
        alone = sb("alone", [P, NBLK, HEADS2])
        loaded = sem("loaded")
        step = sem("step")
        block = ctx.enter_context(nc.Block())
        head = D // HEADS2

        @block.sync
        def _(sp):
            sp.dma_start(left[:], left_table[0:NP, :].rearrange("(b p) f -> p b f", p=P)).then_inc(loaded, 16)
            sp.dma_start(bias_row[:], row_on_all(bias)).then_inc(loaded, 16)

        @block.vector
        def _(dve):
            chain = in_steps(dve, step)
            edge_sum = total[:, :, D:D + HEADS2]
            loop = total[:, :, D + HEADS2:D + 2 * HEADS2]
            chain(nc.vector.tensor_single_scalar(alone[:], edge_sum, 0.0, ALU.is_equal))
            chain(nc.vector.tensor_tensor(loop, loop, alone[:], ALU.add))
            chain(nc.vector.tensor_tensor(den[:], edge_sum, loop, ALU.add))
            chain(nc.vector.tensor_single_scalar(den[:], den[:], TINY, ALU.max))
            chain(nc.vector.reciprocal(den[:], den[:]))
            dve.wait_ge(loaded, 32)
            for h in range(HEADS2):
                f = slice(h * head, (h + 1) * head)
                across = lambda t: t.to_broadcast([P, NBLK, head])
                chain(nc.vector.tensor_tensor(left[:, :, f], left[:, :, f], across(loop[:, :, h:h + 1]), ALU.mult))
                chain(nc.vector.tensor_tensor(left[:, :, f], left[:, :, f], total[:, :, f], ALU.add))
                chain(nc.vector.tensor_tensor(left[:, :, f], left[:, :, f], across(den[:, :, h:h + 1]), ALU.mult))
            x = k.x[:, 0:NBLK, :]
            chain(nc.vector.tensor_tensor(x, x, left[:], ALU.add))
            chain(nc.vector.tensor_tensor(x, x, bias_row[:].rearrange("p (a f) -> p a f", a=1)
                                          .to_broadcast([P, NBLK, D]), ALU.add))


def value_rows(nc, k, total, values, table, name):
    with ExitStack() as ctx:
        sb, ps, sem = tools(nc, k, ctx, name)
        rows = sb("rows", [P, NBLK, D + HEADS3])
        rden = sb("rden", [P, NBLK, HEADS3])
        step = sem("step")
        made = sem("made")
        stored = sem("stored")
        block = ctx.enter_context(nc.Block())
        head = D // HEADS3

        @block.vector
        def _(dve):
            chain = in_steps(dve, step)
            chain(nc.vector.tensor_single_scalar(rden[:], total[:, :, 0:HEADS3], TINY, ALU.max))
            chain(nc.vector.reciprocal(rden[:], rden[:]))
            nc.vector.tensor_copy(rows[:, :, D:D + HEADS3], total[:, :, HEADS3:2 * HEADS3])
            for h in range(HEADS3):
                f = slice(h * head, (h + 1) * head)
                nc.vector.tensor_tensor(rows[:, :, f], values[:, 0:NBLK, f],
                                        rden[:, :, h:h + 1].to_broadcast([P, NBLK, head]), ALU.mult).then_inc(made, 1)

        @block.sync
        def _(sp):
            sp.wait_ge(made, HEADS3)
            sp.dma_start(table[0:NP, D:2 * D + HEADS3].rearrange("(b p) f -> p b f", p=P), rows[:]).then_inc(stored, 16)
            sp.wait_ge(stored, 16)


def load_nodes(nc, k, x, hops, name):
    with ExitStack() as ctx:
        sb, ps, sem = tools(nc, k, ctx, name)
        cleared = sem("cleared")
        loaded = sem("loaded")
        full = NBLK - 1
        block = ctx.enter_context(nc.Block())

        @block.vector
        def _(dve):
            nc.vector.memset(k.x[:], 0.0).then_inc(cleared, 1)

        @block.sync
        def _(sp):
            sp.wait_ge(cleared, 1)
            sp.dma_start(k.x[:, 0:full, :], x[0:full * P, :].rearrange("(b p) f -> p b f", p=P)).then_inc(loaded, 16)
            sp.dma_start(k.x[0:TAIL, full, :], x[full * P:N, :]).then_inc(loaded, 16)
            for h in range(3):
                sp.dma_start(hops[h][NP:NPD, :].rearrange("(b p) f -> p b f", p=P),
                             k.x[:, NBLK:NBD, :]).then_inc(loaded, 16)
            sp.wait_ge(loaded, 80)


def typed_rows(nc, k, o, name):
    with ExitStack() as ctx:
        sb, ps, sem = tools(nc, k, ctx, name)
        block = ctx.enter_context(nc.Block())

        @block.vector
        def _(dve):
            nc.vector.scalar_tensor_tensor(out=o.typed[:], in0=o.typed[:], scalar=float(NPD), in1=o.other[:],
                                           op0=ALU.mult, op1=ALU.add)


def graph_network(nc, a, out):
    k = Shared()
    k.semaphores = []
    with ExitStack() as ctx:
        def sb(name, shape, dt=F32):
            return ctx.enter_context(nc.sbuf_tensor(f"k_{name}", shape, dt))

        def dram(name, shape, dt=F32):
            return nc.dram_tensor(name, shape, dt, kind="Internal").ap()

        k.ident = sb("ident", [P, P])
        k.identb = sb("identb", [P, P], BF16)
        k.before = sb("before", [P, P])
        k.count = sb("count", [P, P])
        k.countb = sb("countb", [P, P], BF16)
        k.ones = sb("ones", [P, P])
        k.x = sb("x", [P, NBD, D])
        mix = sb("mix", [P, NBD, 4 * BASES])
        by_src, by_dst = Order(), Order()
        for o, n in ((by_src, "src"), (by_dst, "dst")):
            o.place = sb(f"{n}_place", [P, CH + SPARE])
            o.begins = sb(f"{n}_begins", [P, CH])
            o.block = sb(f"{n}_block", [1, CH + SPARE], I32)
            o.other = sb(f"{n}_other", [P, CH + SPARE], I32)
            o.sorted = dram(f"{n}_sorted", [LEAD + NSLOT, 4])
            o.breaks = dram(f"{n}_breaks", [NSLOT + P], BF16)
        by_src.weight = sb("src_weight", [P, CH + SPARE])
        by_dst.typed = sb("dst_typed", [P, CH + SPARE], I32)
        hops = [dram(f"hops{h}", [NPD, D]) for h in range(3)]
        related = dram("related", [TYPES, NPD, 2 * D])
        kept = dram("kept", [GROUPS, P, G * D])
        left_table = dram("left_table", [NPD, D])
        key_table = dram("key_table", [NPD, D])
        value_table = dram("value_table", [NPD, D])
        row_table = dram("row_table", [NPD, 2 * D + HEADS3])

        make_constants(nc, k)
        load_nodes(nc, k, a["x"], hops, "nodes")
        type_weights(nc, k, a["node_type_8"], [a[f"L1_gnn_w_comp_{p}"] for p in "qkva"], mix, "types")

        prefill(nc, k, [by_src.sorted, by_dst.sorted], "prefill")
        for o, n, key, fields in ((by_src, "src", a["src"], [a["dst"], a["edge_weight"]]),
                                  (by_dst, "dst", a["dst"], [a["src"], a["edge_type_8"]])):
            with ExitStack() as sort:
                def tmp(name, shape, dt=F32):
                    return sort.enter_context(nc.sbuf_tensor(f"{n}_sort_{name}", shape, dt))

                o.block_base = tmp("block_base", [P, CH])
                with ExitStack() as early:
                    def tmp2(name, shape, dt=F32):
                        return early.enter_context(nc.sbuf_tensor(f"{n}_sort_{name}", shape, dt))

                    rec = tmp2("rec", [P, EC, 4])
                    keys = tmp2("keys", [P, 2, EC + G])
                    counts = tmp2("counts", [HIS, P])
                    first_place = tmp2("first_place", [HIS, P])
                    load_edges(nc, k, key, fields, rec, keys, f"{n}_load")
                    histogram(nc, k, keys, counts, f"{n}_count")
                    place_blocks(nc, k, counts, first_place, o, f"{n}_base")
                    scatter_edges(nc, k, rec, keys, first_place, o.sorted, f"{n}_scatter")
                if o is by_src:
                    read_order(nc, k, o.sorted, o, o.breaks, [(1, o.other)], [(2, o.weight)], f"{n}_read")
                else:
                    read_order(nc, k, o.sorted, o, o.breaks, [(1, o.other), (2, o.typed)], [], f"{n}_read")
        typed_rows(nc, k, by_dst, "typed")

        free_semaphores(nc, k)

        for h in range(3):
            hop(nc, k, by_src, a["x"] if h == 0 else hops[h - 1], hops[h][0:NP, :], f"hop{h}")
        polynomial(nc, k, hops, a["L0_gnn_weights"], "poly")
        layernorm(nc, k, k.x, None, "norm0")

        free_semaphores(nc, k)

        with ExitStack() as layer:
            scores = layer.enter_context(nc.sbuf_tensor("l1_scores", [P, CH, HEADS1], F32))
            with ExitStack() as first:
                spread = first.enter_context(nc.sbuf_tensor("l1_spread", [P, NBD, 3, D], BF16))
                with ExitStack() as dense:
                    def tmp(name, shape, dt=F32):
                        return dense.enter_context(nc.sbuf_tensor(f"l1_{name}", shape, dt))

                    att_sb = tmp("att", [P, TYPES, D])
                    msg_sb = tmp("msg", [P, TYPES, D])
                    queries = tmp("queries", [P, NBD, D])
                    relation_weights(nc, k, a["L1_gnn_relation_att"], a["L1_gnn_relation_msg"],
                                     a["L1_gnn_relation_pri"], att_sb, msg_sb, "l1_relations")
                    relation_tables(nc, k, [a[f"L1_gnn_w_basis_{p}"] for p in "qkv"], att_sb, msg_sb, mix, queries,
                                    related, "l1_tables")
                    split_parts(nc, k, queries[:], spread, 0, "l1_split")
                score_pass(nc, k, by_dst, by_dst.typed, related.rearrange("t n f -> (t n) f"), 2 * D, D // HEADS1, D,
                           kept, spread, scores, None, "l1_score")
            segment_maximum(nc, k, by_dst, by_dst.breaks, HEADS1, scores, [scores], None, "l1_max")
            exponentials(nc, k, [scores], None, "l1_exp")
            with ExitStack() as second:
                total = second.enter_context(nc.sbuf_tensor("l1_total", [P, NBD, D + HEADS1], F32))
                sum_pass(nc, k, by_dst, kept, scores, [scores], total, "l1_sum")
                relation_output(nc, k, total, a["L1_gnn_w_basis_a"], a["L1_gnn_loop_weight"], a["L1_gnn_bias"], mix,
                                "l1_out")
        layernorm(nc, k, k.x, None, "norm1")

        free_semaphores(nc, k)

        with ExitStack() as layer:
            scores = layer.enter_context(nc.sbuf_tensor("l2_scores", [P, CH, HEADS2], F32))
            loops = layer.enter_context(nc.sbuf_tensor("l2_loops", [P, CH, HEADS2], F32))
            with ExitStack() as first:
                def tmp(name, shape, dt=F32):
                    return first.enter_context(nc.sbuf_tensor(f"l2_{name}", shape, dt))

                top = tmp("top", [P, CH, HEADS2])
                att_row = tmp("att_row", [P, D])
                with ExitStack() as edges:
                    spread = edges.enter_context(nc.sbuf_tensor("l2_spread", [P, NBD, 3, D + HEADS2], BF16))
                    att_rows = edges.enter_context(nc.sbuf_tensor("l2_att_rows", [P, G * D], F32))
                    load_all(nc, k, [(att_row[:], row_on_all(a["L2_gnn_att"].rearrange("h f -> (h f)")))]
                             + [(att_rows[:, g * D:(g + 1) * D], row_on_all(a["L2_gnn_att"].rearrange("h f -> (h f)")))
                                for g in range(G)], "l2_att_in")
                    with ExitStack() as dense:
                        w = dense.enter_context(nc.sbuf_tensor("l2_w", [P, 2 * D], F32))
                        right = dense.enter_context(nc.sbuf_tensor("l2_right", [P, NBD, D], F32))
                        left = dense.enter_context(nc.sbuf_tensor("l2_left", [P, NBD, D], F32))
                        loop_scores = dense.enter_context(nc.sbuf_tensor("l2_loop_scores", [P, NBD, HEADS2], F32))
                        turn_weights(nc, k, [(w[:, 0:D], a["L2_gnn_W_l"]), (w[:, D:2 * D], a["L2_gnn_W_r"])], "l2_turn")
                        project(nc, k, k.x, w[:], None, [(0, D, 1.0, left, False), (D, 2 * D, 1.0, right, False)],
                                "l2_project")
                        load_all(nc, k, [(left_table.rearrange("(b p) f -> p b f", p=P), left[:])], "l2_store")
                        self_scores(nc, k, left, right, att_row[:], loop_scores, "l2_self")
                        split_parts(nc, k, right[:], spread, 0, "l2_split")
                        split_parts(nc, k, loop_scores[:], spread, D, "l2_split_self")
                    score_pass(nc, k, by_dst, by_dst.other, left_table, D, D // HEADS2, 0, kept, spread, scores,
                               (att_rows, loops, top), "l2_score")
                segment_maximum(nc, k, by_dst, by_dst.breaks, HEADS2, top, [scores, loops], None, "l2_max")
            exponentials(nc, k, [scores, loops], by_dst.begins, "l2_exp")
            with ExitStack() as second:
                total = second.enter_context(nc.sbuf_tensor("l2_total", [P, NBLK, D + 2 * HEADS2], F32))
                sum_pass(nc, k, by_dst, kept, scores, [scores, loops], total, "l2_sum")
                attention_output(nc, k, total, left_table, a["L2_gnn_bias"], "l2_out")
        layernorm(nc, k, k.x, None, "norm2")

        free_semaphores(nc, k)

        with ExitStack() as layer:
            with ExitStack() as softmax:
                scores = softmax.enter_context(nc.sbuf_tensor("l3_scores", [P, CH, HEADS3], F32))
                with ExitStack() as first:
                    spread = first.enter_context(nc.sbuf_tensor("l3_spread_q", [P, NBD, 3, D], BF16))
                    with ExitStack() as dense:
                        def tmp(name, shape, dt=F32):
                            return dense.enter_context(nc.sbuf_tensor(f"l3_{name}", shape, dt))

                        w = tmp("w", [P, 3 * D])
                        bias = tmp("bias", [P, 3 * D])
                        turn_weights(nc, k, [(w[:, j * D:(j + 1) * D], a[f"L3_gnn_W{p}"]) for j, p in enumerate("qkv")],
                                     "l3_turn")
                        load_all(nc, k, [(bias[:, j * D:(j + 1) * D], row_on_all(a[f"L3_gnn_b{p}"]))
                                      for j, p in enumerate("qkv")], "l3_bias")
                        one, two = tmp("one", [P, NBD, D]), tmp("two", [P, NBD, D])
                        project(nc, k, k.x, w[:, D:3 * D], bias[:, D:3 * D],
                                [(0, D, 1.0, one, False), (D, 2 * D, 1.0, two, False)], "l3_keys_values")
                        load_all(nc, k, [(key_table.rearrange("(b p) f -> p b f", p=P), one[:]),
                                      (value_table.rearrange("(b p) f -> p b f", p=P), two[:])], "l3_store_kv")
                        project(nc, k, k.x, w[:, 0:D], bias[:, 0:D],
                                [(0, D, float(D // HEADS3) ** -0.5, one, False)], "l3_queries")
                        load_all(nc, k, [(row_table[:, 0:D].rearrange("(b p) f -> p b f", p=P), one[:])], "l3_store_q")
                        split_parts(nc, k, one[:], spread, 0, "l3_split_q")
                    score_pass(nc, k, by_src, by_src.other, key_table, D, D // HEADS3, 0, None, spread, scores, None,
                               "l3_score")
                maxima = softmax.enter_context(nc.sbuf_tensor("l3_maxima", [P, CH, HEADS3], F32))
                segment_maximum(nc, k, by_src, by_src.breaks, HEADS3, scores, [scores], maxima, "l3_max")
                exponentials(nc, k, [scores], None, "l3_exp")
                total = softmax.enter_context(nc.sbuf_tensor("l3_softmax_sums", [P, NBLK, 2 * HEADS3], F32))
                sum_pass(nc, k, by_src, None, None, [scores, maxima], total, "l3_sum")
                with ExitStack() as rows:
                    values = rows.enter_context(nc.sbuf_tensor("l3_values", [P, NBD, D], F32))
                    load_all(nc, k, [(values[:], value_table.rearrange("(b p) f -> p b f", p=P))], "l3_load_v")
                    value_rows(nc, k, total, values, row_table, "l3_rows")
            total = layer.enter_context(nc.sbuf_tensor("l3_total", [P, NBD, D], F32))
            with ExitStack() as second:
                spread = second.enter_context(nc.sbuf_tensor("l3_spread_k", [P, NBD, 3, D], BF16))
                with ExitStack() as dense:
                    keys = dense.enter_context(nc.sbuf_tensor("l3_keys", [P, NBD, D], F32))
                    load_all(nc, k, [(keys[:], key_table.rearrange("(b p) f -> p b f", p=P))], "l3_load_k")
                    split_parts(nc, k, keys[:], spread, 0, "l3_split_k")
                weigh_and_sum(nc, k, by_dst, by_dst.other, row_table[0:NP, :], spread, total, "l3_weigh")
            wo = layer.enter_context(nc.sbuf_tensor("l3_wo", [P, D], F32))
            bo = layer.enter_context(nc.sbuf_tensor("l3_bo", [P, D], F32))
            turn_weights(nc, k, [(wo[:], a["L3_gnn_Wo"])], "l3_turn_o")
            load_all(nc, k, [(bo[:], row_on_all(a["L3_gnn_bo"]))], "l3_bias_o")
            project(nc, k, total, wo[:], bo[:], [(0, D, 1.0, k.x, True)], "l3_out")
        layernorm(nc, k, k.x, out, "norm3")


def kernel(**inputs):
    import numpy as _np
    import concourse.bacc as _bacc
    from concourse import mybir as _mybir
    from concourse.bass_utils import run_bass_kernel_spmd as _run

    nc = _bacc.Bacc("TRN2", target_bir_lowering=False, num_devices=1)
    arrays, handles = {}, {}
    for name, value in inputs.items():
        array = _np.ascontiguousarray(value)
        arrays[f"in_{name}"] = array
        handles[name] = nc.dram_tensor(f"in_{name}", array.shape, _mybir.dt.from_np(array.dtype),
                                       kind="ExternalInput").ap()
    out = nc.dram_tensor("out_x", (N, D), F32, kind="ExternalOutput").ap()
    graph_network(nc, handles, out)
    r = _run(nc, [arrays], core_ids=[0])
    return r.results[0]["out_x"]
```

```python
from contextlib import ExitStack

import concourse.bass as bass
from concourse import mybir

ALU = mybir.AluOpType
ACT = mybir.ActivationFunctionType
AX = mybir.AxisListType
F32 = mybir.dt.float32
BF16 = mybir.dt.bfloat16
I32 = mybir.dt.int32

P = 128
N = 6250
E = 100000
D = 128
NBLK = -(-N // P)
NP = NBLK * P
TAIL = N - (NBLK - 1) * P
TYPES = 8
BASES = 4
G = 4
SLOTS = 4
EC = -(-E // (P * G * SLOTS)) * G * SLOTS
PADS = EC * P - E
EMAIN = E // P
HIS = NBLK + 1
CH = -(-((E + NBLK * (P - 1)) // P + -(-PADS // P)) // (G * SLOTS)) * G * SLOTS
NSLOT = CH * P
LEAD = 1
GROUPS = CH // G
ROUNDS = GROUPS // SLOTS
TQ = 104
QT = CH // TQ
SPARE = SLOTS * G
BIG = 1.0e30
EPS = 1e-5
TINY = 1e-16
assert QT * TQ == CH and EC % (G * SLOTS) == 0


class Shared:
    pass


class Order:
    pass


def free_semaphores(nc, k):
    nc.clear_and_free_semaphores(k.semaphores)
    nc.all_engine_barrier()
    k.semaphores = []


def tools(nc, k, ctx, phase):
    def sb(name, shape, dt=F32):
        return ctx.enter_context(nc.sbuf_tensor(f"{phase}_{name}", shape, dt))

    def ps(name, shape, dt=F32):
        return ctx.enter_context(nc.psum_tensor(f"{phase}_{name}", shape, dt))

    def sem(name):
        semaphore = nc.alloc_semaphore(f"{phase}_{name}")
        k.semaphores.append(semaphore)
        return semaphore

    return sb, ps, sem


def load_blocks(nc, engine, chunk, count):
    _, regs = nc.values_load_multi_w_load_instructions(
        chunk, engines=[engine], min_val=0, max_val=NBLK - 1,
        skip_runtime_bounds_check_because="the table is clamped to the last block")
    return regs


def mark(nc, onehots, count, number):
    chunks, width = onehots.shape[1], onehots.shape[2]
    return nc.vector.tensor_tensor(
        onehots, count[:, 0:width].rearrange("p (a j) -> p a j", a=1).to_broadcast([P, chunks, width]),
        number.rearrange("p (g a) -> p g a", a=1).to_broadcast([P, chunks, width]), ALU.is_equal)


def in_rounds(engine, count, body):
    body(0, True)
    with engine.Fori(1, count) as i:
        body(i, False)


def make_constants(nc, k):
    with ExitStack() as ctx:
        sb, ps, sem = tools(nc, k, ctx, "const")
        pool_step = sem("pool_step")
        made = sem("made")
        block = ctx.enter_context(nc.Block())

        @block.gpsimd
        def _(pool):
            nc.gpsimd.memset(k.ident[:], 0.0)
            nc.gpsimd.memset(k.before[:], 1.0).then_inc(pool_step, 1)
            nc.gpsimd.iota(k.count[:], [[1, P]], base=0, channel_multiplier=0,
                           allow_small_or_imprecise_dtypes=True)
            nc.gpsimd.memset(k.ones[:], 1.0)
            pool.wait_ge(pool_step, 1)
            nc.gpsimd.affine_select(out=k.ident[:], in_=k.ident[:], compare_op=ALU.not_equal, fill=1.0,
                                    base=0, pattern=[[-1, P]], channel_multiplier=1)
            nc.gpsimd.affine_select(out=k.before[:], in_=k.before[:], compare_op=ALU.is_gt, fill=0.0,
                                    base=0, pattern=[[-1, P]], channel_multiplier=1).then_inc(made, 1)

        @block.vector
        def _(dve):
            dve.wait_ge(made, 1)
            nc.vector.tensor_copy(k.identb[:], k.ident[:])
            nc.vector.tensor_copy(k.countb[:], k.count[:])


def load_edges(nc, k, key, fields, rec, keys, prepare):
    with ExitStack() as ctx:
        sb, ps, sem = tools(nc, k, ctx, prepare)
        raw = sb("raw", [P, len(fields) + 1, EC], I32)
        hi = sb("hi", [P, EC], I32)
        lo = sb("lo", [P, EC], I32)
        padded = sem("padded")
        loaded = sem("loaded")
        step = sem("step")
        rest = E - EMAIN * P
        block = ctx.enter_context(nc.Block())

        @block.sync
        def _(sp):
            sp.wait_ge(padded, 1)
            for n, field in enumerate([key, *fields]):
                tile = raw[:, n, :] if field.dtype == I32 else raw[:, n, :].bitcast(F32)
                sp.dma_start(tile[:, 0:EMAIN],
                             field[0:EMAIN * P].rearrange("(p c) -> p c", p=P)).then_inc(loaded, 16)
                sp.dma_start(tile[0:rest, EMAIN:EMAIN + 1],
                             field[EMAIN * P:E].rearrange("(p c) -> p c", c=1)).then_inc(loaded, 16)

        @block.vector
        def _(dve):
            nc.vector.memset(raw[:, 1:, EMAIN:], 0)
            nc.vector.memset(raw[:, 0, EMAIN:], NP).then_inc(padded, 1)
            dve.wait_ge(loaded, 32 * (len(fields) + 1))
            for n, field in enumerate([key, *fields]):
                tile = raw[:, n, :] if field.dtype == I32 else raw[:, n, :].bitcast(F32)
                nc.vector.tensor_copy(rec[:, :, n], tile)
            for n in range(len(fields) + 1, 4):
                nc.vector.memset(rec[:, :, n], 0.0)
            nc.vector.tensor_single_scalar(hi[:], raw[:, 0, :], 7, ALU.arith_shift_right).then_inc(step, 1)
            nc.vector.tensor_single_scalar(lo[:], raw[:, 0, :], P - 1, ALU.bitwise_and).then_inc(step, 1)
            dve.wait_ge(step, 2)
            nc.vector.tensor_copy(keys[:, 0, 0:EC], hi[:])
            nc.vector.tensor_copy(keys[:, 1, 0:EC], lo[:])
            nc.vector.memset(keys[:, :, EC:], 0.0)


def prefill(nc, k, tables, name):
    with ExitStack() as ctx:
        sb, ps, sem = tools(nc, k, ctx, name)
        pad = sb("pad", [P, CH, 4])
        filled = sem("filled")
        stored = sem("stored")
        block = ctx.enter_context(nc.Block())

        @block.vector
        def _(dve):
            nc.vector.memset(pad[:, :, 0:1], -1.0)
            nc.vector.memset(pad[:, :, 1:4], 0.0).then_inc(filled, 1)

        @block.sync
        def _(sp):
            sp.wait_ge(filled, 1)
            for table in tables:
                sp.dma_start(table[LEAD:LEAD + NSLOT, :].rearrange("(p c) f -> p (c f)", p=P),
                             pad[:].rearrange("p c f -> p (c f)")).then_inc(stored, 16)
                sp.dma_start(table[0:LEAD, :], pad[0:1, 0, :]).then_inc(stored, 16)
            sp.wait_ge(stored, 32 * len(tables))


def histogram(nc, k, keys, counts, name):
    with ExitStack() as ctx:
        sb, ps, sem = tools(nc, k, ctx, name)
        batch = 2 * G
        steps = EC // batch // 2
        oh_hi = sb("oh_hi", [P, 2, batch, HIS], BF16)
        oh_lo = sb("oh_lo", [P, 2, batch, P], BF16)
        zero = sb("zero", [P, P], BF16)
        total = ps("total", [HIS, P])
        onehots = sem("onehots")
        summed = sem("summed")
        zeroed = sem("zeroed")
        block = ctx.enter_context(nc.Block())

        @block.vector
        def _(dve):
            nc.vector.memset(zero[:], 0.0).then_inc(zeroed, 1)
            with dve.Fori(0, steps) as i:
                for b in range(2):
                    dve.wait_ge(summed, i * 2 + b + 1)
                    here = bass.ds(i * 2 * batch + b * batch, batch)
                    mark(nc, oh_hi[:, b, :, :], k.count, keys[:, 0, here])
                    mark(nc, oh_lo[:, b, :, :], k.count, keys[:, 1, here]).then_inc(onehots, 1)
            dve.wait_ge(summed, 2 * steps + 2)
            nc.vector.tensor_copy(counts[:], total[:])

        @block.tensor
        def _(pe):
            pe.sem_inc(summed, 2)
            pe.wait_ge(zeroed, 1)
            nc.tensor.matmul(total[:], zero[:, 0:HIS], zero[:], start=True, stop=False, skip_group_check=True)
            with pe.Fori(0, steps) as i:
                for b in range(2):
                    pe.wait_ge(onehots, i * 2 + b + 1)
                    for g in range(batch):
                        last = nc.tensor.matmul(total[:], oh_hi[:, b, g, :], oh_lo[:, b, g, :], start=False,
                                                stop=False, skip_group_check=True)
                    last.then_inc(summed, 1)


def place_blocks(nc, k, counts, first_place, o, name):
    with ExitStack() as ctx:
        sb, ps, sem = tools(nc, k, ctx, name)
        edges = sb("edges", [HIS, 1])
        edges_i = sb("edges_i", [HIS, 1], I32)
        chunks_i = sb("chunks_i", [HIS, 1], I32)
        chunks = sb("chunks", [HIS, 1])
        start = sb("start", [HIS, 1])
        upto = sb("upto", [HIS, P])
        zeros = sb("zeros", [HIS, P])
        above = sb("above", [P, P])
        chunk_no = sb("chunk_no", [HIS, CH])
        begun = sb("begun", [HIS, CH])
        block_f = sb("block_f", [P, CH])
        starts = ps("starts", [HIS, 1])
        turned = ps("turned", [P, P])
        begun_n = ps("begun_n", [P, 2, 512])
        half = CH // 2
        numbered = sem("numbered")
        d = sem("d")
        pe_step = sem("pe_step")
        block = ctx.enter_context(nc.Block())

        @block.gpsimd
        def _(pool):
            nc.gpsimd.iota(chunk_no[:], [[1, CH]], base=0, channel_multiplier=0,
                           allow_small_or_imprecise_dtypes=True).then_inc(numbered, 1)

        @block.tensor
        def _(pe):
            nc.tensor.transpose(turned[:], k.before[:], k.ident[:]).then_inc(pe_step, 1)
            pe.wait_ge(d, 6)
            nc.tensor.matmul(starts[:], above[0:HIS, 0:HIS], chunks[:], start=True, stop=True).then_inc(pe_step, 1)
            pe.wait_ge(d, 8)
            for h in range(2):
                last = nc.tensor.matmul(begun_n[:, h, 0:half], k.ones[0:HIS, :], begun[:, h * half:(h + 1) * half],
                                        start=True, stop=True)
            last.then_inc(pe_step, 1)

        @block.vector
        def _(dve):
            nc.vector.memset(zeros[:], 0.0)
            nc.vector.tensor_reduce(edges[:], counts[:], AX.X, ALU.add).then_inc(d, 1)
            dve.wait_ge(d, 1)
            nc.vector.tensor_scalar(edges_i[:], edges[:], float(P - 1), None, ALU.add).then_inc(d, 1)
            dve.wait_ge(d, 2)
            nc.vector.tensor_single_scalar(chunks_i[:], edges_i[:], 7, ALU.arith_shift_right).then_inc(d, 1)
            dve.wait_ge(d, 3)
            nc.vector.tensor_copy(chunks[:], chunks_i[:]).then_inc(d, 1)
            dve.wait_ge(pe_step, 1)
            nc.vector.tensor_copy(above[:], turned[:]).then_inc(d, 1)
            nc.vector.tensor_tensor_scan(upto[:], zeros[:], counts[:], 0.0, ALU.add, ALU.add).then_inc(d, 1)
            dve.wait_ge(pe_step, 2)
            nc.vector.tensor_copy(start[:], starts[:]).then_inc(d, 1)
            dve.wait_ge(numbered, 1)
            dve.wait_ge(d, 7)
            nc.vector.tensor_scalar(begun[:], chunk_no[:], start[:], None, ALU.is_ge).then_inc(d, 1)
            nc.vector.tensor_tensor(upto[:], upto[:], counts[:], ALU.subtract).then_inc(d, 1)
            nc.vector.tensor_scalar(start[:], start[:], float(P), float(LEAD), ALU.mult, ALU.add).then_inc(d, 1)
            dve.wait_ge(d, 10)
            nc.vector.tensor_scalar(first_place[:], upto[:], start[:], None, ALU.add)
            dve.wait_ge(pe_step, 3)
            nc.vector.tensor_scalar(block_f[:].rearrange("p (h c) -> p h c", h=2), begun_n[:, :, 0:half], -1.0,
                                    float(NBLK - 1), ALU.add, ALU.min).then_inc(d, 1)
            dve.wait_ge(d, 11)
            nc.vector.tensor_scalar(o.block_base[:], block_f[:], float(P), None, ALU.mult)
            nc.vector.memset(o.block[:, CH:], 0)
            nc.vector.tensor_copy(o.block[:, 0:CH], block_f[0:1, :])


def scatter_edges(nc, k, rec, keys, first_place, table, name):
    with ExitStack() as ctx:
        sb, ps, sem = tools(nc, k, ctx, name)
        oh_hi = sb("oh_hi", [P, SLOTS, G, HIS], BF16)
        oh_lo = sb("oh_lo", [P, SLOTS, G, P], BF16)
        oh_hi_t = sb("oh_hi_t", [HIS, 2, G, P])
        next_sb = sb("next_sb", [HIS, 2, P])
        picked = sb("picked", [P, G, P])
        same = sb("same", [P, G, P])
        base = sb("base", [P, 2, G])
        earlier = sb("earlier", [P, 2, G])
        places = sb("places", [P, SLOTS, G], I32)
        records = sb("records", [P, SLOTS, G, 4])
        next_ps = ps("next_ps", [HIS, 512])
        turned = ps("turned", [HIS, 2, 2 * G, P], BF16)
        nexts = ps("nexts", [P, 2, G, P])
        keyrow = ps("keyrow", [P, 2, G, P])
        taken = sem("taken")
        onehots = sem("onehots")
        turned_ok = sem("turned_ok")
        hi_t = sem("hi_t")
        rows = sem("rows")
        next_ready = sem("next_ready")
        next_copied = sem("next_copied")
        looked = sem("looked")
        ranked = sem("ranked")
        placed = sem("placed")
        sent = [sem(f"sent{s}") for s in range(SLOTS)]
        running = sem("running")
        groups = EC // G
        block = ctx.enter_context(nc.Block())

        @block.scalar
        def _(act):
            def turn_onehots(n, b):
                act.wait_ge(turned_ok, n + 1)
                act.wait_ge(looked, n * G + G)
                nc.scalar.copy(oh_hi_t[:, b, :, :], turned[:, b, 0:G, :]).then_inc(hi_t, 1)

            def a_round(i, first):
                for s in range(SLOTS):
                    n = i * SLOTS + s
                    if not first:
                        act.wait_ge(sent[s], i * 64)
                    nc.scalar.copy(records[:, s, :, :], rec[:, bass.ds(i * SLOTS * G + s * G, G), :]).then_inc(taken, 1)
                    for g in range(G):
                        if g == G - 1:
                            turn_onehots(n + 1, (s + 1) % 2)
                        act.wait_ge(next_ready, n * G + g + 1)
                        act.wait_ge(looked, n * G + g + 2 * G - 1)
                        nc.scalar.copy(next_sb[:, g % 2, :], next_ps[:, 0:P]).then_inc(next_copied, 1)

            turn_onehots(0, 0)
            in_rounds(act, groups // SLOTS, a_round)

        @block.tensor
        def _(pe):
            def turn_onehots(s):
                for g in range(G):
                    last = nc.tensor.transpose(turned[:, s % 2, g, :], oh_hi[:, s, g, :], k.identb[:])
                last.then_inc(turned_ok, 1)

            pe.sem_inc(looked, 2 * G)
            nc.tensor.matmul(next_ps[:, 0:P], k.ident[0:HIS, 0:HIS], first_place[:], start=True, stop=False,
                             skip_group_check=True).then_inc(next_ready, 1)
            pe.wait_ge(onehots, 1)
            turn_onehots(0)
            with pe.Fori(0, groups // SLOTS) as i:
                for s in range(SLOTS):
                    b = s % 2
                    n = i * SLOTS + s
                    pe.wait_ge(hi_t, n + 1)
                    pe.wait_ge(ranked, n + 1)
                    for g in range(G):
                        pe.wait_ge(next_copied, n * G + g + 1)
                        nc.tensor.matmul(next_ps[:, 0:P], oh_hi[:, s, g, :], oh_lo[:, s, g, :], start=False,
                                         stop=False, skip_group_check=True).then_inc(next_ready, 1)
                        nc.tensor.matmul(nexts[:, b, g, :], oh_hi_t[:, b, g, :], next_sb[:, g % 2, :], start=True,
                                         stop=True).then_inc(looked, 1)
                        if g == 0:
                            pe.wait_ge(taken, n + 1)
                            pe.wait_ge(onehots, n + 2)
                            for h in range(G):
                                last = nc.tensor.transpose(keyrow[:, b, h, :],
                                                           records[:, s, h, 0:1].to_broadcast([P, P]), k.ident[:])
                            last.then_inc(rows, 1)
                            turn_onehots((s + 1) % SLOTS)

        @block.vector
        def _(dve):
            def hot(n, s):
                here = bass.ds(n * G, G)
                mark(nc, oh_hi[:, s, :, :], k.count, keys[:, 0, here])
                mark(nc, oh_lo[:, s, :, :], k.count, keys[:, 1, here]).then_inc(onehots, 1)

            dve.sem_inc(ranked, 2)
            hot(0, 0)
            hot(1, 1)

            def a_round(i, first):
                for s in range(SLOTS):
                    b = s % 2
                    n = i * SLOTS + s
                    dve.wait_ge(ranked, n + 1)
                    dve.wait_ge(looked, n * G + G)
                    hot(n + 2, (s + 2) % SLOTS)
                    dve.wait_ge(rows, n + 1)
                    dve.wait_ge(ranked, n + 2)
                    for g in range(G):
                        nc.vector.scalar_tensor_tensor(out=same[:, g, :], in0=keyrow[:, b, g, :],
                                                       scalar=records[:, s, g, 0:1], in1=k.before[:],
                                                       op0=ALU.is_equal, op1=ALU.mult,
                                                       accum_out=earlier[:, b, g:g + 1])
                    dve.wait_ge(looked, n * G + 3 * G)
                    for g in range(G):
                        last = nc.vector.scalar_tensor_tensor(out=picked[:, g, :], in0=nexts[:, b, g, :], scalar=1.0,
                                                              in1=oh_lo[:, s, g, :], op0=ALU.mult, op1=ALU.mult,
                                                              accum_out=base[:, b, g:g + 1])
                    last.then_inc(ranked, 1)
                    dve.wait_ge(ranked, n + 3)
                    if not first:
                        dve.wait_ge(sent[s], i * 64)
                    nc.vector.tensor_tensor(places[:, s, :], base[:, b, :], earlier[:, b, :], ALU.add).then_inc(placed, 1)

            in_rounds(dve, groups // SLOTS, a_round)

        @block.gpsimd
        def _(pool):
            with pool.Fori(0, groups // SLOTS) as i:
                for s in range(SLOTS):
                    pool.wait_ge(placed, i * SLOTS + s + 1)
                    pool.sem_inc(running, 1)
                    for g in range(G):
                        nc.gpsimd.indirect_dma_start(table, bass.IndirectOffsetOnAxis(ap=places[:, s, g:g + 1], axis=0),
                                                     records[:, s, g, :], None).then_inc(sent[s], 16)
            for s in range(SLOTS):
                pool.wait_ge(sent[s], 64 * (groups // SLOTS))


def read_order(nc, k, table, o, breaks, ints, floats, name):
    with ExitStack() as ctx:
        sb, ps, sem = tools(nc, k, ctx, name)
        lst = sb("lst", [TQ, QT, P * 4])
        prev = sb("prev", [TQ, QT, P * 4])
        starts = sb("starts", [TQ, QT, P])
        breaks_sb = sb("breaks_sb", [TQ, QT, P], BF16)
        end = sb("end", [1, P], BF16)
        fields = [(0, o.place)] + ints + floats
        turned = ps("turned", [P, 8, 512])
        loaded = sem("loaded")
        found = sem("found")
        flagged = sem("flagged")
        turned_ok = sem("turned_ok")
        done = sem("done")
        stored = sem("stored")
        block = ctx.enter_context(nc.Block())

        def chunk_major(row):
            return table[row:row + NSLOT, :].rearrange("(q p e) f -> p q (e f)", q=QT, e=P)

        @block.sync
        def _(sp):
            sp.dma_start(lst[:], chunk_major(LEAD)).then_inc(loaded, 16)
            sp.dma_start(prev[:], chunk_major(LEAD - 1)).then_inc(loaded, 16)
            sp.wait_ge(flagged, 2)
            sp.dma_start(breaks[0:NSLOT].rearrange("(q p e) -> p q e", q=QT, e=P), breaks_sb[:]).then_inc(stored, 16)
            sp.dma_start(breaks[NSLOT:NSLOT + P].rearrange("(a b) -> a b", a=1), end[:]).then_inc(stored, 16)
            sp.wait_ge(stored, 32)

        @block.tensor
        def _(pe):
            pe.wait_ge(loaded, 32)
            for n, (f, _) in enumerate(fields):
                if n >= 2:
                    pe.wait_ge(done, n - 1)
                for q in range(QT):
                    last = nc.tensor.transpose(turned[:, 4 * (n % 2) + q // 4, (q % 4) * TQ:(q % 4 + 1) * TQ],
                                               lst[:, q, :].rearrange("p (e f) -> p f e", f=4)[:, f, :],
                                               k.ident[0:TQ, 0:TQ])
                last.then_inc(turned_ok, 1)
            pe.wait_ge(found, 1)
            n = len(fields)
            pe.wait_ge(done, n - 1)
            for q in range(QT):
                last = nc.tensor.transpose(turned[:, 4 * (n % 2) + q // 4, (q % 4) * TQ:(q % 4 + 1) * TQ],
                                           starts[:, q, :], k.ident[0:TQ, 0:TQ])
            last.then_inc(turned_ok, 1)

        @block.vector
        def _(dve):
            dve.wait_ge(loaded, 32)
            nc.vector.memset(end[:], -BIG)
            nc.vector.tensor_tensor(starts[:], lst[:].rearrange("p q (e f) -> p q e f", f=4)[:, :, :, 0],
                                    prev[:].rearrange("p q (e f) -> p q e f", f=4)[:, :, :, 0],
                                    ALU.not_equal).then_inc(found, 1)
            dve.wait_ge(found, 1)
            nc.vector.tensor_scalar(breaks_sb[:], starts[:], -BIG, None, ALU.mult).then_inc(flagged, 2)
            for n, (f, out) in enumerate(fields + [(None, o.begins)]):
                dve.wait_ge(turned_ok, n + 1)
                src = turned[:, 4 * (n % 2):4 * (n % 2) + QT // 4, 0:4 * TQ]
                dst = out[:, 0:CH].rearrange("p (a c) -> p a c", a=QT // 4)
                if n == 0:
                    base = o.block_base[:].rearrange("p (a c) -> p a c", a=QT // 4)
                    nc.vector.tensor_tensor(dst, src, base, ALU.subtract).then_inc(done, 1)
                else:
                    nc.vector.tensor_copy(dst, src).then_inc(done, 1)
            nc.vector.memset(o.place[:, CH:], -1.0)
            for _, out in ints + floats:
                nc.vector.memset(out[:, CH:], 0)


def hop(nc, k, o, table_in, table_out, name):
    with ExitStack() as ctx:
        sb, ps, sem = tools(nc, k, ctx, name)
        total = sb("total", [P, NBLK, D])
        rows = sb("rows", [P, SLOTS, G, D])
        ring = sb("ring", [P, SLOTS, G], I32)
        weighted = sb("weighted", [P, 2, G, P])
        sums = ps("sums", [P, 2, G, D])
        listed = sem("listed")
        got = [sem(f"got{s}") for s in range(SLOTS)]
        hot = sem("hot")
        summed = sem("summed")
        added = sem("added")
        cleared = sem("cleared")
        stored = sem("stored")
        running = sem("running")
        block = ctx.enter_context(nc.Block())

        @block.scalar
        def _(act):
            with act.Fori(0, ROUNDS) as i:
                for s in range(SLOTS):
                    act.wait_ge(summed, i * SLOTS + s + 1)
                    nc.scalar.copy(ring[:, s, :], o.other[:, bass.ds((i * SLOTS + s) * G, G)]).then_inc(listed, 1)

        @block.gpsimd
        def _(pool):
            with pool.Fori(0, ROUNDS) as i:
                for s in range(SLOTS):
                    pool.wait_ge(listed, i * SLOTS + s + 1)
                    pool.sem_inc(running, 1)
                    for g in range(G):
                        nc.gpsimd.indirect_dma_start(rows[:, s, g, :], None, table_in,
                                                     bass.IndirectOffsetOnAxis(ap=ring[:, s, g:g + 1], axis=0),
                                                     ).then_inc(got[s], 16)

        @block.tensor
        def _(pe):
            pe.sem_inc(summed, SLOTS)
            with pe.Fori(0, ROUNDS) as i:
                for s in range(SLOTS):
                    b = s % 2
                    pe.wait_ge(got[s], i * 16 * G + 16 * G)
                    pe.wait_ge(hot, i * SLOTS + s + 1)
                    pe.wait_ge(added, (i * SLOTS + s + 1) * G)
                    for g in range(G):
                        last = nc.tensor.matmul(sums[:, b, g, :], weighted[:, b, g, :], rows[:, s, g, :],
                                                start=True, stop=True)
                    last.then_inc(summed, 1)

        @block.vector
        def _(dve):
            def weigh(c, b, g):
                return nc.vector.tensor_scalar(weighted[:, b, g, :], k.count[:], o.place[:, bass.ds(c, 1)],
                                               o.weight[:, bass.ds(c, 1)], ALU.is_equal, ALU.mult)

            dve.sem_inc(added, 2 * G - 1)
            nc.vector.memset(total[:], 0.0).then_inc(added, 1)
            for g in range(G):
                last = weigh(g, 0, g)
            last.then_inc(hot, 1)
            with dve.Fori(0, ROUNDS) as i:
                for s in range(SLOTS):
                    b = s % 2
                    n = i * SLOTS + s
                    blocks = load_blocks(nc, dve.engine, o.block[:, bass.ds(n * G, G)], G)
                    dve.wait_ge(summed, n + SLOTS)
                    for g in range(G):
                        last = weigh(n * G + G + g, 1 - b, g)
                    last.then_inc(hot, 1)
                    dve.wait_ge(summed, n + 1 + SLOTS)
                    for g in range(G):
                        dve.wait_ge(added, n * G + g + 2 * G)
                        here = total[:, bass.ds(blocks[g], 1), :]
                        nc.vector.tensor_tensor(here, here, sums[:, b, g:g + 1, :], ALU.add).then_inc(added, 1)

        @block.sync
        def _(sp):
            sp.wait_ge(added, GROUPS * G + 2 * G)
            sp.dma_start(table_out.rearrange("(b p) f -> p b f", p=P), total[:]).then_inc(stored, 16)
            sp.wait_ge(stored, 16)


def segment_maximum(nc, k, o, breaks, heads, scores, minus, keep, name):
    strips = P // heads
    width = CH // strips
    length = width * P
    with ExitStack() as ctx:
        sb, ps, sem = tools(nc, k, ctx, name)
        line = sb("line", [P, length])
        line2 = sb("line2", [P, length])
        brk = sb("brk", [P, length + 1], BF16)
        piece = sb("piece", [P, 2, P])
        column = sb("column", [P, 4])
        row = sb("row", [1, 2, P])
        states = sb("states", [1, P])
        carry = sb("carry", [1, P])
        carried = sb("carried", [P, 1])
        turned = ps("turned", [P, 2, 512])
        small = ps("small", [P, 2, 512])
        back = ps("back", [P, 2, 512])
        loaded = sem("loaded")
        copied = sem("copied")
        turned_ok = sem("turned_ok")
        lined = sem("lined")
        d = sem("d")
        pe_step = sem("pe_step")
        piece2 = sem("piece2")
        back_ok = sem("back_ok")
        used = sem("used")
        view = [t[:].rearrange("p (s c) h -> p s c h", s=strips) for t in [scores, *minus]]
        keep_view = keep[:].rearrange("p (s c) h -> p s c h", s=strips) if keep is not None else None
        begins_view = o.begins[:].rearrange("p (s c) -> p s c", s=strips)
        block = ctx.enter_context(nc.Block())

        @block.sync
        def _(sp):
            for s in range(strips):
                sp.dma_start(brk[s * heads:(s + 1) * heads, :],
                             breaks[s * length:(s + 1) * length + 1].rearrange("(a l) -> a l", a=1)
                             .to_broadcast([heads, length + 1])).then_inc(loaded, 16)

        @block.scalar
        def _(act):
            with act.Fori(0, width // 2) as i:
                for b in range(2):
                    act.wait_ge(turned_ok, i * 2 + b + 1)
                    nc.scalar.copy(piece[:, b, :].rearrange("p (s h) -> p s h", h=heads),
                                   view[0][:, :, bass.ds(i * 2 + b, 1), :]).then_inc(copied, 1)
            act.wait_ge(d, DONE)
            with act.Fori(0, width // 2) as i:
                for b in range(2):
                    act.wait_ge(back_ok, i * 2 + b + 1)
                    nc.scalar.copy(piece[:, b, :], line[:, bass.ds((i * 2 + b) * P, P)]).then_inc(piece2, 1)

        @block.tensor
        def _(pe):
            pe.sem_inc(turned_ok, 2)
            pe.sem_inc(back_ok, 2)
            with pe.Fori(0, width // 2) as i:
                for b in range(2):
                    pe.wait_ge(copied, i * 2 + b + 1)
                    pe.wait_ge(lined, i * 2 + b + 1)
                    nc.tensor.transpose(turned[:, b, 0:P], piece[:, b, :], k.ident[:]).then_inc(turned_ok, 1)
            for step in range(2):
                pe.wait_ge(d, ENDS[step])
                nc.tensor.transpose(small[0:1, 0, 0:P], column[:, 2 * step:2 * step + 1], k.ident[:])
                nc.tensor.transpose(small[0:1, 0, P:2 * P], column[:, 2 * step + 1:2 * step + 2],
                                    k.ident[:]).then_inc(pe_step, 1)
                pe.wait_ge(d, CARRIES[step])
                nc.tensor.transpose(small[:, 1, 0:1], carry[:], k.ident[0:1, 0:1]).then_inc(pe_step, 1)
            with pe.Fori(0, width // 2) as i:
                for b in range(2):
                    pe.wait_ge(piece2, i * 2 + b + 1)
                    pe.wait_ge(used, i * 2 + b + 1)
                    nc.tensor.transpose(back[:, b, 0:P], piece[:, b, :], k.ident[:]).then_inc(back_ok, 1)

        @block.vector
        def _(dve):
            dve.sem_inc(lined, 2)
            dve.sem_inc(used, 2)
            with dve.Fori(0, width // 2) as i:
                for b in range(2):
                    dve.wait_ge(turned_ok, i * 2 + b + 3)
                    nc.vector.tensor_copy(line[:, bass.ds((i * 2 + b) * P, P)], turned[:, b, 0:P]).then_inc(lined, 1)
            dve.wait_ge(lined, width + 2)
            dve.wait_ge(loaded, 16 * strips)
            count = [0]

            def stepped(ins):
                count[0] += 1
                ins.then_inc(d, 1)
                dve.wait_ge(d, count[0])

            for step in range(2):
                flip = slice(None, None, -1 if step else 1)
                src, dst = (line, line2) if step == 0 else (line2, line)
                gaps = brk[:, 0:length] if step == 0 else brk[:, 1:length + 1]
                end = length - 1 if step == 0 else 0
                nc.vector.tensor_reduce(column[:, 2 * step:2 * step + 1], gaps, AX.X, ALU.min)
                stepped(nc.vector.tensor_tensor_scan(dst[:, flip], gaps[:, flip], src[:, flip], -BIG, ALU.add, ALU.max))
                stepped(nc.vector.tensor_copy(column[:, 2 * step + 1:2 * step + 2], dst[:, end:end + 1]))
                assert count[0] == ENDS[step]
                dve.wait_ge(pe_step, 2 * step + 1)
                stepped(nc.vector.tensor_copy(row[:], small[0:1, 0, 0:2 * P].rearrange("p (a c) -> p a c", a=2)))
                for h in range(heads):
                    way = row[:].rearrange("p a (s h) -> p a h s", h=heads)[:, :, h, :]
                    out = states[:].rearrange("p (s h) -> p h s", h=heads)[:, h, :]
                    last = nc.vector.tensor_tensor_scan(out[:, flip], way[:, 0, flip], way[:, 1, flip], -BIG,
                                                        ALU.add, ALU.max)
                stepped(last)
                nc.vector.memset(carry[:], -BIG).then_inc(d, 1)
                count[0] += 1
                dve.wait_ge(d, count[0])
                if step == 0:
                    stepped(nc.vector.tensor_copy(carry[:, heads:P], states[:, 0:P - heads]))
                else:
                    stepped(nc.vector.tensor_copy(carry[:, 0:P - heads], states[:, heads:P]))
                assert count[0] == CARRIES[step]
                dve.wait_ge(pe_step, 2 * step + 2)
                stepped(nc.vector.tensor_copy(carried[:], small[:, 1, 0:1]))
                if step == 0:
                    stepped(nc.vector.tensor_tensor_scan(dst[:, flip], gaps[:, flip], src[:, flip], carried[:],
                                                         ALU.add, ALU.max))
                else:
                    stepped(nc.vector.tensor_tensor_scan(line[:, flip], gaps[:, flip], src[:, flip], carried[:],
                                                         ALU.add, ALU.max))
            assert count[0] == DONE
            with dve.Fori(0, width // 2) as i:
                for b in range(2):
                    dve.wait_ge(back_ok, i * 2 + b + 3)
                    top = back[:, b, 0:P].rearrange("p (s h) -> p s h", h=heads)
                    c = bass.ds(i * 2 + b, 1)
                    if keep is not None:
                        nc.vector.tensor_tensor(keep_view[:, :, c, :].rearrange("p s c h -> p s (c h)"), top,
                                                begins_view[:, :, c].to_broadcast([P, strips, heads]), ALU.mult)
                    for v in view[1:]:
                        here = v[:, :, c, :].rearrange("p s c h -> p s (c h)")
                        last = nc.vector.tensor_tensor(here, here, top, ALU.subtract)
                    last.then_inc(used, 1)


ENDS = [2, 10]
CARRIES = [6, 14]
DONE = 16

NBD = NBLK + NBLK % 2
NPD = NBD * P


def score_pass(nc, k, o, index, table, row, head, values_at, store, spread, scores, extra, name):
    heads = D // head
    with ExitStack() as ctx:
        sb, ps, sem = tools(nc, k, ctx, name)
        rows = sb("rows", [P, SLOTS, G, row])
        ring = sb("ring", [P, SLOTS, G], I32)
        onehot = sb("onehot", [P, SLOTS, G, P], BF16)
        onehot_t = sb("onehot_t", [P, 2, G, P], BF16)
        pair = sb("pair", [P, 2, G, D])
        turned = ps("turned", [P, 2, 2 * G, P], BF16)
        own = ps("own", [P, 2, G, D])
        own_self = ps("own_self", [P, 2, 512]) if extra else None
        listed = sem("listed")
        got = [sem(f"got{s}") for s in range(SLOTS)]
        kept = [sem(f"kept{s}") for s in range(SLOTS)]
        running = sem("running")
        hot_ok = sem("hot_ok")
        turned_ok = sem("turned_ok")
        copied = sem("copied")
        spread_ok = sem("spread_ok")
        scored = sem("scored")
        self_ok = sem("self_ok")
        d = sem("d")
        steps = 3 if extra else 1
        block = ctx.enter_context(nc.Block())

        @block.scalar
        def _(act):
            def list_rows(n, s):
                act.wait_ge(scored, n + 1)
                nc.scalar.copy(ring[:, s, :], index[:, bass.ds(n * G, G)]).then_inc(listed, 1)

            act.sem_inc(copied, 2)
            if extra:
                act.sem_inc(self_ok, 2)
            for n in range(SLOTS - 1):
                list_rows(n, n)
            with act.Fori(0, ROUNDS) as i:
                for s in range(SLOTS):
                    n = i * SLOTS + s
                    b = s % 2
                    act.wait_ge(turned_ok, n + 2)
                    act.wait_ge(spread_ok, n + 1)
                    nc.scalar.copy(onehot_t[:, b, :, :], turned[:, b, 0:G, :]).then_inc(copied, 1)
                    list_rows(n + SLOTS - 1, (s + SLOTS - 1) % SLOTS)
                    if extra:
                        act.wait_ge(spread_ok, n + 3)
                        nc.scalar.copy(extra[1][:, bass.ds(n * G, G), :],
                                       own_self[:, b, 0:G * heads].rearrange("p (g h) -> p g h", h=heads)).then_inc(self_ok, 1)

        @block.gpsimd
        def _(pool):
            def a_round(i, first):
                for s in range(SLOTS):
                    if store is not None and not first:
                        pool.wait_ge(kept[s], i * 16)
                    pool.wait_ge(listed, i * SLOTS + s + 1)
                    pool.sem_inc(running, 1)
                    for g in range(G):
                        nc.gpsimd.indirect_dma_start(rows[:, s, g, :], None, table,
                                                     bass.IndirectOffsetOnAxis(ap=ring[:, s, g:g + 1], axis=0),
                                                     ).then_inc(got[s], 16)

            in_rounds(pool, ROUNDS, a_round)

        @block.sync
        def _(sp):
            if store is not None:
                with sp.Fori(0, ROUNDS) as i:
                    for s in range(SLOTS):
                        sp.wait_ge(got[s], i * 16 * G + 16 * G)
                        sp.dma_start(store[bass.ds(i * SLOTS + s, 1), :, :].rearrange("a p (g f) -> p (a g) f", g=G),
                                     rows[:, s, :, values_at:values_at + D]).then_inc(kept[s], 16)
                for s in range(SLOTS):
                    sp.wait_ge(kept[s], 16 * ROUNDS)

        @block.tensor
        def _(pe):
            pe.sem_inc(turned_ok, 1)
            pe.sem_inc(spread_ok, 2)
            with pe.Fori(0, ROUNDS) as i:
                for s in range(SLOTS):
                    n = i * SLOTS + s
                    b = s % 2
                    blocks = load_blocks(nc, pe.engine, o.block[:, bass.ds(n * G, G)], G)
                    pe.wait_ge(hot_ok, n + 1)
                    pe.wait_ge(copied, n + 1)
                    for g in range(G):
                        last = nc.tensor.transpose(turned[:, b, g, :], onehot[:, s, g, :], k.identb[:])
                    last.then_inc(turned_ok, 1)
                    pe.wait_ge(copied, n + 3)
                    pe.wait_ge(scored, n + SLOTS - 1)
                    if extra:
                        pe.wait_ge(self_ok, n + 1)
                    for g in range(G):
                        for part in range(3):
                            last = nc.tensor.matmul(own[:, b, g, :], onehot_t[:, b, g, :],
                                                    spread[:, bass.ds(blocks[g], 1), part, 0:D],
                                                    start=(part == 0), stop=(part == 2))
                        if extra:
                            for part in range(3):
                                last = nc.tensor.matmul(own_self[:, b, g * heads:(g + 1) * heads], onehot_t[:, b, g, :],
                                                        spread[:, bass.ds(blocks[g], 1), part, D:D + heads],
                                                        start=(part == 0), stop=(part == 2))
                    last.then_inc(spread_ok, 1)

        @block.vector
        def _(dve):
            def hot(n, s):
                mark(nc, onehot[:, s, :, :], k.count, o.place[:, bass.ds(n * G, G)]).then_inc(hot_ok, 1)

            def ahead(n, s):
                dve.wait_ge(turned_ok, n + 1)
                hot(n + 2, (s + 2) % SLOTS)

            dve.sem_inc(scored, SLOTS)
            hot(0, 0)
            hot(1, 1)
            with dve.Fori(0, ROUNDS) as i:
                for s in range(SLOTS):
                    n = i * SLOTS + s
                    b = s % 2
                    here = bass.ds(n * G, G)
                    dve.wait_ge(spread_ok, n + 3)
                    dve.wait_ge(got[s], i * 16 * G + 16 * G)
                    dve.wait_ge(scored, n + SLOTS - 1)
                    if not extra:
                        nc.vector.tensor_tensor(pair[:, b, :, :], own[:, b, :, :], rows[:, s, :, 0:D],
                                                ALU.mult).then_inc(d, 1)
                        ahead(n, s)
                        dve.wait_ge(d, n + 1)
                        nc.vector.tensor_reduce(scores[:, here, :],
                                                pair[:, b, :, :].rearrange("p g (h f) -> p g h f", h=heads),
                                                AX.X, ALU.add).then_inc(scored, 1)
                    else:
                        att, self_score, top = extra
                        nc.vector.tensor_tensor(pair[:, b, :, :], own[:, b, :, :], rows[:, s, :, 0:D],
                                                ALU.add).then_inc(d, 1)
                        ahead(n, s)
                        dve.wait_ge(d, n * steps + 1)
                        flat = pair[:, b, :, :].rearrange("p g f -> p (g f)")
                        nc.vector.scalar_tensor_tensor(out=flat, in0=flat, scalar=0.2, in1=flat, op0=ALU.mult,
                                                       op1=ALU.max).then_inc(d, 1)
                        dve.wait_ge(d, n * steps + 2)
                        nc.vector.tensor_tensor(flat, flat, att[:], ALU.mult).then_inc(d, 1)
                        dve.wait_ge(d, n * steps + 3)
                        nc.vector.tensor_reduce(scores[:, here, :],
                                                pair[:, b, :, :].rearrange("p g (h f) -> p g h f", h=heads),
                                                AX.X, ALU.add).then_inc(scored, 1)
            if extra:
                dve.wait_ge(scored, GROUPS + SLOTS)
                dve.wait_ge(self_ok, GROUPS + 2)
                nc.vector.tensor_tensor(top[:, 0:CH, :], scores[:, 0:CH, :], self_score[:, 0:CH, :], ALU.max)


def exponentials(nc, k, tensors, begins, name):
    with ExitStack() as ctx:
        sb, ps, sem = tools(nc, k, ctx, name)
        raised = sem("raised")
        block = ctx.enter_context(nc.Block())

        @block.scalar
        def _(act):
            for t in tensors:
                nc.scalar.activation(t[:], t[:], ACT.Exp).then_inc(raised, 1)

        @block.vector
        def _(dve):
            if begins is not None:
                dve.wait_ge(raised, len(tensors))
                t = tensors[-1]
                nc.vector.tensor_tensor(t[:], t[:], begins[:, 0:CH].rearrange("p (c a) -> p c a", a=1)
                                        .to_broadcast([P, CH, t[:].shape[2]]), ALU.mult)


def sum_pass(nc, k, o, store, weights, extras, total, name):
    extra_w = sum(t[:].shape[2] for t in extras)
    width = extra_w + (D if store is not None else 0)
    with ExitStack() as ctx:
        sb, ps, sem = tools(nc, k, ctx, name)
        values = sb("values", [P, SLOTS, G * D]) if store is not None else None
        terms = sb("terms", [P, SLOTS, G, width])
        odd = sb("odd", [P, total.shape[1], width])
        onehot = sb("onehot", [P, 2, G, P])
        sums = ps("sums", [P, 2, 2, 512])
        loaded = [sem(f"loaded{s}") for s in range(SLOTS)]
        hot = sem("hot")
        taken = sem("taken")
        weighed = sem("weighed")
        summed = sem("summed")
        added = sem("added")
        block = ctx.enter_context(nc.Block())

        if store is not None:
            @block.sync
            def _(sp):
                with sp.Fori(0, ROUNDS) as i:
                    for s in range(SLOTS):
                        sp.wait_ge(weighed, i * SLOTS + s + 1)
                        sp.dma_start(values[:, s, :], store[bass.ds(i * SLOTS + s, 1), :, :]
                                     .rearrange("a p f -> p (a f)")).then_inc(loaded[s], 16)

        @block.scalar
        def _(act):
            with act.Fori(0, ROUNDS) as i:
                for s in range(SLOTS):
                    n = i * SLOTS + s
                    act.wait_ge(summed, n + 1)
                    at = width - extra_w
                    for t in extras:
                        w = t[:].shape[2]
                        last = nc.scalar.copy(terms[:, s, :, at:at + w], t[:, bass.ds(n * G, G), :])
                        at += w
                    last.then_inc(taken, 1)

        if store is not None:
            @block.gpsimd
            def _(pool):
                heads = weights[:].shape[2]
                pool.sem_inc(weighed, SLOTS)
                with pool.Fori(0, ROUNDS) as i:
                    for s in range(SLOTS):
                        pool.wait_ge(taken, i * SLOTS + s + 1)
                        pool.wait_ge(loaded[s], i * 16 + 16)
                        nc.gpsimd.tensor_tensor(
                            terms[:, s, :, 0:D].rearrange("p g (h f) -> p g h f", h=heads),
                            values[:, s, :].rearrange("p (g h f) -> p g h f", g=G, h=heads),
                            terms[:, s, :, D:D + heads].rearrange("p g (h a) -> p g h a", a=1)
                            .to_broadcast([P, G, heads, D // heads]), ALU.mult).then_inc(weighed, 1)

        @block.tensor
        def _(pe):
            pe.sem_inc(summed, SLOTS)
            with pe.Fori(0, ROUNDS) as i:
                for s in range(SLOTS):
                    n = i * SLOTS + s
                    b = s % 2
                    pe.wait_ge(hot, n + 1)
                    pe.wait_ge(taken, n + 1)
                    if store is not None:
                        pe.wait_ge(weighed, n + 1 + SLOTS)
                    pe.wait_ge(added, (n + 1) * G)
                    for g in range(G):
                        last = nc.tensor.matmul(sums[:, b, g // 2, (g % 2) * width:(g % 2 + 1) * width],
                                                onehot[:, b, g, :], terms[:, s, g, :], start=True, stop=True)
                    last.then_inc(summed, 1)

        @block.vector
        def _(dve):
            dve.sem_inc(added, 2 * G - 1)
            nc.vector.memset(odd[:], 0.0)
            nc.vector.memset(total[:], 0.0).then_inc(added, 1)

            def add(n, b):
                blocks = load_blocks(nc, dve.engine, o.block[:, bass.ds(n * G, G)], G)
                dve.wait_ge(summed, n + SLOTS + 1)
                for g in range(G):
                    dve.wait_ge(added, n * G + g + 2 * G - 1)
                    here = (total, odd)[g % 2][:, bass.ds(blocks[g], 1), :]
                    part = sums[:, b, g // 2:g // 2 + 1, (g % 2) * width:(g % 2 + 1) * width]
                    nc.vector.tensor_tensor(here, here, part, ALU.add).then_inc(added, 1)

            def a_round(i, first):
                for s in range(SLOTS):
                    n = i * SLOTS + s
                    b = s % 2
                    dve.wait_ge(summed, n + SLOTS - 1)
                    mark(nc, onehot[:, b, :, :], k.count, o.place[:, bass.ds(n * G, G)]).then_inc(hot, 1)
                    if not (first and s < 2):
                        add(n - 2, b)

            in_rounds(dve, ROUNDS, a_round)
            for n in (GROUPS - 2, GROUPS - 1):
                add(n, n % 2)
            dve.wait_ge(added, GROUPS * G + 2 * G)
            nc.vector.tensor_tensor(total[:], total[:], odd[:], ALU.add)


def weigh_and_sum(nc, k, o, index, table, spread, total, name):
    heads = 8
    row = 2 * D + heads
    with ExitStack() as ctx:
        sb, ps, sem = tools(nc, k, ctx, name)
        rows = sb("rows", [P, SLOTS, G, row])
        ring = sb("ring", [P, SLOTS, G], I32)
        onehot = sb("onehot", [P, 2, G, P], BF16)
        onehot_f = sb("onehot_f", [P, 2, G, P])
        onehot_t = sb("onehot_t", [P, 2, G, P], BF16)
        pair = sb("pair", [P, 2, G, D])
        score = sb("score", [P, 2, G, heads])
        weight = sb("weight", [P, 2, G, heads])
        terms = sb("terms", [P, 2, G, D])
        turned = ps("turned", [P, 2, 2 * G, P], BF16)
        own = ps("own", [P, 2, G, D])
        sums = ps("sums", [P, 2, G, D])
        listed = sem("listed")
        got = [sem(f"got{s}") for s in range(SLOTS)]
        running = sem("running")
        hot_ok = sem("hot_ok")
        turned_ok = sem("turned_ok")
        copied = sem("copied")
        widened = sem("widened")
        spread_ok = sem("spread_ok")
        lowered = sem("lowered")
        raised = sem("raised")
        weighed = sem("weighed")
        summed = sem("summed")
        added = sem("added")
        d = sem("d")
        block = ctx.enter_context(nc.Block())

        @block.scalar
        def _(act):
            def list_rows(n, s):
                act.wait_ge(weighed, n + 1)
                nc.scalar.copy(ring[:, s, :], index[:, bass.ds(n * G, G)]).then_inc(listed, 1)

            def take_onehots(n, b):
                act.wait_ge(turned_ok, n + 2)
                act.wait_ge(spread_ok, n + 1)
                nc.scalar.copy(onehot_t[:, b, :, :], turned[:, b, 0:G, :]).then_inc(copied, 1)

            def widen(n, b):
                act.wait_ge(summed, n + 1)
                nc.scalar.copy(onehot_f[:, b, :, :], onehot[:, b, :, :]).then_inc(widened, 1)

            act.sem_inc(copied, 2)
            for n in range(SLOTS - 1):
                list_rows(n, n)
            take_onehots(0, 0)
            widen(0, 0)
            with act.Fori(0, ROUNDS) as i:
                for s in range(SLOTS):
                    n = i * SLOTS + s
                    b = s % 2
                    take_onehots(n + 1, 1 - b)
                    act.wait_ge(lowered, n + 1)
                    nc.scalar.activation(weight[:, b, :, :], score[:, b, :, :], ACT.Exp).then_inc(raised, 1)
                    widen(n + 1, 1 - b)
                    list_rows(n + SLOTS - 1, (s + SLOTS - 1) % SLOTS)

        @block.gpsimd
        def _(pool):
            with pool.Fori(0, ROUNDS) as i:
                for s in range(SLOTS):
                    pool.wait_ge(listed, i * SLOTS + s + 1)
                    pool.sem_inc(running, 1)
                    for g in range(G):
                        nc.gpsimd.indirect_dma_start(rows[:, s, g, :], None, table,
                                                     bass.IndirectOffsetOnAxis(ap=ring[:, s, g:g + 1], axis=0),
                                                     ).then_inc(got[s], 16)

        @block.tensor
        def _(pe):
            def spread_own(n, b):
                blocks = load_blocks(nc, pe.engine, o.block[:, bass.ds(n * G, G)], G)
                pe.wait_ge(hot_ok, n + 1)
                pe.wait_ge(copied, n + 1)
                for g in range(G):
                    last = nc.tensor.transpose(turned[:, b, g, :], onehot[:, b, g, :], k.identb[:])
                last.then_inc(turned_ok, 1)
                pe.wait_ge(copied, n + 3)
                pe.wait_ge(weighed, n + SLOTS - 1)
                for g in range(G):
                    for part in range(3):
                        last = nc.tensor.matmul(own[:, b, g, :], onehot_t[:, b, g, :],
                                                spread[:, bass.ds(blocks[g], 1), part, 0:D],
                                                start=(part == 0), stop=(part == 2))
                last.then_inc(spread_ok, 1)

            pe.sem_inc(turned_ok, 1)
            pe.sem_inc(spread_ok, 2)
            pe.sem_inc(summed, 2)
            spread_own(0, 0)
            with pe.Fori(0, ROUNDS) as i:
                for s in range(SLOTS):
                    n = i * SLOTS + s
                    b = s % 2
                    spread_own(n + 1, 1 - b)
                    pe.wait_ge(weighed, n + 1 + SLOTS)
                    pe.wait_ge(widened, n + 1)
                    pe.wait_ge(added, (n + 1) * G)
                    for g in range(G):
                        last = nc.tensor.matmul(sums[:, b, g, :], onehot_f[:, b, g, :], terms[:, b, g, :],
                                                start=True, stop=True)
                    last.then_inc(summed, 1)

        @block.vector
        def _(dve):
            def hot(n, b):
                mark(nc, onehot[:, b, :, :], k.count, o.place[:, bass.ds(n * G, G)]).then_inc(hot_ok, 1)

            def add(n, b, blocks, g):
                dve.wait_ge(added, n * G + g + 2 * G)
                here = total[:, bass.ds(blocks[g], 1), :]
                nc.vector.tensor_tensor(here, here, sums[:, b, g:g + 1, :], ALU.add).then_inc(added, 1)

            dve.sem_inc(added, 2 * G - 1)
            dve.sem_inc(weighed, SLOTS)
            nc.vector.memset(total[:], 0.0).then_inc(added, 1)
            hot(0, 0)

            def a_round(i, first):
                for s in range(SLOTS):
                    n = i * SLOTS + s
                    b = s % 2
                    adding = not (first and s < 2)
                    if adding:
                        blocks = load_blocks(nc, dve.engine, o.block[:, bass.ds(n * G - 2 * G, G)], G)
                    dve.wait_ge(turned_ok, n + 1)
                    if not (first and s == 0):
                        dve.wait_ge(widened, n)
                    hot(n + 1, 1 - b)
                    dve.wait_ge(spread_ok, n + 3)
                    dve.wait_ge(got[s], i * 16 * G + 16 * G)
                    dve.wait_ge(weighed, n + SLOTS - 1)
                    nc.vector.tensor_tensor(pair[:, b, :, :], own[:, b, :, :], rows[:, s, :, 0:D],
                                            ALU.mult).then_inc(d, 1)
                    dve.wait_ge(summed, n + 1)
                    if adding:
                        add(n - 2, b, blocks, 0)
                    dve.wait_ge(d, n * 3 + 1)
                    nc.vector.tensor_reduce(score[:, b, :, :],
                                            pair[:, b, :, :].rearrange("p g (h f) -> p g h f", h=heads),
                                            AX.X, ALU.add).then_inc(d, 1)
                    if adding:
                        add(n - 2, b, blocks, 1)
                    dve.wait_ge(d, n * 3 + 2)
                    nc.vector.tensor_tensor(score[:, b, :, :], score[:, b, :, :], rows[:, s, :, 2 * D:row],
                                            ALU.subtract).then_inc(d, 1)
                    if adding:
                        add(n - 2, b, blocks, 2)
                    dve.wait_ge(d, n * 3 + 3)
                    nc.vector.tensor_single_scalar(score[:, b, :, :], score[:, b, :, :], 0.0,
                                                   ALU.min).then_inc(lowered, 1)
                    if adding:
                        add(n - 2, b, blocks, 3)
                    dve.wait_ge(raised, n + 1)
                    nc.vector.tensor_tensor(
                        terms[:, b, :, :].rearrange("p g (h f) -> p g h f", h=heads),
                        rows[:, s, :, D:2 * D].rearrange("p g (h f) -> p g h f", h=heads),
                        weight[:, b, :, :].rearrange("p g (h a) -> p g h a", a=1)
                        .to_broadcast([P, G, heads, D // heads]), ALU.mult).then_inc(weighed, 1)

            in_rounds(dve, ROUNDS, a_round)
            dve.wait_ge(summed, GROUPS + 2)
            for n in (GROUPS - 2, GROUPS - 1):
                blocks = load_blocks(nc, dve.engine, o.block[:, n * G:(n + 1) * G], G)
                for g in range(G):
                    add(n, n % 2, blocks, g)

HEADS1, HEADS2, HEADS3 = 8, 4, 8
PIECE = 10
PIECES = NBD // PIECE
assert PIECES * PIECE == NBD
BATCH = 5
BATCHES = NBD // BATCH
assert BATCHES * BATCH == NBD and BATCHES % 2 == 0


def in_steps(engine, step):
    count = [0]

    def take(instruction):
        count[0] += 1
        instruction.then_inc(step, 1)
        engine.wait_ge(step, count[0])

    return take


def at(n, value):
    return isinstance(n, int) and n == value


def turn_weights(nc, k, pairs, name):
    with ExitStack() as ctx:
        sb, ps, sem = tools(nc, k, ctx, name)
        w = sb("w", [P, len(pairs), D])
        turned = ps("turned", [P, 512])
        loaded = sem("loaded")
        turned_ok = sem("turned_ok")
        block = ctx.enter_context(nc.Block())

        @block.sync
        def _(sp):
            for n, (_, source) in enumerate(pairs):
                sp.dma_start(w[:, n, :], source).then_inc(loaded, 16)

        @block.tensor
        def _(pe):
            pe.wait_ge(loaded, 16 * len(pairs))
            for n in range(len(pairs)):
                last = nc.tensor.transpose(turned[:, n * D:(n + 1) * D], w[:, n, :], k.ident[:])
            last.then_inc(turned_ok, 1)

        @block.vector
        def _(dve):
            dve.wait_ge(turned_ok, 1)
            for n, (out, _) in enumerate(pairs):
                nc.vector.tensor_copy(out, turned[:, n * D:(n + 1) * D])


def load_all(nc, k, pairs, name):
    with ExitStack() as ctx:
        sb, ps, sem = tools(nc, k, ctx, name)
        loaded = sem("loaded")
        block = ctx.enter_context(nc.Block())

        @block.sync
        def _(sp):
            for out, source in pairs:
                sp.dma_start(out, source).then_inc(loaded, 16)
            sp.wait_ge(loaded, 16 * len(pairs))


def row_on_all(vector):
    return vector.rearrange("(a f) -> a f", a=1).to_broadcast([P, vector.shape[0]])


def split_parts(nc, k, source, spread, at, name):
    width = source.shape[2]
    with ExitStack() as ctx:
        sb, ps, sem = tools(nc, k, ctx, name)
        rounded = sem("rounded")
        left = sem("left")
        pieces = [slice(n * PIECE, (n + 1) * PIECE) for n in range(PIECES)]
        block = ctx.enter_context(nc.Block())

        @block.scalar
        def _(act):
            for part in range(2):
                for n, piece in enumerate(pieces):
                    if part > 0:
                        act.wait_ge(left, n + 1)
                    nc.scalar.copy(spread[:, piece, part, at:at + width], source[:, piece, :]).then_inc(rounded, 1)

        @block.vector
        def _(dve):
            for part in range(2):
                for n, piece in enumerate(pieces):
                    dve.wait_ge(rounded, part * PIECES + n + 1)
                    nc.vector.tensor_tensor(source[:, piece, :], source[:, piece, :],
                                            spread[:, piece, part, at:at + width], ALU.subtract).then_inc(left, 1)
            for n, piece in enumerate(pieces):
                dve.wait_ge(left, PIECES + n + 1)
                nc.vector.tensor_copy(spread[:, piece, 2, at:at + width], source[:, piece, :])


def layernorm(nc, k, x, out, name):
    with ExitStack() as ctx:
        sb, ps, sem = tools(nc, k, ctx, name)
        square = sb("square", [P, 2, PIECE, D])
        mean = sb("mean", [P, NBD])
        var = sb("var", [P, NBD])
        root = sb("root", [P, NBD])
        scale = sb("scale", [P, NBD])
        centred = sem("centred")
        squared = sem("squared")
        summed = sem("summed")
        deviated = sem("deviated")
        step = sem("step")
        scaled = sem("scaled")
        stored = sem("stored")
        block = ctx.enter_context(nc.Block())
        spread = lambda t, n: t[:, n * PIECE:(n + 1) * PIECE].rearrange("p (b a) -> p b a", a=1).to_broadcast([P, PIECE, D])

        @block.vector
        def _(dve):
            chain = in_steps(dve, step)
            dve.sem_inc(summed, 2)
            for n in range(PIECES):
                here = x[:, n * PIECE:(n + 1) * PIECE, :]
                m = mean[:, n * PIECE:(n + 1) * PIECE]
                chain(nc.vector.tensor_reduce(m, here, AX.X, ALU.add))
                chain(nc.vector.tensor_scalar(m, m, 1.0 / D, None, ALU.mult))
                nc.vector.tensor_tensor(here, here, spread(mean, n), ALU.subtract).then_inc(centred, 1)
            for n in range(PIECES):
                dve.wait_ge(squared, n + 1)
                nc.vector.tensor_reduce(var[:, n * PIECE:(n + 1) * PIECE], square[:, n % 2, :, :], AX.X,
                                        ALU.add).then_inc(summed, 1)
            dve.wait_ge(summed, PIECES + 2)
            chain(nc.vector.tensor_scalar(var[:], var[:], 1.0 / D, EPS, ALU.mult, ALU.add))
            dve.wait_ge(deviated, 1)
            chain(nc.vector.reciprocal(scale[:], root[:]))
            for n in range(PIECES):
                here = x[:, n * PIECE:(n + 1) * PIECE, :]
                nc.vector.tensor_tensor(here, here, spread(scale, n), ALU.mult).then_inc(scaled, 1)

        @block.scalar
        def _(act):
            for n in range(PIECES):
                act.wait_ge(centred, n + 1)
                act.wait_ge(summed, n + 1)
                nc.scalar.activation(square[:, n % 2, :, :], x[:, n * PIECE:(n + 1) * PIECE, :],
                                     ACT.Square).then_inc(squared, 1)
            act.wait_ge(step, 2 * PIECES + 1)
            nc.scalar.activation(root[:], var[:], ACT.Sqrt).then_inc(deviated, 1)

        if out is not None:
            @block.sync
            def _(sp):
                full = NBLK - 1
                sp.wait_ge(scaled, PIECES)
                sp.dma_start(out[0:full * P, :].rearrange("(b p) f -> p b f", p=P), x[:, 0:full, :]).then_inc(stored, 16)
                sp.dma_start(out[full * P:N, :], x[0:TAIL, full, :]).then_inc(stored, 16)
                sp.wait_ge(stored, 32)


def polynomial(nc, k, hops, weights, name):
    with ExitStack() as ctx:
        sb, ps, sem = tools(nc, k, ctx, name)
        w = sb("w", [P, 4, D])
        z = sb("z", [P, 2, 4, BATCH, D])
        zt = sb("zt", [P, 2, 4, P])
        turned = ps("turned", [P, 2, 4, P])
        y = ps("y", [P, 2, 1024])
        loaded_w = sem("loaded_w")
        loaded = [sem("loaded0"), sem("loaded1")]
        own = sem("own")
        turned_ok = sem("turned_ok")
        copied = sem("copied")
        mixed = sem("mixed")
        added = sem("added")
        block = ctx.enter_context(nc.Block())

        @block.sync
        def _(sp):
            sp.dma_start(w[:], weights.rearrange("t p f -> p t f")).then_inc(loaded_w, 16)
            with sp.Fori(0, BATCHES // 2) as i:
                for b in range(2):
                    n = i * 2 + b
                    sp.wait_ge(turned_ok, n * BATCH + BATCH)
                    for h in range(3):
                        sp.dma_start(z[:, b, 1 + h, :, :], hops[h][bass.ds(n * BATCH * P, BATCH * P), :]
                                     .rearrange("(j p) f -> p j f", p=P)).then_inc(loaded[b], 16)

        @block.scalar
        def _(act):
            act.sem_inc(copied, 2)
            with act.Fori(0, BATCHES // 2) as i:
                for b in range(2):
                    n = i * 2 + b
                    act.wait_ge(turned_ok, n * BATCH + BATCH)
                    nc.scalar.copy(z[:, b, 0, :, :], k.x[:, bass.ds(n * BATCH, BATCH), :]).then_inc(own, 1)
                    for j in range(BATCH):
                        c = (b * BATCH + j) % 2
                        act.wait_ge(turned_ok, n * BATCH + j + 2 * BATCH + 1)
                        act.wait_ge(mixed, n * BATCH + j + 1)
                        nc.scalar.copy(zt[:, c, :, :], turned[:, c, :, :]).then_inc(copied, 1)

        @block.tensor
        def _(pe):
            def turn(n, m, b, j):
                if j == 0:
                    pe.wait_ge(own, n + 1)
                c = (b * BATCH + j) % 2
                pe.wait_ge(copied, m + 1)
                for t in range(4):
                    last = nc.tensor.transpose(turned[:, c, t, :], z[:, b, t, j, :], k.ident[:])
                last.then_inc(turned_ok, 1)

            def multiply(m, b, j):
                c = (b * BATCH + j) % 2
                pe.wait_ge(copied, m + 3)
                for t in range(4):
                    last = nc.tensor.matmul(y[:, b, j * D:(j + 1) * D], zt[:, c, t, :], w[:, t, :], start=(t == 0),
                                            stop=(t == 3))
                last.then_inc(mixed, 1)

            pe.sem_inc(turned_ok, 2 * BATCH)
            pe.sem_inc(mixed, 2)
            pe.wait_ge(loaded_w, 16)
            with pe.Fori(0, BATCHES // 2) as i:
                for b in range(2):
                    n = i * 2 + b
                    m = n * BATCH
                    pe.wait_ge(loaded[b], i * 48 + 48)
                    pe.wait_ge(added, n + 1)
                    turn(n, m, b, 0)
                    for j in range(1, BATCH):
                        turn(n, m + j, b, j)
                        multiply(m + (j - 1), b, j - 1)
                    multiply(m + (BATCH - 1), b, BATCH - 1)

        @block.vector
        def _(dve):
            dve.sem_inc(added, 2)
            with dve.Fori(0, BATCHES // 2) as i:
                for b in range(2):
                    n = i * 2 + b
                    dve.wait_ge(mixed, n * BATCH + BATCH + 2)
                    here = k.x[:, bass.ds(n * BATCH, BATCH), :]
                    nc.vector.scalar_tensor_tensor(out=here, in0=y[:, b, 0:BATCH * D].rearrange("p (j f) -> p j f", j=BATCH),
                                                   scalar=float(D) ** -0.5, in1=here,
                                                   op0=ALU.mult, op1=ALU.add).then_inc(added, 1)


def type_weights(nc, k, node_type, comps, mix, name):
    with ExitStack() as ctx:
        sb, ps, sem = tools(nc, k, ctx, name)
        kind_i = sb("kind_i", [P, NBD], I32)
        kind = sb("kind", [P, NBD])
        comp = sb("comp", [P, TYPES, 4 * BASES])
        is_type = sb("is_type", [P, 2, NBD])
        part = sb("part", [P, 2, NBD, 4 * BASES])
        step = sem("step")
        padded = sem("padded")
        loaded = sem("loaded")
        full = NBLK - 1
        block = ctx.enter_context(nc.Block())

        @block.sync
        def _(sp):
            for n, c in enumerate(comps):
                sp.dma_start(comp[:, :, n * BASES:(n + 1) * BASES],
                             c.rearrange("(a t) b -> a t b", a=1).to_broadcast([P, TYPES, BASES])).then_inc(loaded, 16)
            sp.wait_ge(padded, 1)
            with nc.allow_non_contiguous_dma(reason="one integer per node, once"):
                sp.dma_start(kind_i[:, 0:full], node_type[0:full * P].rearrange("(b p) -> p b", p=P)).then_inc(loaded, 16)
                sp.dma_start(kind_i[0:TAIL, full:full + 1],
                             node_type[full * P:N].rearrange("(p a) -> p a", a=1)).then_inc(loaded, 16)

        @block.vector
        def _(dve):
            chain = in_steps(dve, step)
            nc.vector.memset(kind_i[:], 0).then_inc(padded, 1)
            nc.vector.memset(mix[:], 0.0)
            dve.wait_ge(loaded, 16 * 6)
            chain(nc.vector.tensor_copy(kind[:], kind_i[:]))
            for t in range(TYPES):
                chain(nc.vector.tensor_single_scalar(is_type[:, t % 2, :], kind[:], float(t), ALU.is_equal))
                chain(nc.vector.tensor_tensor(
                    part[:, t % 2, :, :],
                    is_type[:, t % 2, :].rearrange("p (b a) -> p b a", a=1).to_broadcast([P, NBD, 4 * BASES]),
                    comp[:, t:t + 1, :].to_broadcast([P, NBD, 4 * BASES]), ALU.mult))
                chain(nc.vector.tensor_tensor(mix[:], mix[:], part[:, t % 2, :, :], ALU.add))


def relation_weights(nc, k, att, msg, pri, att_sb, msg_sb, name):
    head = D // HEADS1
    with ExitStack() as ctx:
        sb, ps, sem = tools(nc, k, ctx, name)
        priority = sb("priority", [P, TYPES * HEADS1])
        cleared = sem("cleared")
        loaded = sem("loaded")
        block = ctx.enter_context(nc.Block())

        @block.vector
        def _(dve):
            nc.vector.memset(att_sb[:], 0.0)
            nc.vector.memset(msg_sb[:], 0.0).then_inc(cleared, 1)
            dve.wait_ge(loaded, 16 * (2 * HEADS1 + 1))
            a = att_sb[:].rearrange("p t (h j) -> p (t h) j", h=HEADS1)
            nc.vector.scalar_tensor_tensor(out=a, in0=a, scalar=float(head) ** -0.5,
                                           in1=priority[:].rearrange("p (t a) -> p t a", a=1)
                                           .to_broadcast([P, TYPES * HEADS1, head]), op0=ALU.mult, op1=ALU.mult)

        @block.sync
        def _(sp):
            sp.dma_start(priority[:], row_on_all(pri.rearrange("t h -> (t h)"))).then_inc(loaded, 16)
            sp.wait_ge(cleared, 1)
            for source, out in ((att, att_sb), (msg, msg_sb)):
                for h in range(HEADS1):
                    sp.dma_start(out[h * head:(h + 1) * head, :, h * head:(h + 1) * head],
                                 source[:, h, :, :].rearrange("t i j -> i t j")).then_inc(loaded, 16)


def in_blocks(engine, step):
    step(0, 0, None)
    step(1, 1, None)
    step(2, 0, None)
    with engine.Fori(0, (NBD - 4) // 2) as i:
        step(i * 2 + 3, 1, i * 16 + 16)
        step(i * 2 + 4, 0, i * 16 + 16)
    step(NBD - 1, 1, 16 * (NBD // 2 - 1))


def relation_tables(nc, k, bases, att_sb, msg_sb, mix, queries, table, name):
    with ExitStack() as ctx:
        sb, ps, sem = tools(nc, k, ctx, name)
        w = sb("w", [P, 3, BASES * D])
        x = sb("x", [P, 2, D])
        xt = sb("xt", [P, 2, P])
        scaled = sb("scaled", [P, 4, D])
        kv = sb("kv", [P, 2, D])
        kvt = sb("kvt", [P, 2, P])
        rows = sb("rows", [P, 2, TYPES, 2 * D])
        turned = ps("turned", [P, 4, P])
        based = ps("based", [P, 3, BASES, D])
        related = ps("related", [P, 4, 4, D])
        loaded = sem("loaded")
        own = sem("own")
        turned_x = sem("turned_x")
        xt_ok = sem("xt_ok")
        based_ok = sem("based_ok")
        mixed = sem("mixed")
        d = sem("d")
        turned_kv = sem("turned_kv")
        kvt_ok = sem("kvt_ok")
        related_ok = sem("related_ok")
        left = sem("left")
        right = sem("right")
        stored = [sem("stored0"), sem("stored1")]
        block = ctx.enter_context(nc.Block())
        rows_of = lambda b, half: rows[:, b, :, half * D:(half + 1) * D]

        @block.sync
        def _(sp):
            for n, base in enumerate(bases):
                sp.dma_start(w[:, n, :].rearrange("p (b o) -> p b o", b=BASES),
                             base.rearrange("b (i o) -> i b o", o=D)).then_inc(loaded, 16)
            with sp.Fori(0, NBD // 2) as i:
                for b in range(2):
                    n = i * 2 + b
                    sp.wait_ge(left, n + 1)
                    sp.wait_ge(right, n + 1)
                    sp.dma_start(table[:, bass.ds(n * P, P), :].rearrange("t p f -> p t f"),
                                 rows[:, b, :, :]).then_inc(stored[b], 16)
            for b in range(2):
                sp.wait_ge(stored[b], 16 * (NBD // 2))

        @block.scalar
        def _(act):
            def own_rows(n, b):
                act.wait_ge(turned_x, n + 1)
                nc.scalar.copy(x[:, b, :], k.x[:, bass.ds(n, 1), :]).then_inc(own, 1)

            def take_turned(n, b):
                act.wait_ge(turned_x, n + 3)
                nc.scalar.copy(xt[:, b, :], turned[:, 0, :]).then_inc(xt_ok, 1)

            def take_rows(n, b, saved):
                act.wait_ge(related_ok, n + 1)
                if saved is not None:
                    act.wait_ge(stored[b], saved)
                nc.scalar.copy(rows_of(b, 0), related[:, 0:2, :, :].rearrange("p a t f -> p (a t) f")).then_inc(left, 1)

            def step(n, b, saved):
                if not at(n, NBD - 1):
                    own_rows(n + 1, 1 - b)
                    take_turned(n + 1, 1 - b)
                if not at(n, 0):
                    take_rows(n - 1, 1 - b, saved)
                act.wait_ge(turned_kv, n + 1)
                nc.scalar.copy(kvt[:], turned[:, 2:4, :]).then_inc(kvt_ok, 1)

            own_rows(0, 0)
            take_turned(0, 0)
            in_blocks(act, step)
            take_rows(NBD - 1, 1, 16 * (NBD // 2 - 1))

        @block.tensor
        def _(pe):
            def turn_x(n, b):
                pe.wait_ge(own, n + 1)
                nc.tensor.transpose(turned[:, 0, :], x[:, b, :], k.ident[:]).then_inc(turned_x, 1)

            def relate():
                for j, rel in enumerate((att_sb, msg_sb)):
                    for half in range(2):
                        last = nc.tensor.matmul(related[:, 2 * j + half, :, :], kvt[:, j, :],
                                                rel[:, 4 * half:4 * half + 4, :], start=True, stop=True)
                last.then_inc(related_ok, 1)

            def step(n, b, saved):
                pe.wait_ge(xt_ok, n + 1)
                if not at(n, 0):
                    pe.wait_ge(mixed, n)
                for j in range(3):
                    nc.tensor.matmul(based[:, j, :, :], xt[:, b, :], w[:, j, :], start=True,
                                     stop=True).then_inc(based_ok, 1)
                if not at(n, 0):
                    pe.wait_ge(kvt_ok, n)
                if not at(n, NBD - 1):
                    turn_x(n + 1, 1 - b)
                if not at(n, 0):
                    if not at(n, 1):
                        pe.wait_ge(left, n - 1)
                        pe.wait_ge(right, n - 1)
                    relate()
                pe.wait_ge(mixed, n + 1)
                if not at(n, NBD - 1):
                    pe.wait_ge(xt_ok, n + 2)
                for j in range(2):
                    turn = nc.tensor.transpose(turned[:, 2 + j, :], kv[:, j, :], k.ident[:])
                turn.then_inc(turned_kv, 1)

            pe.sem_inc(turned_x, 2)
            pe.wait_ge(loaded, 48)
            turn_x(0, 0)
            in_blocks(pe, step)
            pe.wait_ge(kvt_ok, NBD)
            pe.wait_ge(left, NBD - 1)
            pe.wait_ge(right, NBD - 1)
            relate()

        @block.vector
        def _(dve):
            def take_rows(n, b, saved):
                dve.wait_ge(related_ok, n + 1)
                if saved is not None:
                    dve.wait_ge(stored[b], saved)
                nc.vector.tensor_copy(rows_of(b, 1), related[:, 2:4, :, :].rearrange("p a t f -> p (a t) f")).then_inc(right, 1)

            def step(n, b, saved):
                for basis in range(BASES):
                    for j, out in enumerate((queries[:, bass.ds(n, 1), :], kv[:, 0:1, :], kv[:, 1:2, :])):
                        part = based[:, j:j + 1, basis, :]
                        by = mix[:, bass.ds(n, 1), j * BASES + basis:j * BASES + basis + 1].rearrange("p a b -> p (a b)")
                        if basis == 0:
                            dve.wait_ge(based_ok, n * 3 + 1 + j)
                            if j > 0 and not at(n, 0):
                                dve.wait_ge(turned_kv, n)
                            made = nc.vector.tensor_scalar(out, part, by, None, ALU.mult)
                        else:
                            dve.wait_ge(d, n * 12 + (basis - 1) * 3 + j + 1)
                            made = nc.vector.scalar_tensor_tensor(out=out, in0=part, scalar=by, in1=out,
                                                                  op0=ALU.mult, op1=ALU.add)
                        made.then_inc(d, 1)
                dve.wait_ge(d, n * 12 + 12)
                dve.sem_inc(mixed, 1)
                if not at(n, 0):
                    take_rows(n - 1, 1 - b, saved)

            in_blocks(dve, step)
            take_rows(NBD - 1, 1, 16 * (NBD // 2 - 1))


def relation_output(nc, k, total, base, loop_w, bias, mix, name):
    pairs = NBD // 2
    with ExitStack() as ctx:
        sb, ps, sem = tools(nc, k, ctx, name)
        w = sb("w", [P, BASES * D])
        wl = sb("wl", [P, D])
        bias_row = sb("bias_row", [P, D])
        inputs = sb("inputs", [P, 2, 2, 2, D])
        by = sb("by", [P, 2, 2, BASES])
        turned_sb = sb("turned_sb", [P, 2, 4, P])
        mixed = sb("mixed", [P, 2, 2, D])
        turned = ps("turned", [P, 2, 4, P])
        based = ps("based", [P, 2, 2, BASES, D])
        looped = ps("looped", [P, 2, 512])
        loaded = sem("loaded")
        normed = sem("normed")
        step = sem("step")
        own = sem("own")
        turned_ok = sem("turned_ok")
        copied = sem("copied")
        based_ok = sem("based_ok")
        weights = sem("weights")
        d = sem("d")
        done = sem("done")
        block = ctx.enter_context(nc.Block())

        @block.sync
        def _(sp):
            sp.dma_start(w[:].rearrange("p (b o) -> p b o", b=BASES), base.rearrange("b (i o) -> i b o", o=D)).then_inc(loaded, 16)
            sp.dma_start(wl[:], loop_w).then_inc(loaded, 16)
            sp.dma_start(bias_row[:], row_on_all(bias)).then_inc(loaded, 16)

        @block.scalar
        def _(act):
            def own_rows(n, b):
                act.wait_ge(normed, n * 2 + 2)
                act.wait_ge(turned_ok, n + 1)
                nc.scalar.copy(inputs[:, b, 0, :, :], total[:, bass.ds(n * 2, 2), 0:D])
                nc.scalar.copy(inputs[:, b, 1, :, :], k.x[:, bass.ds(n * 2, 2), :]).then_inc(own, 1)

            def a_pair(n, b, last=False):
                if not last:
                    own_rows(n + 1, 1 - b)
                act.wait_ge(turned_ok, n + 3)
                act.wait_ge(based_ok, n + 1)
                nc.scalar.copy(turned_sb[:, b, :, :], turned[:, b, :, :]).then_inc(copied, 1)
                act.wait_ge(done, n + 1)
                nc.scalar.copy(by[:, b, :, :], mix[:, bass.ds(n * 2, 2), 3 * BASES:4 * BASES]).then_inc(weights, 1)

            act.sem_inc(copied, 2)
            own_rows(0, 0)
            with act.Fori(0, pairs // 2) as i:
                a_pair(i * 2, 0)
                a_pair(i * 2 + 1, 1)
            a_pair(pairs - 1, 0, True)

        @block.tensor
        def _(pe):
            def turn(n, b):
                pe.wait_ge(own, n + 1)
                pe.wait_ge(copied, n + 1)
                for j in range(4):
                    last = nc.tensor.transpose(turned[:, b, j, :], inputs[:, b, j // 2, j % 2, :], k.ident[:])
                last.then_inc(turned_ok, 1)

            def a_pair(n, b, last=False):
                if not last:
                    turn(n + 1, 1 - b)
                pe.wait_ge(copied, n + 3)
                pe.wait_ge(done, n + 1)
                for j in range(2):
                    nc.tensor.matmul(based[:, b, j, :, :], turned_sb[:, b, j, :], w[:], start=True, stop=True)
                    product = nc.tensor.matmul(looped[:, b, j * D:(j + 1) * D], turned_sb[:, b, 2 + j, :], wl[:],
                                               start=True, stop=True)
                product.then_inc(based_ok, 1)

            pe.sem_inc(turned_ok, 2)
            pe.sem_inc(based_ok, 2)
            pe.wait_ge(loaded, 48)
            turn(0, 0)
            with pe.Fori(0, pairs // 2) as i:
                a_pair(i * 2, 0)
                a_pair(i * 2 + 1, 1)
            a_pair(pairs - 1, 0, True)

        @block.vector
        def _(dve):
            chain = in_steps(dve, step)
            den = total[:, 0:NBLK, D:D + HEADS1]
            chain(nc.vector.tensor_single_scalar(den, den, TINY, ALU.max))
            chain(nc.vector.reciprocal(den, den))
            for n in range(NBLK):
                part = total[:, n, 0:D].rearrange("p (h f) -> p h f", h=HEADS1)
                over = total[:, n, D:D + HEADS1].rearrange("p (h a) -> p h a", a=1).to_broadcast([P, HEADS1, D // HEADS1])
                nc.vector.tensor_tensor(part, part, over, ALU.mult).then_inc(
                    normed, 1 if n < NBLK - 1 else 1 + NBD - NBLK)
            dve.sem_inc(done, 2)
            dve.wait_ge(loaded, 48)
            steps = 1 + 2 * BASES

            def a_pair(n, b):
                m = mixed[:, b, :, :]
                dve.wait_ge(based_ok, n + 3)
                dve.wait_ge(weights, n + 1)
                dve.wait_ge(done, n + 1)
                nc.vector.tensor_tensor(m, looped[:, b, 0:2 * D].rearrange("p (j f) -> p j f", j=2),
                                        bias_row[:].rearrange("p (a f) -> p a f", a=1).to_broadcast([P, 2, D]),
                                        ALU.add).then_inc(d, 1)
                for basis in range(BASES):
                    for j in range(2):
                        if basis > 0 or j == 0:
                            dve.wait_ge(d, n * steps + max(1, 2 * basis + j))
                        nc.vector.scalar_tensor_tensor(out=mixed[:, b, j, :], in0=based[:, b, j, basis, :],
                                                       scalar=by[:, b, j, basis:basis + 1], in1=mixed[:, b, j, :],
                                                       op0=ALU.mult, op1=ALU.add).then_inc(d, 1)
                dve.wait_ge(d, n * steps + steps)
                here = k.x[:, bass.ds(n * 2, 2), :]
                nc.vector.scalar_tensor_tensor(out=here, in0=m, scalar=0.0, in1=here, op0=ALU.max,
                                               op1=ALU.add).then_inc(done, 1)

            with dve.Fori(0, pairs // 2) as i:
                a_pair(i * 2, 0)
                a_pair(i * 2 + 1, 1)
            a_pair(pairs - 1, 0)


def project(nc, k, source, w, bias, outputs, name):
    width = w.shape[1]
    with ExitStack() as ctx:
        sb, ps, sem = tools(nc, k, ctx, name)
        x = sb("x", [P, 2, BATCH, D])
        xt = sb("xt", [P, 2, BATCH, P])
        y = sb("y", [P, 2, BATCH, width]) if any(add for *_, add in outputs) else None
        turned = ps("turned", [P, 1024])
        product = ps("product", [P, 2, -(-BATCH * width // 512) * 512])
        own = sem("own")
        turned_ok = sem("turned_ok")
        copied = sem("copied")
        made = sem("made")
        scaled = sem("scaled")
        d = sem("d")
        used = sem("used")
        block = ctx.enter_context(nc.Block())

        @block.scalar
        def _(act):
            def own_rows(n, b):
                act.wait_ge(turned_ok, n + 1)
                nc.scalar.copy(x[:, b, :, :], source[:, bass.ds(n * BATCH, BATCH), :]).then_inc(own, 1)

            def take_turned(n, b):
                act.wait_ge(turned_ok, n + 3)
                act.wait_ge(made, n + 1)
                nc.scalar.copy(xt[:, b, :, :].rearrange("p j f -> p (j f)"), turned[:, 0:BATCH * P]).then_inc(copied, 1)

            own_rows(0, 0)
            with act.Fori(0, BATCHES // 2 - 1) as i:
                for b in range(2):
                    own_rows(i * 2 + b + 1, 1 - b)
                    take_turned(i * 2 + b, b)
            own_rows(BATCHES - 1, 1)
            take_turned(BATCHES - 2, 0)
            take_turned(BATCHES - 1, 1)

        @block.tensor
        def _(pe):
            def turn(n, b):
                pe.wait_ge(own, n + 1)
                if not at(n, 0):
                    pe.wait_ge(copied, n)
                for j in range(BATCH):
                    last = nc.tensor.transpose(turned[:, j * P:(j + 1) * P], x[:, b, j, :], k.ident[:])
                last.then_inc(turned_ok, 1)

            def multiply(n, b):
                pe.wait_ge(copied, n + 1)
                pe.wait_ge(used, n + 1)
                for j in range(BATCH):
                    last = nc.tensor.matmul(product[:, b, j * width:(j + 1) * width], xt[:, b, j, :], w, start=True,
                                            stop=True)
                last.then_inc(made, 1)

            pe.sem_inc(turned_ok, 2)
            pe.sem_inc(made, 2)
            turn(0, 0)
            with pe.Fori(0, BATCHES // 2 - 1) as i:
                for b in range(2):
                    turn(i * 2 + b + 1, 1 - b)
                    multiply(i * 2 + b, b)
            turn(BATCHES - 1, 1)
            multiply(BATCHES - 2, 0)
            multiply(BATCHES - 1, 1)

        @block.vector
        def _(dve):
            count = 0
            if bias is not None:
                for lo, hi, scale, _, _ in outputs:
                    if scale != 1.0:
                        count += 1
                        nc.vector.tensor_scalar(bias[:, lo:hi], bias[:, lo:hi], scale, None, ALU.mult).then_inc(scaled, 1)
                if count:
                    dve.wait_ge(scaled, count)
            dve.sem_inc(used, 2)
            with dve.Fori(0, BATCHES // 2) as i:
                for b in range(2):
                    n = i * 2 + b
                    dve.wait_ge(made, n + 3)
                    dve.wait_ge(used, n + 1)
                    whole = product[:, b, 0:BATCH * width].rearrange("p (j f) -> p j f", j=BATCH)
                    for lo, hi, scale, out, add in outputs:
                        here = out[:, bass.ds(n * BATCH, BATCH), :]
                        src = whole[:, :, lo:hi]
                        if bias is None:
                            last = nc.vector.tensor_copy(here, src)
                            continue
                        row = bias[:, lo:hi].rearrange("p (a f) -> p a f", a=1).to_broadcast([P, BATCH, hi - lo])
                        if add:
                            nc.vector.tensor_tensor(y[:, b, :, :], src, row, ALU.add).then_inc(d, 1)
                            dve.wait_ge(d, n + 1)
                            last = nc.vector.tensor_tensor(here, here, y[:, b, :, :], ALU.add)
                        elif scale != 1.0:
                            last = nc.vector.scalar_tensor_tensor(out=here, in0=src, scalar=scale, in1=row,
                                                                  op0=ALU.mult, op1=ALU.add)
                        else:
                            last = nc.vector.tensor_tensor(here, src, row, ALU.add)
                    last.then_inc(used, 1)


def self_scores(nc, k, left, right, att_row, scores, name):
    with ExitStack() as ctx:
        sb, ps, sem = tools(nc, k, ctx, name)
        pair = sb("pair", [P, PIECE, D])
        step = sem("step")
        block = ctx.enter_context(nc.Block())

        @block.vector
        def _(dve):
            chain = in_steps(dve, step)
            for n in range(PIECES):
                here = slice(n * PIECE, (n + 1) * PIECE)
                flat = pair[:].rearrange("p b f -> p (b f)")
                chain(nc.vector.tensor_tensor(pair[:], left[:, here, :], right[:, here, :], ALU.add))
                chain(nc.vector.scalar_tensor_tensor(out=flat, in0=flat, scalar=0.2, in1=flat, op0=ALU.mult, op1=ALU.max))
                chain(nc.vector.tensor_tensor(pair[:], pair[:],
                                              att_row.rearrange("p (a f) -> p a f", a=1).to_broadcast([P, PIECE, D]),
                                              ALU.mult))
                chain(nc.vector.tensor_reduce(scores[:, here, :], pair[:].rearrange("p b (h f) -> p b h f", h=HEADS2),
                                              AX.X, ALU.add))


def attention_output(nc, k, total, left_table, bias, name):
    with ExitStack() as ctx:
        sb, ps, sem = tools(nc, k, ctx, name)
        left = sb("left", [P, NBLK, D])
        bias_row = sb("bias_row", [P, D])
        den = sb("den", [P, NBLK, HEADS2])
        alone = sb("alone", [P, NBLK, HEADS2])
        loaded = sem("loaded")
        step = sem("step")
        block = ctx.enter_context(nc.Block())
        head = D // HEADS2

        @block.sync
        def _(sp):
            sp.dma_start(left[:], left_table[0:NP, :].rearrange("(b p) f -> p b f", p=P)).then_inc(loaded, 16)
            sp.dma_start(bias_row[:], row_on_all(bias)).then_inc(loaded, 16)

        @block.vector
        def _(dve):
            chain = in_steps(dve, step)
            edge_sum = total[:, :, D:D + HEADS2]
            loop = total[:, :, D + HEADS2:D + 2 * HEADS2]
            chain(nc.vector.tensor_single_scalar(alone[:], edge_sum, 0.0, ALU.is_equal))
            chain(nc.vector.tensor_tensor(loop, loop, alone[:], ALU.add))
            chain(nc.vector.tensor_tensor(den[:], edge_sum, loop, ALU.add))
            chain(nc.vector.tensor_single_scalar(den[:], den[:], TINY, ALU.max))
            chain(nc.vector.reciprocal(den[:], den[:]))
            dve.wait_ge(loaded, 32)
            for h in range(HEADS2):
                f = slice(h * head, (h + 1) * head)
                across = lambda t: t.to_broadcast([P, NBLK, head])
                chain(nc.vector.tensor_tensor(left[:, :, f], left[:, :, f], across(loop[:, :, h:h + 1]), ALU.mult))
                chain(nc.vector.tensor_tensor(left[:, :, f], left[:, :, f], total[:, :, f], ALU.add))
                chain(nc.vector.tensor_tensor(left[:, :, f], left[:, :, f], across(den[:, :, h:h + 1]), ALU.mult))
            x = k.x[:, 0:NBLK, :]
            chain(nc.vector.tensor_tensor(x, x, left[:], ALU.add))
            chain(nc.vector.tensor_tensor(x, x, bias_row[:].rearrange("p (a f) -> p a f", a=1)
                                          .to_broadcast([P, NBLK, D]), ALU.add))


def value_rows(nc, k, total, values, table, name):
    with ExitStack() as ctx:
        sb, ps, sem = tools(nc, k, ctx, name)
        rows = sb("rows", [P, NBLK, D + HEADS3])
        rden = sb("rden", [P, NBLK, HEADS3])
        step = sem("step")
        made = sem("made")
        stored = sem("stored")
        block = ctx.enter_context(nc.Block())
        head = D // HEADS3

        @block.vector
        def _(dve):
            chain = in_steps(dve, step)
            chain(nc.vector.tensor_single_scalar(rden[:], total[:, :, 0:HEADS3], TINY, ALU.max))
            chain(nc.vector.reciprocal(rden[:], rden[:]))
            nc.vector.tensor_copy(rows[:, :, D:D + HEADS3], total[:, :, HEADS3:2 * HEADS3])
            for h in range(HEADS3):
                f = slice(h * head, (h + 1) * head)
                nc.vector.tensor_tensor(rows[:, :, f], values[:, 0:NBLK, f],
                                        rden[:, :, h:h + 1].to_broadcast([P, NBLK, head]), ALU.mult).then_inc(made, 1)

        @block.sync
        def _(sp):
            sp.wait_ge(made, HEADS3)
            sp.dma_start(table[0:NP, D:2 * D + HEADS3].rearrange("(b p) f -> p b f", p=P), rows[:]).then_inc(stored, 16)
            sp.wait_ge(stored, 16)


def load_nodes(nc, k, x, hops, name):
    with ExitStack() as ctx:
        sb, ps, sem = tools(nc, k, ctx, name)
        cleared = sem("cleared")
        loaded = sem("loaded")
        full = NBLK - 1
        block = ctx.enter_context(nc.Block())

        @block.vector
        def _(dve):
            nc.vector.memset(k.x[:], 0.0).then_inc(cleared, 1)

        @block.sync
        def _(sp):
            sp.wait_ge(cleared, 1)
            sp.dma_start(k.x[:, 0:full, :], x[0:full * P, :].rearrange("(b p) f -> p b f", p=P)).then_inc(loaded, 16)
            sp.dma_start(k.x[0:TAIL, full, :], x[full * P:N, :]).then_inc(loaded, 16)
            for h in range(3):
                sp.dma_start(hops[h][NP:NPD, :].rearrange("(b p) f -> p b f", p=P),
                             k.x[:, NBLK:NBD, :]).then_inc(loaded, 16)
            sp.wait_ge(loaded, 80)


def typed_rows(nc, k, o, name):
    with ExitStack() as ctx:
        sb, ps, sem = tools(nc, k, ctx, name)
        block = ctx.enter_context(nc.Block())

        @block.vector
        def _(dve):
            nc.vector.scalar_tensor_tensor(out=o.typed[:], in0=o.typed[:], scalar=float(NPD), in1=o.other[:],
                                           op0=ALU.mult, op1=ALU.add)


def graph_network(nc, a, out):
    k = Shared()
    k.semaphores = []
    with ExitStack() as ctx:
        def sb(name, shape, dt=F32):
            return ctx.enter_context(nc.sbuf_tensor(f"k_{name}", shape, dt))

        def dram(name, shape, dt=F32):
            return nc.dram_tensor(name, shape, dt, kind="Internal").ap()

        k.ident = sb("ident", [P, P])
        k.identb = sb("identb", [P, P], BF16)
        k.before = sb("before", [P, P])
        k.count = sb("count", [P, P])
        k.countb = sb("countb", [P, P], BF16)
        k.ones = sb("ones", [P, P])
        k.x = sb("x", [P, NBD, D])
        mix = sb("mix", [P, NBD, 4 * BASES])
        by_src, by_dst = Order(), Order()
        for o, n in ((by_src, "src"), (by_dst, "dst")):
            o.place = sb(f"{n}_place", [P, CH + SPARE])
            o.begins = sb(f"{n}_begins", [P, CH])
            o.block = sb(f"{n}_block", [1, CH + SPARE], I32)
            o.other = sb(f"{n}_other", [P, CH + SPARE], I32)
            o.sorted = dram(f"{n}_sorted", [LEAD + NSLOT, 4])
            o.breaks = dram(f"{n}_breaks", [NSLOT + P], BF16)
        by_src.weight = sb("src_weight", [P, CH + SPARE])
        by_dst.typed = sb("dst_typed", [P, CH + SPARE], I32)
        hops = [dram(f"hops{h}", [NPD, D]) for h in range(3)]
        related = dram("related", [TYPES, NPD, 2 * D])
        kept = dram("kept", [GROUPS, P, G * D])
        left_table = dram("left_table", [NPD, D])
        key_table = dram("key_table", [NPD, D])
        value_table = dram("value_table", [NPD, D])
        row_table = dram("row_table", [NPD, 2 * D + HEADS3])

        make_constants(nc, k)
        load_nodes(nc, k, a["x"], hops, "nodes")
        type_weights(nc, k, a["node_type_8"], [a[f"L1_gnn_w_comp_{p}"] for p in "qkva"], mix, "types")

        prefill(nc, k, [by_src.sorted, by_dst.sorted], "prefill")
        for o, n, key, fields in ((by_src, "src", a["src"], [a["dst"], a["edge_weight"]]),
                                  (by_dst, "dst", a["dst"], [a["src"], a["edge_type_8"]])):
            with ExitStack() as sort:
                def tmp(name, shape, dt=F32):
                    return sort.enter_context(nc.sbuf_tensor(f"{n}_sort_{name}", shape, dt))

                o.block_base = tmp("block_base", [P, CH])
                with ExitStack() as early:
                    def tmp2(name, shape, dt=F32):
                        return early.enter_context(nc.sbuf_tensor(f"{n}_sort_{name}", shape, dt))

                    rec = tmp2("rec", [P, EC, 4])
                    keys = tmp2("keys", [P, 2, EC + 2 * G])
                    counts = tmp2("counts", [HIS, P])
                    first_place = tmp2("first_place", [HIS, P])
                    load_edges(nc, k, key, fields, rec, keys, f"{n}_load")
                    histogram(nc, k, keys, counts, f"{n}_count")
                    place_blocks(nc, k, counts, first_place, o, f"{n}_base")
                    scatter_edges(nc, k, rec, keys, first_place, o.sorted, f"{n}_scatter")
                if o is by_src:
                    read_order(nc, k, o.sorted, o, o.breaks, [(1, o.other)], [(2, o.weight)], f"{n}_read")
                else:
                    read_order(nc, k, o.sorted, o, o.breaks, [(1, o.other), (2, o.typed)], [], f"{n}_read")
        typed_rows(nc, k, by_dst, "typed")

        free_semaphores(nc, k)

        for h in range(3):
            hop(nc, k, by_src, a["x"] if h == 0 else hops[h - 1], hops[h][0:NP, :], f"hop{h}")
        polynomial(nc, k, hops, a["L0_gnn_weights"], "poly")
        layernorm(nc, k, k.x, None, "norm0")

        free_semaphores(nc, k)

        with ExitStack() as layer:
            scores = layer.enter_context(nc.sbuf_tensor("l1_scores", [P, CH, HEADS1], F32))
            with ExitStack() as first:
                spread = first.enter_context(nc.sbuf_tensor("l1_spread", [P, NBD, 3, D], BF16))
                with ExitStack() as dense:
                    def tmp(name, shape, dt=F32):
                        return dense.enter_context(nc.sbuf_tensor(f"l1_{name}", shape, dt))

                    att_sb = tmp("att", [P, TYPES, D])
                    msg_sb = tmp("msg", [P, TYPES, D])
                    queries = tmp("queries", [P, NBD, D])
                    relation_weights(nc, k, a["L1_gnn_relation_att"], a["L1_gnn_relation_msg"],
                                     a["L1_gnn_relation_pri"], att_sb, msg_sb, "l1_relations")
                    relation_tables(nc, k, [a[f"L1_gnn_w_basis_{p}"] for p in "qkv"], att_sb, msg_sb, mix, queries,
                                    related, "l1_tables")
                    split_parts(nc, k, queries[:], spread, 0, "l1_split")
                score_pass(nc, k, by_dst, by_dst.typed, related.rearrange("t n f -> (t n) f"), 2 * D, D // HEADS1, D,
                           kept, spread, scores, None, "l1_score")
            segment_maximum(nc, k, by_dst, by_dst.breaks, HEADS1, scores, [scores], None, "l1_max")
            exponentials(nc, k, [scores], None, "l1_exp")
            with ExitStack() as second:
                total = second.enter_context(nc.sbuf_tensor("l1_total", [P, NBD, D + HEADS1], F32))
                sum_pass(nc, k, by_dst, kept, scores, [scores], total, "l1_sum")
                relation_output(nc, k, total, a["L1_gnn_w_basis_a"], a["L1_gnn_loop_weight"], a["L1_gnn_bias"], mix,
                                "l1_out")
        layernorm(nc, k, k.x, None, "norm1")

        free_semaphores(nc, k)

        with ExitStack() as layer:
            scores = layer.enter_context(nc.sbuf_tensor("l2_scores", [P, CH, HEADS2], F32))
            loops = layer.enter_context(nc.sbuf_tensor("l2_loops", [P, CH, HEADS2], F32))
            with ExitStack() as first:
                def tmp(name, shape, dt=F32):
                    return first.enter_context(nc.sbuf_tensor(f"l2_{name}", shape, dt))

                top = tmp("top", [P, CH, HEADS2])
                att_row = tmp("att_row", [P, D])
                with ExitStack() as edges:
                    spread = edges.enter_context(nc.sbuf_tensor("l2_spread", [P, NBD, 3, D + HEADS2], BF16))
                    att_rows = edges.enter_context(nc.sbuf_tensor("l2_att_rows", [P, G * D], F32))
                    load_all(nc, k, [(att_row[:], row_on_all(a["L2_gnn_att"].rearrange("h f -> (h f)")))]
                             + [(att_rows[:, g * D:(g + 1) * D], row_on_all(a["L2_gnn_att"].rearrange("h f -> (h f)")))
                                for g in range(G)], "l2_att_in")
                    with ExitStack() as dense:
                        w = dense.enter_context(nc.sbuf_tensor("l2_w", [P, 2 * D], F32))
                        right = dense.enter_context(nc.sbuf_tensor("l2_right", [P, NBD, D], F32))
                        left = dense.enter_context(nc.sbuf_tensor("l2_left", [P, NBD, D], F32))
                        loop_scores = dense.enter_context(nc.sbuf_tensor("l2_loop_scores", [P, NBD, HEADS2], F32))
                        turn_weights(nc, k, [(w[:, 0:D], a["L2_gnn_W_l"]), (w[:, D:2 * D], a["L2_gnn_W_r"])], "l2_turn")
                        project(nc, k, k.x, w[:], None, [(0, D, 1.0, left, False), (D, 2 * D, 1.0, right, False)],
                                "l2_project")
                        load_all(nc, k, [(left_table.rearrange("(b p) f -> p b f", p=P), left[:])], "l2_store")
                        self_scores(nc, k, left, right, att_row[:], loop_scores, "l2_self")
                        split_parts(nc, k, right[:], spread, 0, "l2_split")
                        split_parts(nc, k, loop_scores[:], spread, D, "l2_split_self")
                    score_pass(nc, k, by_dst, by_dst.other, left_table, D, D // HEADS2, 0, kept, spread, scores,
                               (att_rows, loops, top), "l2_score")
                segment_maximum(nc, k, by_dst, by_dst.breaks, HEADS2, top, [scores, loops], None, "l2_max")
            exponentials(nc, k, [scores, loops], by_dst.begins, "l2_exp")
            with ExitStack() as second:
                total = second.enter_context(nc.sbuf_tensor("l2_total", [P, NBLK, D + 2 * HEADS2], F32))
                sum_pass(nc, k, by_dst, kept, scores, [scores, loops], total, "l2_sum")
                attention_output(nc, k, total, left_table, a["L2_gnn_bias"], "l2_out")
        layernorm(nc, k, k.x, None, "norm2")

        free_semaphores(nc, k)

        with ExitStack() as layer:
            with ExitStack() as softmax:
                scores = softmax.enter_context(nc.sbuf_tensor("l3_scores", [P, CH, HEADS3], F32))
                with ExitStack() as first:
                    spread = first.enter_context(nc.sbuf_tensor("l3_spread_q", [P, NBD, 3, D], BF16))
                    with ExitStack() as dense:
                        def tmp(name, shape, dt=F32):
                            return dense.enter_context(nc.sbuf_tensor(f"l3_{name}", shape, dt))

                        w = tmp("w", [P, 3 * D])
                        bias = tmp("bias", [P, 3 * D])
                        turn_weights(nc, k, [(w[:, j * D:(j + 1) * D], a[f"L3_gnn_W{p}"]) for j, p in enumerate("qkv")],
                                     "l3_turn")
                        load_all(nc, k, [(bias[:, j * D:(j + 1) * D], row_on_all(a[f"L3_gnn_b{p}"]))
                                      for j, p in enumerate("qkv")], "l3_bias")
                        one, two = tmp("one", [P, NBD, D]), tmp("two", [P, NBD, D])
                        project(nc, k, k.x, w[:, D:3 * D], bias[:, D:3 * D],
                                [(0, D, 1.0, one, False), (D, 2 * D, 1.0, two, False)], "l3_keys_values")
                        load_all(nc, k, [(key_table.rearrange("(b p) f -> p b f", p=P), one[:]),
                                      (value_table.rearrange("(b p) f -> p b f", p=P), two[:])], "l3_store_kv")
                        project(nc, k, k.x, w[:, 0:D], bias[:, 0:D],
                                [(0, D, float(D // HEADS3) ** -0.5, one, False)], "l3_queries")
                        load_all(nc, k, [(row_table[:, 0:D].rearrange("(b p) f -> p b f", p=P), one[:])], "l3_store_q")
                        split_parts(nc, k, one[:], spread, 0, "l3_split_q")
                    score_pass(nc, k, by_src, by_src.other, key_table, D, D // HEADS3, 0, None, spread, scores, None,
                               "l3_score")
                maxima = softmax.enter_context(nc.sbuf_tensor("l3_maxima", [P, CH, HEADS3], F32))
                segment_maximum(nc, k, by_src, by_src.breaks, HEADS3, scores, [scores], maxima, "l3_max")
                exponentials(nc, k, [scores], None, "l3_exp")
                total = softmax.enter_context(nc.sbuf_tensor("l3_softmax_sums", [P, NBLK, 2 * HEADS3], F32))
                sum_pass(nc, k, by_src, None, None, [scores, maxima], total, "l3_sum")
                with ExitStack() as rows:
                    values = rows.enter_context(nc.sbuf_tensor("l3_values", [P, NBD, D], F32))
                    load_all(nc, k, [(values[:], value_table.rearrange("(b p) f -> p b f", p=P))], "l3_load_v")
                    value_rows(nc, k, total, values, row_table, "l3_rows")
            total = layer.enter_context(nc.sbuf_tensor("l3_total", [P, NBD, D], F32))
            with ExitStack() as second:
                spread = second.enter_context(nc.sbuf_tensor("l3_spread_k", [P, NBD, 3, D], BF16))
                with ExitStack() as dense:
                    keys = dense.enter_context(nc.sbuf_tensor("l3_keys", [P, NBD, D], F32))
                    load_all(nc, k, [(keys[:], key_table.rearrange("(b p) f -> p b f", p=P))], "l3_load_k")
                    split_parts(nc, k, keys[:], spread, 0, "l3_split_k")
                weigh_and_sum(nc, k, by_dst, by_dst.other, row_table[0:NP, :], spread, total, "l3_weigh")
            wo = layer.enter_context(nc.sbuf_tensor("l3_wo", [P, D], F32))
            bo = layer.enter_context(nc.sbuf_tensor("l3_bo", [P, D], F32))
            turn_weights(nc, k, [(wo[:], a["L3_gnn_Wo"])], "l3_turn_o")
            load_all(nc, k, [(bo[:], row_on_all(a["L3_gnn_bo"]))], "l3_bias_o")
            project(nc, k, total, wo[:], bo[:], [(0, D, 1.0, k.x, True)], "l3_out")
        layernorm(nc, k, k.x, out, "norm3")


def kernel(**inputs):
    import numpy as _np
    import concourse.bacc as _bacc
    from concourse import mybir as _mybir
    from concourse.bass_utils import run_bass_kernel_spmd as _run

    nc = _bacc.Bacc("TRN2", target_bir_lowering=False, num_devices=1)
    arrays, handles = {}, {}
    for name, value in inputs.items():
        array = _np.ascontiguousarray(value)
        arrays[f"in_{name}"] = array
        handles[name] = nc.dram_tensor(f"in_{name}", array.shape, _mybir.dt.from_np(array.dtype),
                                       kind="ExternalInput").ap()
    out = nc.dram_tensor("out_x", (N, D), F32, kind="ExternalOutput").ap()
    graph_network(nc, handles, out)
    r = _run(nc, [arrays], core_ids=[0])
    return r.results[0]["out_x"]
```
